# Optimizing a Trainium2 kernel written in Bass

```python
import numpy as np
import jax
import jax.numpy as jnp

def _softmax(x, axis=-1):
    return jax.nn.softmax(x, axis=axis)

def _gelu(x):
    return jax.nn.gelu(x, approximate=True)

def _silu(x):
    return jax.nn.silu(x)

def _sigmoid(x):
    return jax.nn.sigmoid(x)

def _layernorm(x, axis=-1, eps=1e-05):
    m = jnp.mean(x, axis=axis, keepdims=True)
    v = jnp.var(x, axis=axis, keepdims=True)
    return (x - m) / jnp.sqrt(v + eps)

def _scatter_add(tgt, idx, src, axis=0):
    return tgt.at[idx].add(src)

def _segment_sum(src, seg, n):
    return jax.ops.segment_sum(src, seg, n)
kernel_name = 'mk_sandwich_d2_jaxref_r8_80c9d9'

def setup_inputs(seed: int=0):
    np.random.seed(seed)
    _w = jnp.asarray

    def _L0_attn_setup():
        import jax, jax.numpy as jnp
        import numpy as np
        EMB, HEADS, HIDDEN = (128, 16, 64)
        BS, N = (2, 256)
        key = jax.random.key(seed)
        ks = jax.random.split(key, 7)
        s_in = 1.0 / np.sqrt(EMB)
        s_u = 1.0 / np.sqrt(HEADS * HIDDEN)
        return {'x': jax.random.normal(ks[0], (BS, N, EMB), dtype=jnp.float32), 'w_q': jax.random.uniform(ks[1], (EMB, HEADS * HIDDEN), jnp.float32, -s_in, s_in), 'w_k': jax.random.uniform(ks[2], (EMB, HEADS * HIDDEN), jnp.float32, -s_in, s_in), 'w_v': jax.random.uniform(ks[3], (EMB, HEADS * HIDDEN), jnp.float32, -s_in, s_in), 'w_u': jax.random.uniform(ks[4], (HEADS * HIDDEN, EMB), jnp.float32, -s_u, s_u), 'b_u': jax.random.uniform(ks[5], (EMB,), jnp.float32, -s_u, s_u)}
    _L0_attn_in = _L0_attn_setup()

    def _L0_ffn_setup():
        import jax, jax.numpy as jnp
        import numpy as np
        B, T, D, H = (4, 256, 128, 256)
        E, S, K = (8, 2, 2)

        def _swiglu_stacked(x, w1, b1, w2, b2, w3, b3):
            p1 = jnp.einsum('btd,ndh->nbth', x, w1) + b1[:, None, None, :]
            p2 = jnp.einsum('btd,ndh->nbth', x, w2) + b2[:, None, None, :]
            glu = jax.nn.silu(p1) * p2
            return jnp.einsum('nbth,nhd->nbtd', glu, w3) + b3[:, None, None, :]
        key = jax.random.key(seed)
        ks = jax.random.split(key, 10)
        s = 0.02
        return {'x': jax.random.normal(ks[0], (B, T, D), jnp.float32), 'gate_w': jax.random.normal(ks[1], (D, E), jnp.float32) * s, 'gate_b': jnp.zeros((E,), jnp.float32), 'rw1': jax.random.normal(ks[2], (E, D, H), jnp.float32) * s, 'rb1': jnp.zeros((E, H), jnp.float32), 'rw2': jax.random.normal(ks[3], (E, D, H), jnp.float32) * s, 'rb2': jnp.zeros((E, H), jnp.float32), 'rw3': jax.random.normal(ks[4], (E, H, D), jnp.float32) * s, 'rb3': jnp.zeros((E, D), jnp.float32), 'sw1': jax.random.normal(ks[5], (S, D, H), jnp.float32) * s, 'sb1': jnp.zeros((S, H), jnp.float32), 'sw2': jax.random.normal(ks[6], (S, D, H), jnp.float32) * s, 'sb2': jnp.zeros((S, H), jnp.float32), 'sw3': jax.random.normal(ks[7], (S, H, D), jnp.float32) * s, 'sb3': jnp.zeros((S, D), jnp.float32)}
    _L0_ffn_in = _L0_ffn_setup()

    def _L1_attn_setup():
        import jax, jax.numpy as jnp
        import numpy as np
        D = 128
        H = 16
        KVH = 4
        HD = D // H
        LAT = 32
        WIN = 32
        B, S = (1, 256)
        BASE_G, BASE_L = (1000000.0, 10000.0)
        EPS = 1e-06

        def rmsnorm(x, w):
            return x * jax.lax.rsqrt(jnp.mean(x * x, axis=-1, keepdims=True) + EPS) * w

        def qk_norm(x):
            return x * jax.lax.rsqrt(jnp.mean(x * x, axis=-1, keepdims=True) + EPS)

        def rope(x, base):
            s, hd = (x.shape[-2], x.shape[-1])
            inv_freq = 1.0 / base ** (jnp.arange(0, hd, 2, dtype=jnp.float32) / hd)
            freqs = jnp.arange(s, dtype=jnp.float32)[:, None] * inv_freq[None, :]
            cos, sin = (jnp.cos(freqs), jnp.sin(freqs))
            xe, xo = (x[..., ::2], x[..., 1::2])
            out = jnp.stack([xe * cos - xo * sin, xe * sin + xo * cos], axis=-1)
            return out.reshape(x.shape)

        def split_heads(x, n_heads):
            b, s, _ = x.shape
            return x.reshape(b, s, n_heads, HD).transpose(0, 2, 1, 3)

        def repeat_kv(x):
            return jnp.repeat(x, H // KVH, axis=1)

        def sdpa(q, k, v, mask):
            scores = jnp.einsum('bhqd,bhkd->bhqk', q, k) / np.sqrt(HD).astype(np.float32)
            scores = jnp.where(mask, scores, jnp.float32(-1e+30))
            probs = jax.nn.softmax(scores, axis=-1)
            return jnp.einsum('bhqk,bhkd->bhqd', probs, v)

        def merge_heads(x):
            b, h, s, hd = x.shape
            return x.transpose(0, 2, 1, 3).reshape(b, s, h * hd)

        def global_latent_attn(x, wq, w_kv_down, w_k_up, w_v_up, wo):
            q = split_heads(x @ wq, H)
            latent = x @ w_kv_down
            k = split_heads(latent @ w_k_up, KVH)
            v = split_heads(latent @ w_v_up, KVH)
            q, k = (rope(q, BASE_G), rope(k, BASE_G))
            q, k = (qk_norm(q), qk_norm(k))
            k, v = (repeat_kv(k), repeat_kv(v))
            i = jnp.arange(x.shape[1])
            causal = i[:, None] >= i[None, :]
            return merge_heads(sdpa(q, k, v, causal)) @ wo

        def local_gqa_attn(x, wq, wk, wv, wo):
            q = split_heads(x @ wq, H)
            k = split_heads(x @ wk, KVH)
            v = split_heads(x @ wv, KVH)
            q, k = (rope(q, BASE_L), rope(k, BASE_L))
            q, k = (qk_norm(q), qk_norm(k))
            k, v = (repeat_kv(k), repeat_kv(v))
            i = jnp.arange(x.shape[1])
            diff = i[:, None] - i[None, :]
            mask = (diff >= 0) & (diff < WIN)
            return merge_heads(sdpa(q, k, v, mask)) @ wo
        key = jax.random.key(seed)
        ks = jax.random.split(key, 12)
        std = 0.02
        return {'hidden': jax.random.normal(ks[0], (B, S, D), dtype=jnp.float32), 'norm1_w': jnp.ones((D,), jnp.float32), 'norm2_w': jnp.ones((D,), jnp.float32), 'g_wq': jax.random.normal(ks[1], (D, H * HD), jnp.float32) * std, 'g_kv_down': jax.random.normal(ks[2], (D, LAT), jnp.float32) * std, 'g_k_up': jax.random.normal(ks[3], (LAT, KVH * HD), jnp.float32) * std, 'g_v_up': jax.random.normal(ks[4], (LAT, KVH * HD), jnp.float32) * std, 'g_wo': jax.random.normal(ks[5], (D, D), jnp.float32) * std, 'l_wq': jax.random.normal(ks[6], (D, H * HD), jnp.float32) * std, 'l_wk': jax.random.normal(ks[7], (D, KVH * HD), jnp.float32) * std, 'l_wv': jax.random.normal(ks[8], (D, KVH * HD), jnp.float32) * std, 'l_wo': jax.random.normal(ks[9], (D, D), jnp.float32) * std}
    _L1_attn_in = _L1_attn_setup()

    def _L1_ffn_setup():
        import jax, jax.numpy as jnp
        import numpy as np
        B, SEQ, DIM = (2, 512, 128)
        E, S = (8, 64)
        HID = 4 * DIM
        SCALE = DIM ** 0.5

        def rmsnorm(x, gamma):
            n = jnp.linalg.norm(x, axis=-1, keepdims=True)
            return x / jnp.maximum(n, 1e-12) * SCALE * gamma
        key = jax.random.key(seed)
        ks = jax.random.split(key, 4)
        w_init = lambda k, shape: jax.random.normal(k, shape, dtype=jnp.float32) * 0.02
        return {'x': jax.random.normal(ks[0], (B, SEQ, DIM), dtype=jnp.float32), 'norm_gamma': jnp.ones((DIM,), jnp.float32), 'slot_norm_gamma': jnp.ones((DIM,), jnp.float32), 'slot_embeds': jax.random.normal(ks[1], (E, S, DIM), dtype=jnp.float32), 'w1': w_init(ks[2], (E, DIM, HID)), 'b1': jnp.zeros((E, HID), jnp.float32), 'w2': w_init(ks[3], (E, HID, DIM)), 'b2': jnp.zeros((E, DIM), jnp.float32)}
    _L1_ffn_in = _L1_ffn_setup()
    _d = {'L0_attn_x': _L0_attn_in['x'], 'L0_attn_w_q': _L0_attn_in['w_q'], 'L0_attn_w_k': _L0_attn_in['w_k'], 'L0_attn_w_v': _L0_attn_in['w_v'], 'L0_attn_w_u': _L0_attn_in['w_u'], 'L0_attn_b_u': _L0_attn_in['b_u'], 'L0_ffn_gate_w': _L0_ffn_in['gate_w'], 'L0_ffn_gate_b': _L0_ffn_in['gate_b'], 'L0_ffn_rw1': _L0_ffn_in['rw1'], 'L0_ffn_rb1': _L0_ffn_in['rb1'], 'L0_ffn_rw2': _L0_ffn_in['rw2'], 'L0_ffn_rb2': _L0_ffn_in['rb2'], 'L0_ffn_rw3': _L0_ffn_in['rw3'], 'L0_ffn_rb3': _L0_ffn_in['rb3'], 'L0_ffn_sw1': _L0_ffn_in['sw1'], 'L0_ffn_sb1': _L0_ffn_in['sb1'], 'L0_ffn_sw2': _L0_ffn_in['sw2'], 'L0_ffn_sb2': _L0_ffn_in['sb2'], 'L0_ffn_sw3': _L0_ffn_in['sw3'], 'L0_ffn_sb3': _L0_ffn_in['sb3'], 'L1_attn_norm1_w': _L1_attn_in['norm1_w'], 'L1_attn_norm2_w': _L1_attn_in['norm2_w'], 'L1_attn_g_wq': _L1_attn_in['g_wq'], 'L1_attn_g_kv_down': _L1_attn_in['g_kv_down'], 'L1_attn_g_k_up': _L1_attn_in['g_k_up'], 'L1_attn_g_v_up': _L1_attn_in['g_v_up'], 'L1_attn_g_wo': _L1_attn_in['g_wo'], 'L1_attn_l_wq': _L1_attn_in['l_wq'], 'L1_attn_l_wk': _L1_attn_in['l_wk'], 'L1_attn_l_wv': _L1_attn_in['l_wv'], 'L1_attn_l_wo': _L1_attn_in['l_wo'], 'L1_ffn_norm_gamma': _L1_ffn_in['norm_gamma'], 'L1_ffn_slot_norm_gamma': _L1_ffn_in['slot_norm_gamma'], 'L1_ffn_slot_embeds': _L1_ffn_in['slot_embeds'], 'L1_ffn_w1': _L1_ffn_in['w1'], 'L1_ffn_b1': _L1_ffn_in['b1'], 'L1_ffn_w2': _L1_ffn_in['w2'], 'L1_ffn_b2': _L1_ffn_in['b2']}
    _x0 = _d['L0_attn_x']
    _d['L0_attn_x'] = jax.random.normal(jax.random.fold_in(jax.random.key(seed), 1), (4, 1024, 128), dtype=_x0.dtype)
    del _x0
    return _d

def reference(L0_attn_x, L0_attn_w_q, L0_attn_w_k, L0_attn_w_v, L0_attn_w_u, L0_attn_b_u, L0_ffn_gate_w, L0_ffn_gate_b, L0_ffn_rw1, L0_ffn_rb1, L0_ffn_rw2, L0_ffn_rb2, L0_ffn_rw3, L0_ffn_rb3, L0_ffn_sw1, L0_ffn_sb1, L0_ffn_sw2, L0_ffn_sb2, L0_ffn_sw3, L0_ffn_sb3, L1_attn_norm1_w, L1_attn_norm2_w, L1_attn_g_wq, L1_attn_g_kv_down, L1_attn_g_k_up, L1_attn_g_v_up, L1_attn_g_wo, L1_attn_l_wq, L1_attn_l_wk, L1_attn_l_wv, L1_attn_l_wo, L1_ffn_norm_gamma, L1_ffn_slot_norm_gamma, L1_ffn_slot_embeds, L1_ffn_w1, L1_ffn_b1, L1_ffn_w2, L1_ffn_b2):

    def _L0_attn_ref(x, w_q, w_k, w_v, w_u, b_u):
        import jax, jax.numpy as jnp
        import numpy as np
        EMB, HEADS, HIDDEN = (128, 16, 64)
        BS, N = (2, 256)
        bs, n, emb = x.shape
        h, hd = (HEADS, HIDDEN)
        q = (x @ w_q).reshape(bs, n, h, hd)
        k = (x @ w_k).reshape(bs, n, h, hd)
        v = (x @ w_v).reshape(bs, n, h, hd)
        scale = 1.0 / jnp.sqrt(jnp.asarray(hd, dtype=x.dtype))
        q = q * scale
        k = k * scale
        dot = jnp.einsum('bqhd,bkhd->bhqk', q, k)
        causal = jnp.tril(jnp.ones((n, n), dtype=bool))
        dot = jnp.where(causal, dot, jnp.asarray(-jnp.inf, dtype=dot.dtype))
        att = jax.nn.softmax(dot, axis=-1)
        out = jnp.einsum('bhqk,bkhd->bqhd', att, v).reshape(bs, n, h * hd)
        return out @ w_u + b_u

    def _L0_ffn_ref(x, gate_w, gate_b, rw1, rb1, rw2, rb2, rw3, rb3, sw1, sb1, sw2, sb2, sw3, sb3):
        import jax, jax.numpy as jnp
        import numpy as np
        B, T, D, H = (4, 256, 128, 256)
        E, S, K = (8, 2, 2)

        def _swiglu_stacked(x, w1, b1, w2, b2, w3, b3):
            p1 = jnp.einsum('btd,ndh->nbth', x, w1) + b1[:, None, None, :]
            p2 = jnp.einsum('btd,ndh->nbth', x, w2) + b2[:, None, None, :]
            glu = jax.nn.silu(p1) * p2
            return jnp.einsum('nbth,nhd->nbtd', glu, w3) + b3[:, None, None, :]
        scores = jax.nn.softmax(x @ gate_w + gate_b, axis=-1)
        weights, indices = jax.lax.top_k(scores, K)
        routed_all = _swiglu_stacked(x, rw1, rb1, rw2, rb2, rw3, rb3)
        out_bted = jnp.transpose(routed_all, (1, 2, 0, 3))
        gathered = jnp.take_along_axis(out_bted, indices[..., None], axis=2)
        routed = jnp.sum(weights[..., None] * gathered, axis=2)
        shared = _swiglu_stacked(x, sw1, sb1, sw2, sb2, sw3, sb3).mean(axis=0)
        return shared + routed

    def _L1_attn_ref(hidden, norm1_w, norm2_w, g_wq, g_kv_down, g_k_up, g_v_up, g_wo, l_wq, l_wk, l_wv, l_wo):
        import jax, jax.numpy as jnp
        import numpy as np
        D = 128
        H = 16
        KVH = 4
        HD = D // H
        LAT = 32
        WIN = 32
        B, S = (1, 256)
        BASE_G, BASE_L = (1000000.0, 10000.0)
        EPS = 1e-06

        def rmsnorm(x, w):
            return x * jax.lax.rsqrt(jnp.mean(x * x, axis=-1, keepdims=True) + EPS) * w

        def qk_norm(x):
            return x * jax.lax.rsqrt(jnp.mean(x * x, axis=-1, keepdims=True) + EPS)

        def rope(x, base):
            s, hd = (x.shape[-2], x.shape[-1])
            inv_freq = 1.0 / base ** (jnp.arange(0, hd, 2, dtype=jnp.float32) / hd)
            freqs = jnp.arange(s, dtype=jnp.float32)[:, None] * inv_freq[None, :]
            cos, sin = (jnp.cos(freqs), jnp.sin(freqs))
            xe, xo = (x[..., ::2], x[..., 1::2])
            out = jnp.stack([xe * cos - xo * sin, xe * sin + xo * cos], axis=-1)
            return out.reshape(x.shape)

        def split_heads(x, n_heads):
            b, s, _ = x.shape
            return x.reshape(b, s, n_heads, HD).transpose(0, 2, 1, 3)

        def repeat_kv(x):
            return jnp.repeat(x, H // KVH, axis=1)

        def sdpa(q, k, v, mask):
            scores = jnp.einsum('bhqd,bhkd->bhqk', q, k) / np.sqrt(HD).astype(np.float32)
            scores = jnp.where(mask, scores, jnp.float32(-1e+30))
            probs = jax.nn.softmax(scores, axis=-1)
            return jnp.einsum('bhqk,bhkd->bhqd', probs, v)

        def merge_heads(x):
            b, h, s, hd = x.shape
            return x.transpose(0, 2, 1, 3).reshape(b, s, h * hd)

        def global_latent_attn(x, wq, w_kv_down, w_k_up, w_v_up, wo):
            q = split_heads(x @ wq, H)
            latent = x @ w_kv_down
            k = split_heads(latent @ w_k_up, KVH)
            v = split_heads(latent @ w_v_up, KVH)
            q, k = (rope(q, BASE_G), rope(k, BASE_G))
            q, k = (qk_norm(q), qk_norm(k))
            k, v = (repeat_kv(k), repeat_kv(v))
            i = jnp.arange(x.shape[1])
            causal = i[:, None] >= i[None, :]
            return merge_heads(sdpa(q, k, v, causal)) @ wo

        def local_gqa_attn(x, wq, wk, wv, wo):
            q = split_heads(x @ wq, H)
            k = split_heads(x @ wk, KVH)
            v = split_heads(x @ wv, KVH)
            q, k = (rope(q, BASE_L), rope(k, BASE_L))
            q, k = (qk_norm(q), qk_norm(k))
            k, v = (repeat_kv(k), repeat_kv(v))
            i = jnp.arange(x.shape[1])
            diff = i[:, None] - i[None, :]
            mask = (diff >= 0) & (diff < WIN)
            return merge_heads(sdpa(q, k, v, mask)) @ wo
        x = hidden
        x = x + global_latent_attn(rmsnorm(x, norm1_w), g_wq, g_kv_down, g_k_up, g_v_up, g_wo)
        x = x + local_gqa_attn(rmsnorm(x, norm2_w), l_wq, l_wk, l_wv, l_wo)
        return x

    def _L1_ffn_ref(x, norm_gamma, slot_norm_gamma, slot_embeds, w1, b1, w2, b2):
        import jax, jax.numpy as jnp
        import numpy as np
        B, SEQ, DIM = (2, 512, 128)
        E, S = (8, 64)
        HID = 4 * DIM
        SCALE = DIM ** 0.5

        def rmsnorm(x, gamma):
            n = jnp.linalg.norm(x, axis=-1, keepdims=True)
            return x / jnp.maximum(n, 1e-12) * SCALE * gamma
        xn = rmsnorm(x, norm_gamma)
        sn = rmsnorm(slot_embeds, slot_norm_gamma)
        logits = jnp.einsum('bnd,esd->bnes', xn, sn)
        dispatch = jax.nn.softmax(logits, axis=1)
        b, n, e, s = logits.shape
        combine = jax.nn.softmax(logits.reshape(b, n, e * s), axis=-1)
        slots = jnp.einsum('bnd,bnes->besd', xn, dispatch)
        h = jnp.einsum('besd,edh->besh', slots, w1) + b1[None, :, None, :]
        h = jax.nn.gelu(h, approximate=False)
        eo = jnp.einsum('besh,ehd->besd', h, w2) + b2[None, :, None, :]
        eo = eo.reshape(b, e * s, DIM)
        out = jnp.einsum('bmd,bnm->bnd', eo, combine)
        return out
    x = L0_attn_x
    x = x + _layernorm(_L0_attn_ref(_layernorm(x, axis=-1), L0_attn_w_q, L0_attn_w_k, L0_attn_w_v, L0_attn_w_u, L0_attn_b_u), axis=-1)
    x = x + _layernorm(_L0_ffn_ref(_layernorm(x, axis=-1), L0_ffn_gate_w, L0_ffn_gate_b, L0_ffn_rw1, L0_ffn_rb1, L0_ffn_rw2, L0_ffn_rb2, L0_ffn_rw3, L0_ffn_rb3, L0_ffn_sw1, L0_ffn_sb1, L0_ffn_sw2, L0_ffn_sb2, L0_ffn_sw3, L0_ffn_sb3), axis=-1)
    x = x + _layernorm(_L1_attn_ref(_layernorm(x, axis=-1), L1_attn_norm1_w, L1_attn_norm2_w, L1_attn_g_wq, L1_attn_g_kv_down, L1_attn_g_k_up, L1_attn_g_v_up, L1_attn_g_wo, L1_attn_l_wq, L1_attn_l_wk, L1_attn_l_wv, L1_attn_l_wo), axis=-1)
    x = x + _layernorm(_L1_ffn_ref(_layernorm(x, axis=-1), L1_ffn_norm_gamma, L1_ffn_slot_norm_gamma, L1_ffn_slot_embeds, L1_ffn_w1, L1_ffn_b1, L1_ffn_w2, L1_ffn_b2), axis=-1)
    return x

_drawn_inputs = setup_inputs


def setup_inputs(seed=0):
    import zlib

    import numpy as np

    out = dict(_drawn_inputs(seed))
    spreads = {'L0_ffn_gate_b': (0.0, 0.1),
     'L0_ffn_rb1': (0.0, 0.592),
     'L0_ffn_rb2': (0.0, 0.54),
     'L0_ffn_rb3': (0.0, 0.1),
     'L0_ffn_sb1': (0.0, 0.1),
     'L0_ffn_sb2': (0.0, 0.1),
     'L0_ffn_sb3': (0.0, 0.1),
     'L1_attn_norm1_w': (1.0, 0.6),
     'L1_attn_norm2_w': (1.0, 0.6),
     'L1_ffn_norm_gamma': (1.0, 0.2),
     'L1_ffn_slot_norm_gamma': (1.0, 0.2),
     'L1_ffn_b1': (0.0, 0.1),
     'L1_ffn_b2': (0.0, 0.1)}
    factors = {'L1_attn_g_wq': 8.0,
     'L1_attn_g_kv_down': 8.0,
     'L1_attn_g_k_up': 8.0,
     'L1_attn_g_v_up': 8.0,
     'L1_attn_g_wo': 8.0,
     'L1_attn_l_wq': 64.0,
     'L1_attn_l_wk': 64.0,
     'L1_attn_l_wv': 3.093,
     'L1_attn_l_wo': 3.609}
    for name, (base, spread) in spreads.items():
        noise = np.random.default_rng([zlib.crc32(name.encode()), seed]).standard_normal(out[name].shape)
        drawn = base * np.exp(spread * noise) if base else spread * noise
        out[name] = jnp.asarray(drawn.astype(out[name].dtype))
    for name, factor in factors.items():
        out[name] = (out[name] * factor).astype(out[name].dtype)
    return out
```

```python
import numpy as np
import concourse.bass as bass
from concourse import mybir
from contextlib import ExitStack

F32 = mybir.dt.float32
F32R = mybir.dt.float32r
BF16 = mybir.dt.bfloat16
U32 = mybir.dt.uint32
ALU = mybir.AluOpType
ACT = mybir.ActivationFunctionType
AX = mybir.AxisListType
ds = bass.ds

P = 128
BATCH, SEQ, D = 4, 1024, 128
NB = SEQ // P
NBLK = BATCH * NB
HALF = 512
LN_EPS = 1e-5


class Chain:

    def __init__(self, eng, sem, base=0):
        self.eng, self.sem, self.base, self.n = eng, sem, base, 0

    def did(self, ins):
        ins.then_inc(self.sem, 1)
        self.n += 1

    def settle(self):
        self.eng.wait_ge(self.sem, self.base + self.n)


def split_passes(hi_lo_a, hi_lo_b):
    (ah, al), (bh, bl) = hi_lo_a, hi_lo_b
    return [(ah, bh), (ah, bl), (al, bh)]




NORM_STEPS = 2 * NB + 5


def layernorm_parts(dve, chain, x_of, out_of, t, count):
    def statistics(blks):
        for blk in blks:
            chain.did(dve.bn_stats(t.stats[:, blk, :], x_of(blk)))

    def variance():
        chain.settle()
        mean_e, sq_e, mean_o, sq_o = (t.stats[:, :, c] for c in (1, 2, 4, 5))
        chain.did(dve.scalar_tensor_tensor(t.square[:], sq_e, D * LN_EPS, sq_o, ALU.add, ALU.add))
        chain.did(dve.tensor_tensor(t.gap[:], mean_e, mean_o, ALU.subtract))
        chain.did(dve.tensor_tensor(t.twice[:], mean_e, mean_o, ALU.add))
        chain.settle()
        chain.did(dve.scalar_tensor_tensor(t.gap[:], t.gap[:], 0.25, t.gap[:], ALU.mult, ALU.mult))
        chain.did(dve.tensor_scalar(t.mean[:], t.twice[:], 0.5, None, ALU.mult))
        chain.settle()
        dve.scalar_tensor_tensor(t.var[:], t.square[:], 1.0 / D, t.gap[:], ALU.mult, ALU.add).then_inc(t.var_ready, 1)

    def normalize(blks):
        dve.wait_ge(t.rstd_ready, count + 1)
        for blk in blks:
            chain.did(dve.tensor_scalar(out_of(blk), x_of(blk), t.mean[:, blk:blk + 1], t.rstd[:, blk:blk + 1],
                                        ALU.subtract, ALU.mult))

    quarters = [range(blk, blk + 2) for blk in range(0, NB, 2)]
    return [*(lambda q=q: statistics(q) for q in quarters), variance,
            *(lambda q=q: normalize(q) for q in (range(0, 4), range(4, NB))), chain.settle]


def layernorm(*args):
    for part in layernorm_parts(*args):
        part()


def inverse_root(pool, t, minus_half, count):
    pool.wait_ge(t.var_ready, count + 1)
    pool.tensor_tensor(t.rstd[:], t.var[:], minus_half, ALU.pow).then_inc(t.rstd_ready, 1)


class NormTiles:

    def __init__(self, ctx, nc, name):
        sb = lambda n, shape: ctx.enter_context(nc.sbuf_tensor(f"{name}_{n}", shape, F32))
        sem = lambda n: ctx.enter_context(nc.semaphore(f"{name}_{n}"))
        self.stats = sb("stats", [P, NB, 6])
        self.square, self.gap, self.twice, self.mean, self.var, self.rstd = (
            sb(n, [P, NB]) for n in ("square", "gap", "twice", "mean", "var", "rstd"))
        self.var_ready, self.rstd_ready, self.chain = sem("var_ready"), sem("rstd_ready"), sem("chain")


A_HEADS, A_HD = 16, 64
PAIRS = A_HEADS // 2
QK_GROUPS, V_GROUPS = 8, 2
GROUPS = QK_GROUPS + V_GROUPS
KEYS_SCALE = 1.0 / A_HD
BANK_TURNS = sum((i + 4) // 4 for i in range(NB))
GROUPS_OF_STEP = [(0, 1)] + [(k + 1,) for k in range(1, NB - 1)] + [(QK_GROUPS, QK_GROUPS + 1)]


def first_pair(run, b, extra=()):
    run(0, 0, 1, True, True, b, extra)


def other_pairs(eng, run, b, extra=()):
    with eng.Fori(0, PAIRS // 2 - 1) as q:
        for par, pair in ((1, q * 2 + 1), (0, q * 2 + 2)):
            run(par, pair, q + 2, False, True, b, ())
    run(1, PAIRS - 1, 0, False, False, b, extra)


def attention_layer0(nc, g):
    with ExitStack() as ctx:
        def sb(name, shape, dt=F32):
            return ctx.enter_context(nc.sbuf_tensor("a_" + name, shape, dt))

        def pb(name, shape):
            return ctx.enter_context(nc.psum_tensor("a_" + name, shape, F32))

        def sem(name):
            sems.append(nc.alloc_semaphore(name="a_" + name))
            return sems[-1]

        sems = []

        w_hl = sb("w_hl", [P, 6, D * 8], F32R)
        w_u = sb("w_u", [P, PAIRS, D])
        b_u = sb("b_u", [P, D])
        w_pair = [sb(f"w_pair{i}", [P, 4, 2, P], F32R) for i in range(2)]
        wv_pair = [sb(f"wv_pair{i}", [P, 2, P], F32R) for i in range(2)]
        x_norm = sb("x_norm", [P, NB, D])
        y = sb("y", [P, NB, D])
        xT_hi = sb("xT_hi", [P, SEQ], F32R)
        xT_lo = sb("xT_lo", [P, SEQ], F32R)
        q_st = [[sb(f"q_st{i}{h}", [P, SEQ], F32R) for h in range(2)] for i in range(2)]
        k_hh = [[sb(f"k_hh{i}{h}", [P, SEQ], F32R) for h in range(2)] for i in range(2)]
        k_ll = [[sb(f"k_ll{i}{h}", [P, SEQ], F32R) for h in range(2)] for i in range(2)]
        v_sb = [sb(f"v{i}", [P, NB, P]) for i in range(2)]
        probs = [sb(f"probs{i}", [P, 2, SEQ]) for i in range(2)]
        probsT = [sb(f"probsT{i}", [P, 2, SEQ]) for i in range(2)]
        outT = sb("outT", [P, PAIRS, SEQ])
        r_bc = [sb(f"r_bc{i}", [P, P]) for i in range(2)]
        neg_max, row_sum, row_inv = (sb(n, [P, NB, 2]) for n in ("neg_max", "row_sum", "row_inv"))
        norm = NormTiles(ctx, nc, "a_norm")

        scores = [pb(f"scores{h}", [P, SEQ]) for h in range(2)]
        tr = [pb(f"tr{i}", [P, HALF]) for i in range(2)]
        o_ps = pb("o_ps", [P, HALF])
        p_ps = pb("p_ps", [P, HALF])
        raw = outT

        loaded, split_hi, split_lo = sem("loaded"), sem("split_hi"), sem("split_lo")
        pair_loaded = [sem(f"pair_loaded{i}") for i in range(2)]
        xT_done, xT_hi_done, xT_lo_done = sem("xT_done"), sem("xT_hi_done"), sem("xT_lo_done")
        proj_done, proj_hi, proj_lo = sem("proj_done"), sem("proj_hi"), sem("proj_lo")
        scored, max_ready, exp_done = sem("scored"), sem("max_ready"), sem("exp_done")
        tr_done, tr_out = sem("tr_done"), [sem("tr_out_act"), sem("tr_out_dve")]
        inv_ready, inv_bc, inv_sb = sem("inv_ready"), sem("inv_bc"), sem("inv_sb")
        pv_done, out_kept = sem("pv_done"), sem("out_kept")
        y_done, y_used = sem("y_done"), sem("y_used")

        with nc.Block() as block:
            @block.sync
            def _(sp):
                for n, w in enumerate((g.inputs["L0_attn_w_q"], g.inputs["L0_attn_w_k"], g.inputs["L0_attn_w_v"])):
                    sp.dma_start(raw[:, n, :], w).then_inc(loaded, 16)
                sp.dma_start(w_u[:], g.inputs["L0_attn_w_u"].rearrange("(t p) n -> p t n", p=P)).then_inc(loaded, 16)
                sp.dma_start(b_u[:], g.inputs["L0_attn_b_u"].partition_broadcast(P)).then_inc(loaded, 16)

            @block.scalar
            def _(act):
                act.wait_ge(loaded, 5 * 16)
                for n in range(3):
                    act.activation(w_hl[:, 2 * n, :], raw[:, n, :], ACT.Copy).then_inc(split_hi, 1)

            @block.vector
            def _(dve):
                for n in range(3):
                    dve.wait_ge(split_hi, n + 1)
                    dve.tensor_tensor(w_hl[:, 2 * n + 1, :], raw[:, n, :],
                                      w_hl[:, 2 * n, :].bitcast(F32), ALU.subtract).then_inc(split_lo, 1)
                dve.wait_ge(split_lo, 3)

        CHAIN = 2 * NORM_STEPS + 1

        LAST_TURN = BANK_TURNS - 1

        with nc.Block() as block:
            @block.sync
            def _(sp):
                def fetch(par, pair, b, q, projected):
                    sp.wait_ge(proj_done, projected)
                    for n in range(4):
                        head_cols = w_hl[:, n, ds(pair * P, P)].bitcast(F32).rearrange("p (h c) -> p h c", h=2)
                        for t in range(2):
                            sp.dma_start(w_pair[par][:, n, :, t * A_HD:(t + 1) * A_HD].bitcast(F32),
                                         head_cols).then_inc(pair_loaded[par], 16)
                    sp.dma_start(wv_pair[par][:].bitcast(F32),
                                 w_hl[:, 4:6, ds(pair * P, P)].bitcast(F32)).then_inc(pair_loaded[par], 16)

                with sp.Fori(0, BATCH) as b:
                    base = b * (PAIRS * GROUPS)
                    fetch(0, 0, b, 0, base)
                    fetch(1, 1, b, 0, base)
                    with sp.Fori(0, PAIRS // 2 - 1) as q:
                        fetch(0, q * 2 + 2, b, q, base + (q * 2 + 1) * GROUPS)
                        fetch(1, q * 2 + 3, b, q, base + (q * 2 + 2) * GROUPS)

            @block.gpsimd
            def _(pool):
                with pool.Fori(0, 2 * BATCH) as n:
                    inverse_root(pool, norm, g.minus_half[:, 0:NB], n)

            @block.tensor
            def _(pe):
                def project(par, k, loads, before):
                    if k == 0:
                        pe.wait_ge(pair_loaded[par], loads * (9 * 16))
                    pe.wait_ge(proj_hi, before * GROUPS + k)
                    pe.wait_ge(proj_lo, before * QK_GROUPS + min(k, QK_GROUPS))
                    w = w_pair[par]
                    if k < QK_GROUPS:
                        qk, head, half = k // 4, k // 2 % 2, k % 2
                        cols = slice(half * HALF, (half + 1) * HALF)
                        w_hi, w_lo = (w[:, 2 * qk + part, head, :] for part in range(2))
                        todo = split_passes((w_hi, w_lo), (xT_hi[:, cols], xT_lo[:, cols]))
                        for n, (a, r) in enumerate(todo):
                            last = pe.matmul(p_ps[:], a, r, start=n == 0, stop=n == len(todo) - 1)
                    else:
                        for t in range(4):
                            blk = (k - QK_GROUPS) * 4 + t
                            toks = slice(blk * P, (blk + 1) * P)
                            todo = split_passes((xT_hi[:, toks], xT_lo[:, toks]), (wv_pair[par][:, 0, :], wv_pair[par][:, 1, :]))
                            for n, (a, r) in enumerate(todo):
                                last = pe.matmul(p_ps[:, t * P:(t + 1) * P], a, r,
                                                 start=n == 0, stop=n == len(todo) - 1)
                    last.then_inc(proj_done, 1)

                def score(par, i, n, k, h):
                    width = (i + 1) * P
                    if True:
                        pe.wait_ge(exp_done, n * (2 * NB) + (2 * k - 1 + h if k else 0))
                        q = q_st[par][h][:, i * P:(i + 1) * P]
                        for c in range(0, width, HALF):
                            e = min(c + HALF, width)
                            pe.matmul(scores[h][:, c:e], q, k_hh[par][h][:, c:e], start=True, stop=False)
                            last = pe.matmul(scores[h][:, c:e], q, k_ll[par][h][:, c:e], start=False,
                                             stop=e < width)
                        last = pe.matmul(scores[h][:, i * P:width], g.ident_bf[:], g.mask_qk[:],
                                         start=False, stop=True)
                        last.then_inc(scored, 1)

                def turn(i, n, k, turns, h):
                    m = h * ((i + 4) // 4)
                    if True:
                        pe.wait_ge(exp_done, n * (2 * NB) + 2 * k + 1 + h)
                        for c in range(0, i + 1, 4):
                            pe.wait_ge(tr_out[m % 2], n * BANK_TURNS + turns + m // 2)
                            for j in range(c, min(c + 4, i + 1)):
                                last = pe.transpose(tr[m % 2][:, (j - c) * P:(j - c + 1) * P],
                                                    probs[i % 2][:, h, j * P:(j + 1) * P], g.ident[:])
                            last.then_inc(tr_done, 1)
                            m += 1

                def spread(i, step):
                    pe.wait_ge(out_kept, step)
                    pe.wait_ge(inv_ready, step + 1)
                    for h in range(2):
                        last = pe.matmul(o_ps[h * A_HD:(h + 1) * A_HD, P:2 * P],
                                         row_inv[:, i, h:h + 1].to_broadcast([P, A_HD]), g.ident[:],
                                         start=True, stop=True)
                    last.then_inc(inv_bc, 1)

                def weigh(par, i, n, step, turns):
                    pe.wait_ge(inv_sb, step + 1)
                    pe.wait_ge(tr_out[0], n * BANK_TURNS + turns)
                    pe.wait_ge(tr_out[1], n * BANK_TURNS + turns)
                    for j in range(i + 1):
                        for h in range(2):
                            rows = slice(h * A_HD, (h + 1) * A_HD)
                            last = pe.matmul(o_ps[rows, 0:P], v_sb[par][:, j, rows],
                                             probsT[i % 2][:, h, j * P:(j + 1) * P], start=j == 0, stop=j == i)
                    last.then_inc(pv_done, 1)

                def attend(par, pair, loads, first, more, b, extra):
                    n = b * PAIRS + pair
                    turns = 0

                    def projections(groups):
                        for k in groups if more else ():
                            project(1 - par, k, b * (PAIRS // 2) + loads, n + 1)

                    pe.wait_ge(proj_hi, n * GROUPS + GROUPS)
                    pe.wait_ge(proj_lo, n * QK_GROUPS + QK_GROUPS)
                    for k in range(NB):
                        i = NB - 1 - k
                        if k:
                            turn(i + 1, n, k - 1, turns, 0)
                        score(par, i, n, k, 0)
                        if k:
                            turn(i + 1, n, k - 1, turns, 1)
                            turns += (i + 5) // 4
                            spread(i + 1, n * NB + k - 1)
                        elif not first:
                            turn_last(n - 1)
                        if k == 0:
                            projections(GROUPS_OF_STEP[k][:1])
                        score(par, i, n, k, 1)
                        if k:
                            projections(GROUPS_OF_STEP[k][:1])
                            weigh(par, i + 1, n, n * NB + k - 1, turns)
                        elif not first:
                            weigh_last(1 - par, n - 1)
                        projections(GROUPS_OF_STEP[k][1:])

                def turn_last(n):
                    for h in range(2):
                        turn(0, n, NB - 1, LAST_TURN, h)
                    spread(0, n * NB + NB - 1)

                def weigh_last(par, n):
                    weigh(par, 0, n, n * NB + NB - 1, BANK_TURNS)

                def input_turned(b, chained):
                    pe.wait_ge(norm.chain, chained)
                    for c in range(2):
                        pe.wait_ge(tr_out[c], b * (PAIRS * BANK_TURNS))
                        for t in range(4):
                            last = pe.transpose(tr[c][:, t * P:(t + 1) * P], x_norm[:, c * 4 + t, :], g.ident[:])
                        last.then_inc(xT_done, 1)

                def output_block(blk):
                    c, t = blk // 4, blk % 4
                    for hp in range(PAIRS):
                        last = pe.matmul(scores[0][:, blk * P:(blk + 1) * P], outT[:, hp, blk * P:(blk + 1) * P],
                                         w_u[:, hp, :], start=hp == 0, stop=hp == PAIRS - 1)
                    if t == 3:
                        last.then_inc(y_done, 1)

                def input_projected(b, between):
                    between(0)
                    pe.wait_ge(xT_hi_done, b * 2 + 2)
                    pe.wait_ge(xT_lo_done, b * 2 + 2)
                    for k in range(GROUPS):
                        project(0, k, b * (PAIRS // 2) + 1, b * PAIRS)
                        between(k + 1)

                input_turned(0, NORM_STEPS)
                input_projected(0, lambda k: None)
                first_pair(attend, 0)
                with pe.Fori(0, BATCH - 1) as b:
                    other_pairs(pe, attend, b)
                    turn_last(b * PAIRS + PAIRS - 1)
                    weigh_last(1, b * PAIRS + PAIRS - 1)
                    input_turned(b + 1, b * CHAIN + 2 * NORM_STEPS)
                    pe.wait_ge(out_kept, b * (PAIRS * NB) + PAIRS * NB)
                    input_projected(b + 1, lambda k: output_block(k) if k < NB else None)
                    pe.wait_ge(y_used, b * 2 + 2)
                    first_pair(attend, b + 1)
                other_pairs(pe, attend, BATCH - 1)
                turn_last(BATCH * PAIRS - 1)
                weigh_last(1, BATCH * PAIRS - 1)
                pe.wait_ge(out_kept, BATCH * PAIRS * NB)
                for blk in range(NB):
                    output_block(blk)

            def keep_turned_groups(eng, bank, i, n, turns, h):
                m = h * ((i + 4) // 4)
                if True:
                    for c in range(0, i + 1, 4):
                        if m % 2 == bank:
                            width = min(4, i + 1 - c) * P
                            eng.wait_ge(tr_done, n * (2 * BANK_TURNS) + 2 * turns + m + 1)
                            out = probsT[i % 2][:, h, c * P:c * P + width]
                            if bank:
                                ins = eng.tensor_copy(out, tr[bank][:, 0:width])
                            else:
                                ins = eng.activation(out, tr[bank][:, 0:width], ACT.Copy)
                            ins.then_inc(tr_out[bank], 1)
                        m += 1

            @block.scalar
            def _(act):
                def keep_projection(par, k, before):
                    act.wait_ge(proj_done, before * GROUPS + k + 1)
                    if k < QK_GROUPS:
                        qk, head, half = k // 4, k // 2 % 2, k % 2
                        out = (q_st, k_hh)[qk][par][head][:, half * HALF:(half + 1) * HALF]
                        act.activation(out, p_ps[:], ACT.Copy,
                                       scale=KEYS_SCALE if qk else 1.0).then_inc(proj_hi, 1)
                    else:
                        t = (k - QK_GROUPS) * 4
                        act.activation(v_sb[par][:, t:t + 4, :], p_ps[:].rearrange("p (t n) -> p t n", t=4),
                                       ACT.Copy).then_inc(proj_hi, 1)

                def exponentials(i, n, k, h):
                    act.wait_ge(max_ready, n * (2 * NB) + 2 * k + h + 1)
                    width = (i + 1) * P
                    act.activation(probs[i % 2][:, h, 0:width], scores[h][:, 0:width], ACT.Exp,
                                   bias=neg_max[:, i, h:h + 1],
                                   accum_out=row_sum[:, i, h:h + 1]).then_inc(exp_done, 1)

                def attend(par, pair, loads, first, more, b, extra):
                    n = b * PAIRS + pair
                    turns = 0

                    def projections(groups):
                        for k in groups if more else ():
                            keep_projection(1 - par, k, n + 1)

                    for k in range(NB):
                        i = NB - 1 - k
                        if k:
                            keep_turned(i + 1, n, turns)
                            turns += (i + 5) // 4
                            keep_inverse(i + 1, n * NB + k - 1)
                        if k == 0:
                            if not first:
                                keep_last(n - 1)
                            projections(GROUPS_OF_STEP[k][:1])
                        exponentials(i, n, k, 0)
                        if k:
                            projections(GROUPS_OF_STEP[k][:1])
                        exponentials(i, n, k, 1)
                        projections(GROUPS_OF_STEP[k][1:])

                def keep_turned(i, n, turns):
                    for h in range(2):
                        keep_turned_groups(act, 0, i, n, turns, h)

                def keep_inverse(i, step):
                    act.wait_ge(inv_bc, step + 1)
                    act.activation(r_bc[i % 2][:], o_ps[:, P:2 * P], ACT.Copy).then_inc(inv_sb, 1)

                def keep_last(n):
                    keep_turned(0, n, LAST_TURN)
                    keep_inverse(0, n * NB + NB - 1)

                def keep_input(b):
                    for c in range(2):
                        act.wait_ge(xT_done, b * 2 + c + 1)
                        act.activation(xT_hi[:, c * HALF:(c + 1) * HALF], tr[c][:], ACT.Copy).then_inc(xT_hi_done, 1)
                    for k in range(GROUPS):
                        keep_projection(0, k, b * PAIRS)

                keep_input(0)
                first_pair(attend, 0)
                with act.Fori(0, BATCH - 1) as b:
                    other_pairs(act, attend, b)
                    keep_last(b * PAIRS + PAIRS - 1)
                    keep_input(b + 1)
                    first_pair(attend, b + 1)
                other_pairs(act, attend, BATCH - 1)
                keep_last(BATCH * PAIRS - 1)

            @block.vector
            def _(dve):
                def keep_low_part(par, k, before):
                    if k >= QK_GROUPS:
                        return
                    qk, head, half = k // 4, k // 2 % 2, k % 2
                    cols = slice(half * HALF, (half + 1) * HALF)
                    dve.wait_ge(proj_hi, before * GROUPS + k + 1)
                    if qk:
                        dve.scalar_tensor_tensor(k_ll[par][head][:, cols], p_ps[:], KEYS_SCALE,
                                                 k_hh[par][head][:, cols].bitcast(F32), ALU.mult,
                                                 ALU.subtract).then_inc(proj_lo, 1)
                    else:
                        low = q_st[par][head][A_HD:P, cols]
                        dve.tensor_tensor(low, p_ps[A_HD:P, :], low.bitcast(F32), ALU.subtract).then_inc(proj_lo, 1)

                def maximum(i, n, k, h):
                    dve.wait_ge(scored, n * (2 * NB) + 2 * k + h + 1)
                    dve.tensor_reduce(neg_max[:, i, h:h + 1], scores[h][:, 0:(i + 1) * P], AX.X, ALU.max,
                                      negate=True).then_inc(max_ready, 1)

                def attend(par, pair, loads, first, more, b, extra):
                    n = b * PAIRS + pair
                    turns = 0

                    def projections(groups):
                        for k in groups if more else ():
                            keep_low_part(1 - par, k, n + 1)

                    for k in range(NB):
                        i = NB - 1 - k
                        if k:
                            invert(i + 1, n, k - 1)
                            keep_turned_groups(dve, 1, i + 1, n, turns, 0)
                        elif not first:
                            invert(0, n - 1, NB - 1)
                        maximum(i, n, k, 0)
                        if k == 0:
                            if not first:
                                keep_last(n - 1)
                            projections(GROUPS_OF_STEP[k][:1])
                        if k:
                            keep_turned_groups(dve, 1, i + 1, n, turns, 1)
                            turns += (i + 5) // 4
                        maximum(i, n, k, 1)
                        if k:
                            projections(GROUPS_OF_STEP[k][:1])
                        elif not first:
                            keep_output(0, pair - 1, n * NB - 1)
                        projections(GROUPS_OF_STEP[k][1:])
                        if k:
                            keep_output(i + 1, pair, n * NB + k - 1)
                        if extra:
                            extra[k]()

                def invert(i, n, k):
                    dve.wait_ge(exp_done, n * (2 * NB) + 2 * k + 2)
                    dve.reciprocal(row_inv[:, i, :], row_sum[:, i, :]).then_inc(inv_ready, 1)

                def keep_output(i, pair, step):
                    dve.wait_ge(pv_done, step + 1)
                    dve.tensor_tensor(outT[:, pair, i * P:(i + 1) * P], o_ps[:, 0:P], r_bc[i % 2][:],
                                      ALU.mult).then_inc(out_kept, 1)

                def keep_last(n):
                    for h in range(2):
                        keep_turned_groups(dve, 1, 0, n, LAST_TURN, h)

                def keep_input(b):
                    for c in range(2):
                        cols = slice(c * HALF, (c + 1) * HALF)
                        dve.wait_ge(xT_hi_done, b * 2 + c + 1)
                        dve.tensor_tensor(xT_lo[:, cols], tr[c][:], xT_hi[:, cols].bitcast(F32),
                                          ALU.subtract).then_inc(xT_lo_done, 1)
                    for k in range(GROUPS):
                        keep_low_part(0, k, b * PAIRS)

                def finish_pairs(b):
                    invert(0, b * PAIRS + PAIRS - 1, NB - 1)
                    keep_last(b * PAIRS + PAIRS - 1)
                    keep_output(0, PAIRS - 1, b * (PAIRS * NB) + PAIRS * NB - 1)

                def normalized(b, chain, count):
                    return layernorm_parts(dve, chain, lambda blk: g.x[:, b * NB + blk, :],
                                           lambda blk: x_norm[:, blk, :], norm, count)

                def add_bias(b):
                    for c in range(2):
                        dve.wait_ge(y_done, b * 2 + c + 1)
                        src = scores[0][:, c * HALF:(c + 1) * HALF].rearrange("p (t n) -> p t n", t=4)
                        dve.tensor_tensor(y[:, 4 * c:4 * c + 4, :], src, b_u[:].unsqueeze(1).to_broadcast([P, 4, D]),
                                          ALU.add).then_inc(y_used, 1)
                    dve.wait_ge(y_used, b * 2 + 2)

                def finish_batch(b, chain, count):
                    y_of = lambda blk: y[:, blk, :]
                    x_all = g.x[:, ds(b * NB, NB), :]

                    def residual():
                        chain.settle()
                        chain.did(dve.tensor_tensor(x_all, x_all, y[:], ALU.add))
                        chain.settle()

                    return layernorm_parts(dve, chain, y_of, y_of, norm, count)[:-1] + [residual]

                for part in normalized(0, Chain(dve, norm.chain), 0):
                    part()
                keep_input(0)
                first_pair(attend, 0)
                with dve.Fori(0, BATCH - 1) as b:
                    chain = Chain(dve, norm.chain, b * CHAIN + NORM_STEPS)
                    other_pairs(dve, attend, b, normalized(b + 1, chain, b * 2 + 1))
                    finish_pairs(b)
                    keep_input(b + 1)
                    add_bias(b)
                    first_pair(attend, b + 1, finish_batch(b, chain, b * 2 + 2))
                    assert chain.n == CHAIN
                chain = Chain(dve, norm.chain, (BATCH - 1) * CHAIN + NORM_STEPS)
                other_pairs(dve, attend, BATCH - 1)
                finish_pairs(BATCH - 1)
                add_bias(BATCH - 1)
                for part in finish_batch(BATCH - 1, chain, BATCH * 2 - 1):
                    part()

        nc.clear_and_free_semaphores(sems)
        nc.all_engine_barrier()


E_ROUTED, E_SHARED = 8, 2
EXPERTS = E_ROUTED + E_SHARED
HID = 256
HB = HID // P
CHUNKS = NBLK * P // HALF
TOP = 8


def mixture_layer0(nc, g):
    with ExitStack() as ctx:
        def sb(name, shape, dt=F32):
            return ctx.enter_context(nc.sbuf_tensor("m_" + name, shape, dt))

        def sem(name):
            return ctx.enter_context(nc.semaphore("m_" + name))

        w12 = sb("w12", [P, EXPERTS, 2, HID])
        w3 = sb("w3", [P, EXPERTS, HB, D])
        w_hl = [sb(f"w_hl{i}", [P, 2, 2, HID], F32R) for i in range(2)]
        b12 = sb("b12", [P, 2, EXPERTS, HB])
        b3 = sb("b3", [EXPERTS, D])
        gate_hl = sb("gate_hl", [P, 2, E_ROUTED], F32R)
        gate_w = sb("gate_w", [P, E_ROUTED])
        gate_b = sb("gate_b", [E_ROUTED, 1])
        iota = sb("iota", [P, E_ROUTED])
        x_norm = sb("x_norm", [P, NB, D])
        xT_hi = sb("xT_hi", [P, NBLK * P], F32R)
        xT_lo = sb("xT_lo", [P, NBLK * P], F32R)
        acc = sb("acc", [P, NBLK, D])
        gates = sb("gates", [P, NBLK, EXPERTS])
        norm = NormTiles(ctx, nc, "m_norm")

        loaded, prepared = sem("loaded"), sem("prepared")
        xT_done, xT_hi_done, xT_lo_done = sem("xT_done"), sem("xT_hi_done"), sem("xT_lo_done")
        lg_done, lgT_kept, turned, gexp_ready, gexp_done = (sem(n) for n in (
            "lg_done", "lgT_kept", "turned", "gexp_ready", "gexp_done"))
        gates_turned, gatesT_kept, b3_done, b3_kept = (sem(n) for n in (
            "gates_turned", "gatesT_kept", "b3_done", "b3_kept"))
        w_free, w_hi_done, w_split = sem("w_free"), sem("w_hi_done"), sem("w_split")
        up_done, silu_done, glu_done = sem("up_done"), sem("silu_done"), sem("glu_done")
        down_done, weighed, added = sem("down_done"), sem("weighed"), sem("added")

        with ExitStack() as pctx:
            def psb(name, shape, dt=F32):
                return pctx.enter_context(nc.sbuf_tensor("m_" + name, shape, dt))

            lgT = psb("lgT", [E_ROUTED, SEQ])
            first = psb("first", [P, 1])
            lg = psb("lg", [P, NB, E_ROUTED])
            top = psb("top", [P, NB, TOP])
            idx = psb("idx", [P, NB, TOP], U32)
            idx_f = psb("idx_f", [P, NB, 2])
            diff = psb("diff", [P, NB, E_ROUTED + 1])
            g_exp = psb("g_exp", [P, NB, E_ROUTED + 1])
            g_sum = psb("g_sum", [P, NB])
            weight = psb("weight", [P, NB, 2])
            hot = [psb(f"hot{i}", [P, NB, E_ROUTED]) for i in range(2)]
            gates_b = psb("gates_b", [P, NB, EXPERTS])
            gatesT = psb("gatesT", [EXPERTS, SEQ])
            tr = [pctx.enter_context(nc.psum_tensor(f"m_tr{i}", [P, HALF], F32)) for i in range(2)]
            lg_ps = pctx.enter_context(nc.psum_tensor("m_lg_ps", [E_ROUTED, SEQ], F32))
            lgt_ps = pctx.enter_context(nc.psum_tensor("m_lgt_ps", [P, HALF], F32))
            gt_ps = pctx.enter_context(nc.psum_tensor("m_gt_ps", [EXPERTS, SEQ], F32))

            CHAIN = NORM_STEPS + 2 * NB + 13

            with nc.Block() as block:
                @block.sync
                def _(sp):
                    small = ((gate_w[:], g.inputs["L0_ffn_gate_w"]), (gate_b[:], g.inputs["L0_ffn_gate_b"].rearrange("(e a) -> e a", a=1)),
                             (iota[:], g.inputs["c_iota"].partition_broadcast(P)),
                             (b3[0:E_ROUTED, :], g.inputs["L0_ffn_rb3"]), (b3[E_ROUTED:EXPERTS, :], g.inputs["L0_ffn_sb3"]))
                    for out, src in small:
                        sp.dma_start(out, src).then_inc(loaded, 16)
                    with nc.allow_non_contiguous_dma(reason="biases, one value per partition"):
                        for e0, n, letter in ((0, E_ROUTED, "r"), (E_ROUTED, E_SHARED, "s")):
                            for j in range(2):
                                src = g.inputs[f"L0_ffn_{letter}b{j + 1}"].rearrange("e (h p) -> p (e h)", p=P)
                                sp.dma_start(b12[:, j, e0:e0 + n, :].rearrange("p e h -> p (e h)"),
                                             src).then_inc(loaded, 16)
                                sp.dma_start(w12[:, e0:e0 + n, j, :], g.inputs[f"L0_ffn_{letter}w{j + 1}"]
                                             .rearrange("e p n -> p e n")).then_inc(loaded, 16)
                            for h in range(HB):
                                sp.dma_start(w3[:, e0:e0 + n, h, :], g.inputs[f"L0_ffn_{letter}w3"]
                                             [:, h * P:(h + 1) * P, :].rearrange("e p n -> p e n")).then_inc(loaded, 16)
                    sp.wait_ge(loaded, 17 * 16)

                @block.gpsimd
                def _(pool):
                    pool.memset(gates[:, :, E_ROUTED:EXPERTS], 1.0 / E_SHARED).then_inc(prepared, 1)
                    with pool.Fori(0, BATCH) as n:
                        inverse_root(pool, norm, g.minus_half[:, 0:NB], n)

                @block.tensor
                def _(pe):
                    with pe.Fori(0, BATCH) as b:
                        pe.wait_ge(norm.chain, b * CHAIN + NORM_STEPS)
                        pe.wait_ge(b3_kept, b * 2)
                        for c in range(2):
                            for t in range(4):
                                last = pe.transpose(tr[c][:, t * P:(t + 1) * P], x_norm[:, c * 4 + t, :], g.ident[:])
                            last.then_inc(xT_done, 1)
                        pe.wait_ge(prepared, 4)
                        for c in range(2):
                            pe.wait_ge(xT_lo_done, b * 2 + c + 1)
                            cols = ds(b * SEQ + c * HALF, HALF)
                            todo = split_passes((gate_hl[:, 0, :], gate_hl[:, 1, :]), (xT_hi[:, cols], xT_lo[:, cols]))
                            for n, (a, r) in enumerate(todo):
                                last = pe.matmul(lg_ps[:, c * HALF:(c + 1) * HALF], a, r, start=n == 0, stop=n == 2)
                        last.then_inc(lg_done, 1)
                        pe.wait_ge(lgT_kept, b + 1)
                        for t in range(NB):
                            last = pe.matmul(lgt_ps[:, t * E_ROUTED:(t + 1) * E_ROUTED], lgT[:, t * P:(t + 1) * P],
                                             g.ident[0:E_ROUTED, 0:E_ROUTED], start=True, stop=True)
                        last.then_inc(turned, 1)
                        pe.wait_ge(norm.chain, b * CHAIN + CHAIN)
                        for t in range(NB):
                            last = pe.transpose(gt_ps[:, t * P:(t + 1) * P], gates_b[:, t, :], g.ident[:])
                        last.then_inc(gates_turned, 1)
                        pe.wait_ge(gatesT_kept, b + 1)
                        for c in range(2):
                            for t in range(4):
                                blk = c * 4 + t
                                last = pe.matmul(tr[c][:, t * P:(t + 1) * P], gatesT[:, blk * P:(blk + 1) * P],
                                                 b3[:], start=True, stop=True)
                            last.then_inc(b3_done, 1)

                @block.scalar
                def _(act):
                    act.wait_ge(loaded, 17 * 16)
                    act.activation(gate_hl[:, 0, :], gate_w[:], ACT.Copy).then_inc(prepared, 1)
                    with act.Fori(0, BATCH) as b:
                        for c in range(2):
                            act.wait_ge(xT_done, b * 2 + c + 1)
                            act.activation(xT_hi[:, ds(b * SEQ + c * HALF, HALF)], tr[c][:],
                                           ACT.Copy).then_inc(xT_hi_done, 1)
                        act.wait_ge(lg_done, b + 1)
                        act.activation(lgT[:], lg_ps[:], ACT.Identity, bias=gate_b[:]).then_inc(lgT_kept, 1)
                        act.wait_ge(gexp_ready, b + 1)
                        act.activation(g_exp[:], diff[:], ACT.Exp).then_inc(gexp_done, 1)
                        act.wait_ge(gates_turned, b + 1)
                        act.activation(gatesT[:], gt_ps[:], ACT.Copy).then_inc(gatesT_kept, 1)

                @block.vector
                def _(dve):
                    dve.wait_ge(prepared, 2)
                    dve.tensor_tensor(gate_hl[:, 1, :], gate_w[:], gate_hl[:, 0, :].bitcast(F32),
                                      ALU.subtract).then_inc(prepared, 1)
                    dve.tensor_copy(gates_b[:, :, E_ROUTED:EXPERTS], gates[:, 0:NB, E_ROUTED:EXPERTS]
                                    ).then_inc(prepared, 1)
                    with dve.Fori(0, BATCH) as b:
                        chain = Chain(dve, norm.chain, b * CHAIN)
                        layernorm(dve, chain, lambda blk: g.x[:, b * NB + blk, :], lambda blk: x_norm[:, blk, :], norm, b)
                        for c in range(2):
                            cols = ds(b * SEQ + c * HALF, HALF)
                            dve.wait_ge(xT_hi_done, b * 2 + c + 1)
                            dve.tensor_tensor(xT_lo[:, cols], tr[c][:], xT_hi[:, cols].bitcast(F32),
                                              ALU.subtract).then_inc(xT_lo_done, 1)
                        dve.wait_ge(turned, b + 1)
                        chain.did(dve.tensor_copy(lg[:], lgt_ps[:, 0:NB * E_ROUTED].rearrange("p (t e) -> p t e", t=NB)))
                        chain.settle()
                        chain.did(dve.tensor_copy(first[:], lg[:, 0, 0:1]))
                        for t in range(NB):
                            chain.did(dve.max(top[:, t, :], lg[:, t, :]))
                        chain.settle()
                        largest = top[:, :, 0:1]
                        chain.did(dve.tensor_tensor(diff[:, :, 0:E_ROUTED], lg[:],
                                                    largest.to_broadcast([P, NB, E_ROUTED]), ALU.subtract))
                        dve.tensor_tensor(diff[:, :, E_ROUTED:], top[:, :, 1:2], largest, ALU.subtract
                                          ).then_inc(gexp_ready, 1)
                        for t in range(NB):
                            chain.did(dve.max_index(idx[:, t, :], top[:, t, :], lg[:, t, :]))
                        chain.settle()
                        chain.did(dve.tensor_copy(idx_f[:], idx[:, :, 0:2]))
                        dve.wait_ge(gexp_done, b + 1)
                        chain.did(dve.tensor_reduce(g_sum[:], g_exp[:, :, 0:E_ROUTED], AX.X, ALU.add))
                        chain.settle()
                        chain.did(dve.reciprocal(weight[:, :, 0], g_sum[:]))
                        for j in range(2):
                            chain.did(dve.tensor_tensor(hot[j][:], iota[:].unsqueeze(1).to_broadcast([P, NB, E_ROUTED]),
                                                        idx_f[:, :, j:j + 1].to_broadcast([P, NB, E_ROUTED]),
                                                        ALU.is_equal))
                        chain.settle()
                        chain.did(dve.tensor_tensor(weight[:, :, 1:2], weight[:, :, 0:1], g_exp[:, :, E_ROUTED:],
                                                    ALU.mult))
                        chain.settle()
                        for j in range(2):
                            chain.did(dve.tensor_tensor(hot[j][:], hot[j][:],
                                                        weight[:, :, j:j + 1].to_broadcast([P, NB, E_ROUTED]), ALU.mult))
                        chain.settle()
                        chain.did(dve.tensor_tensor(gates[:, ds(b * NB, NB), 0:E_ROUTED], hot[0][:], hot[1][:], ALU.add))
                        chain.did(dve.tensor_tensor(gates_b[:, :, 0:E_ROUTED], hot[0][:], hot[1][:], ALU.add))
                        chain.settle()
                        assert chain.n == CHAIN, chain.n
                        for c in range(2):
                            dve.wait_ge(b3_done, b * 2 + c + 1)
                            dve.tensor_copy(acc[:, ds(b * NB + c * 4, 4), :],
                                            tr[c][:].rearrange("p (t n) -> p t n", t=4)).then_inc(b3_kept, 1)

        with ExitStack() as ectx:
            def esb(name, shape, dt=F32):
                return ectx.enter_context(nc.sbuf_tensor("m_" + name, shape, dt))

            silu = [esb(f"silu{i}", [P, HALF]) for i in range(2)]
            glu = [[esb(f"glu{i}{h}", [P, HALF]) for h in range(HB)] for i in range(2)]
            bias = [esb(f"bias{i}", [P, 2, HB]) for i in range(2)]
            taken = esb("taken", [P, 1])
            part = [esb(f"part{i}", [P, 4, D]) for i in range(2)]
            up = [[ectx.enter_context(nc.psum_tensor(f"m_up{i}{j}", [P, HALF], F32)) for j in range(2)]
                  for i in range(2)]
            down = [ectx.enter_context(nc.psum_tensor(f"m_down{i}", [P, HALF], F32)) for i in range(2)]

            def experts(eng, run):
                with eng.Fori(0, EXPERTS // 2 - 1) as q:
                    for par in range(2):
                        run(par, q, True)
                for par in range(2):
                    run(par, EXPERTS // 2 - 1, par == 0)

            def chunk_pairs(eng, par, q, run):
                with eng.Fori(0, CHUNKS // 2) as t:
                    run(t, (q * 2 + par) * CHUNKS + t * 2)

            with nc.Block() as block:
                @block.gpsimd
                def _(pool):
                    def split_hi(par, e):
                        pool.tensor_copy(w_hl[par][:, 0], w12[:, e]).then_inc(w_hi_done, 1)
                        pool.tensor_copy(bias[par][:], b12[:, :, e, :]).then_inc(w_hi_done, 1)

                    def expert(par, q, more):
                        if more:
                            pool.wait_ge(glu_done, (q * 2 + par) * (CHUNKS * HB))
                            pool.tensor_tensor(taken[:], norm.mean[:, 0:1], norm.mean[:, 0:1], ALU.add
                                               ).then_inc(w_free, 1)
                            split_hi(1 - par, q * 2 + par + 1)

                    split_hi(0, 0)
                    experts(pool, expert)

                @block.tensor
                def _(pe):
                    def expert(par, q, more):
                        e = q * 2 + par

                        def chunks(t, before):
                            pe.wait_ge(w_split, e + 1)

                            def raise_(c, h):
                                cols = ds(t * (2 * HALF) + c * HALF, HALF)
                                pe.wait_ge(glu_done, before * HB + max(c * HB + h - 1, 0))
                                for j in range(2):
                                    w = [w_hl[par][:, s, j, h * P:(h + 1) * P] for s in range(2)]
                                    todo = split_passes(w, (xT_hi[:, cols], xT_lo[:, cols]))
                                    for n, (a, r) in enumerate(todo):
                                        last = pe.matmul(up[h][j][:], a, r, start=n == 0, stop=n == 2)
                                last.then_inc(up_done, 1)

                            def lower(c):
                                n = before + c
                                pe.wait_ge(weighed, before)
                                for h in range(HB):
                                    pe.wait_ge(glu_done, n * HB + h + 1)
                                    for b in range(4):
                                        last = pe.matmul(down[c][:, b * P:(b + 1) * P], glu[c][h][:, b * P:(b + 1) * P],
                                                         w3[:, e, h, :], start=h == 0 and b == 0, stop=h == HB - 1,
                                                         skip_group_check=True)
                                last.then_inc(down_done, 1)

                            raise_(0, 0)
                            raise_(0, 1)
                            raise_(1, 0)
                            lower(0)
                            raise_(1, 1)
                            lower(1)

                        chunk_pairs(pe, par, q, chunks)

                    experts(pe, expert)

                @block.scalar
                def _(act):
                    def expert(par, q, more):
                        def chunks(t, before):
                            for u in range(2 * HB):
                                h = u % HB
                                act.wait_ge(up_done, before * HB + u + 1)
                                act.activation(silu[h][:], up[h][0][:], ACT.Silu,
                                               bias=bias[par][:, 0, h:h + 1]).then_inc(silu_done, 1)

                        chunk_pairs(act, par, q, chunks)

                    experts(act, expert)

                @block.vector
                def _(dve):
                    def expert(par, q, more):
                        e = q * 2 + par

                        def chunks(t, before):
                            def gate_up(c, h):
                                dve.wait_ge(silu_done, before * HB + c * HB + h + 1)
                                dve.scalar_tensor_tensor(glu[c][h][:], up[h][1][:], bias[par][:, 1, h:h + 1], silu[h][:],
                                                         ALU.add, ALU.mult).then_inc(glu_done, 1)

                            def weigh(c):
                                dve.wait_ge(down_done, before + c + 1)
                                dve.wait_ge(added, before)
                                dve.tensor_tensor(part[c][:], down[c][:].rearrange("p (t n) -> p t n", t=4),
                                                  gates[:, ds(t * 8 + c * 4, 4), e].unsqueeze(2).to_broadcast([P, 4, D]),
                                                  ALU.mult).then_inc(weighed, 1)
                                sums = acc[:, ds(t * 8 + c * 4, 4), :]
                                dve.wait_ge(weighed, before + c + 1)
                                dve.tensor_tensor(sums, sums, part[c][:], ALU.add).then_inc(added, 1)

                            gate_up(0, 0)
                            gate_up(0, 1)
                            gate_up(1, 0)
                            weigh(0)
                            gate_up(1, 1)
                            weigh(1)

                        if more:
                            split_lo(1 - par, e + 1)
                        chunk_pairs(dve, par, q, chunks)

                    def split_lo(par, e):
                        dve.wait_ge(w_hi_done, e * 2 + 2)
                        dve.tensor_tensor(w_hl[par][:, 1], w12[:, e], w_hl[par][:, 0].bitcast(F32),
                                          ALU.subtract).then_inc(w_split, 1)

                    split_lo(0, 0)
                    experts(dve, expert)

            with nc.Block() as block:
                @block.gpsimd
                def _(pool):
                    with pool.Fori(0, BATCH) as n:
                        inverse_root(pool, norm, g.minus_half[:, 0:NB], n + BATCH)

                @block.vector
                def _(dve):
                    with dve.Fori(0, BATCH) as b:
                        chain = Chain(dve, norm.chain, BATCH * CHAIN + b * (NORM_STEPS + 1))
                        y_of = lambda blk: acc[:, b * NB + blk, :]
                        layernorm(dve, chain, y_of, y_of, norm, b + BATCH)
                        batch = g.x[:, ds(b * NB, NB), :]
                        chain.did(dve.tensor_tensor(batch, batch, acc[:, ds(b * NB, NB), :], ALU.add))
                        chain.settle()


HEADS, KV, HD = 16, 4, 8
GQ = HEADS // KV
LAT = 32
WINDOW = 32
QK = (HEADS + KV) * HD
SLOT = 32
REPS = SLOT // HD
LOCAL_W = P + WINDOW
RMS_EPS = 1e-6


def attention_layer1(nc, g, local):
    tag = "l_" if local else "g_"
    with ExitStack() as ctx:
        def sb(name, shape, dt=F32):
            return ctx.enter_context(nc.sbuf_tensor(tag + name, shape, dt))

        def sem(name):
            return ctx.enter_context(nc.semaphore(tag + name))

        w_in = sb("w_in", [P, 192])
        w_up = sb("w_up", [LAT, 2 * KV * HD])
        w_o = sb("w_o", [P, D])
        norm_w = sb("norm_w", [P, 1])
        cos, sin = sb("cos", [P, NB, HD // 2]), sb("sin", [P, NB, HD // 2])
        normed = sb("normed", [P, NB, D])
        normedT = sb("normedT", [P, SEQ])
        latT = sb("latT", [LAT, SEQ])
        qk = sb("qk", [P, NB, QK])
        squares = sb("squares", [P, NB, QK])
        part = [sb(f"part{i}", [P, NB * QK // 2]) for i in range(4)]
        turned = sb("turned", [P, NB, QK])
        ssq, rs = sb("ssq", [P, NB * (HEADS + KV)]), sb("rs", [P, NB * (HEADS + KV)])
        newton = sb("newton", [P, NB * (HEADS + KV)])
        ss_h, rs_h = sb("ss_h", [P, NB]), sb("rs_h", [P, NB])
        q_slots = [sb(f"q_slots{j}", [P, NB, P], F32R) for j in range(GQ)]
        k_slots = sb("k_slots", [P, NB, P], F32R)
        values = sb("values", [P, NB, KV, SLOT])
        qT = [sb(f"qT{j}", [P, SEQ], F32R) for j in range(GQ)]
        kT = [sb(f"kT{h}", [P, SEQ], F32R) for h in range(KV)]
        PW = LOCAL_W if local else SEQ
        probsT = [sb(f"probsT{i}", [P, GQ, PW]) for i in range(2)]
        outT = [sb(f"outT{i}", [P, SEQ]) for i in range(2)]
        inv = sb("inv", [P, NB, GQ])
        att = sb("att", [P, NB, D])
        attT = sb("attT", [P, SEQ])

        s_ps = [ctx.enter_context(nc.psum_tensor(f"{tag}s_ps{i}", [P, SEQ], F32)) for i in range(2)]
        o_ps = ctx.enter_context(nc.psum_tensor(f"{tag}o_ps", [P, SEQ], F32))
        x_ps = ctx.enter_context(nc.psum_tensor(f"{tag}x_ps", [P, SEQ], F32))

        loaded, scaled, zeroed = sem("loaded"), sem("scaled"), sem("zeroed")
        chain, var_ready, rs_ready = sem("chain"), sem("var_ready"), sem("rs_ready")
        normedT_done, normedT_kept, lat_done, lat_kept = (sem(n) for n in (
            "normedT_done", "normedT_kept", "lat_done", "lat_kept"))
        qkv_done, qk_kept, v_kept, squared = sem("qkv_done"), sem("qk_kept"), sem("v_kept"), sem("squared")
        qk_var, qk_root = sem("qk_var"), sem("qk_root")
        half_rot, q_hi, k_hi = sem("half_rot"), sem("q_hi"), sem("k_hi")
        kT_done, kT_kept_act, kT_kept_dve = sem("kT_done"), sem("kT_kept_act"), sem("kT_kept_dve")
        qT_done, qT_kept = sem("qT_done"), [sem("qT_kept_act"), sem("qT_kept_dve")]
        scored, exp_done, pv_done, o_kept = sem("scored"), sem("exp_done"), sem("pv_done"), sem("o_kept")
        back_done, att_kept, attT_done, attT_kept, out_done = (sem(n) for n in (
            "back_done", "att_kept", "attT_done", "attT_kept", "out_done"))

        names = {False: ("g_wq", "g_kv_down", "g_wo", "norm1_w", "c_rope_g"),
                 True: ("l_wq", "l_wk", "l_wo", "norm2_w", "c_rope_l")}[local]
        wq, wk, wo, nw = (g.inputs[f"L1_attn_{n}"] for n in names[:4])
        rope = g.inputs[names[4]]
        UNITS = KV * NB if local else KV * NB * GQ
        CHAIN_NORMED, CHAIN_TURNED = 3, 13
        CHAIN_KEYS = CHAIN_TURNED + 1
        CHAIN = CHAIN_KEYS + GQ + KV * GQ + 1

        with nc.Block() as block:
            @block.sync
            def _(sp):
                sp.dma_start(w_in[:, 0:D], wq).then_inc(loaded, 16)
                sp.dma_start(w_in[:, D:D + 32], wk).then_inc(loaded, 16)
                if local:
                    sp.dma_start(w_in[:, D + 32:D + 64], g.inputs["L1_attn_l_wv"]).then_inc(loaded, 16)
                    sp.dma_start(w_up[:, 0:32], g.inputs["L1_attn_g_k_up"]).then_inc(loaded, 16)
                else:
                    sp.dma_start(w_up[:, 0:32], g.inputs["L1_attn_g_k_up"]).then_inc(loaded, 16)
                    sp.dma_start(w_up[:, 32:64], g.inputs["L1_attn_g_v_up"]).then_inc(loaded, 16)
                sp.dma_start(w_o[:], wo).then_inc(loaded, 16)
                sp.dma_start(norm_w[:], nw.rearrange("(p a) -> p a", a=1)).then_inc(loaded, 16)
                sp.dma_start(cos[:], rope[0].rearrange("(t p) n -> p t n", p=P)).then_inc(loaded, 16)
                sp.dma_start(sin[:], rope[1].rearrange("(t p) n -> p t n", p=P)).then_inc(loaded, 16)

            @block.gpsimd
            def _(pool):
                for j in range(GQ):
                    pool.memset(q_slots[j][:].bitcast(F32), 0.0)
                pool.memset(k_slots[:].bitcast(F32), 0.0)
                pool.memset(values[:], 0.0).then_inc(zeroed, 1)
                pool.wait_ge(zeroed, 1)
                pool.memset(values[:, :, :, HD:HD + 1], 1.0)

            @block.vector
            def _(dve):
                for h in range(KV):
                    dve.memset(kT[h][:].bitcast(F32), 0.0)
                dve.wait_ge(loaded, 8 * 16)
                width = 192 if local else 160
                dve.tensor_scalar(w_in[:, 0:width], w_in[:, 0:width], norm_w[:], None, ALU.mult)

        heads = QK // HD
        as_pairs = lambda t: t[:].rearrange("p t (h n two) -> p t h n two", h=heads, two=2)
        even, odd = (as_pairs(qk)[:, :, :, :, c] for c in range(2))
        t_even, t_odd = (as_pairs(turned)[:, :, :, :, c] for c in range(2))
        parts = [p[:].rearrange("p (t h n) -> p t h n", t=NB, h=heads) for p in part]
        spread = lambda t: t[:].unsqueeze(2).to_broadcast([P, NB, heads, HD // 2])
        slots = lambda t: t[:].rearrange("p t (s r d) -> p t s r d", s=KV, r=REPS)
        q_of = lambda j: turned[:, :, 0:HEADS * HD].rearrange("p t (s j d) -> p t s j d", s=KV, j=GQ)[:, :, :, j, :]
        k_of = turned[:, :, HEADS * HD:QK].rearrange("p t (s d) -> p t s d", s=KV)

        def q_cols(kb):
            lo, hi = kb * P, min(kb * P + LOCAL_W, SEQ) if local else SEQ
            starts = [lo] + ([HALF] if lo < HALF < hi else [])
            return [(a, min(hi, a // HALF * HALF + HALF)) for a in starts]

        with nc.Block() as block:
            @block.gpsimd
            def _(pool):
                with pool.Fori(0, BATCH) as b:
                    if not local:
                        inverse_root(pool, g.norm1, g.minus_half[:, 0:NB], b)
                    pool.wait_ge(var_ready, b + 1)
                    pool.tensor_tensor(rs_h[:], ss_h[:], g.minus_half[:, 0:NB], ALU.pow).then_inc(rs_ready, 1)
                    pool.wait_ge(qk_kept, b * 2 + 2)
                    pool.tensor_tensor(parts[2], even, spread(sin), ALU.mult).then_inc(half_rot, 1)
                    pool.tensor_tensor(parts[3], odd, spread(cos), ALU.mult).then_inc(half_rot, 1)

            @block.tensor
            def _(pe):
                with pe.Fori(0, BATCH) as b:
                    pe.wait_ge(chain, b * CHAIN + CHAIN_NORMED)
                    for blk in range(NB):
                        last = pe.transpose(x_ps[:, blk * P:(blk + 1) * P], normed[:, blk, :], g.ident[:])
                    last.then_inc(normedT_done, 1)
                    pe.wait_ge(normedT_kept, b + 1)
                    if not local:
                        for c in range(2):
                            last = pe.matmul(o_ps[0:LAT, c * HALF:(c + 1) * HALF], w_in[:, D:D + LAT],
                                             normedT[:, c * HALF:(c + 1) * HALF], start=True, stop=True)
                        last.then_inc(lat_done, 1)
                    for blk in range(NB):
                        out = s_ps[blk // 4][:, blk % 4 * 256:blk % 4 * 256 + 192]
                        rows = slice(blk * P, (blk + 1) * P)
                        if local:
                            last = pe.matmul(out, normedT[:, rows], w_in[:], start=True, stop=True)
                        else:
                            pe.matmul(out[:, 0:D], normedT[:, rows], w_in[:, 0:D], start=True, stop=True)
                            if blk == 0:
                                pe.wait_ge(lat_kept, b + 1)
                            last = pe.matmul(out[:, D:], latT[:, rows], w_up[:], start=True, stop=True)
                        if blk % 4 == 3:
                            last.then_inc(qkv_done, 1)
                    pe.wait_ge(chain, b * CHAIN + CHAIN_KEYS)
                    for blk in range(NB):
                        last = pe.transpose(x_ps[:, blk * P:(blk + 1) * P], k_slots[:, blk, :].bitcast(F32), g.ident[:])
                    last.then_inc(kT_done, 1)
                    for j in range(GQ):
                        pe.wait_ge(chain, b * CHAIN + CHAIN_KEYS + 1 + j)
                        if j == 1:
                            pe.wait_ge(kT_kept_act, b * 2 + 2)
                            pe.wait_ge(kT_kept_dve, b * 2 + 2)
                        if j >= 2:
                            pe.wait_ge(qT_kept[j % 2], b * 2 + 1)
                        for blk in range(NB):
                            last = pe.transpose((o_ps, x_ps)[j % 2][:, blk * P:(blk + 1) * P],
                                                q_slots[j][:, blk, :].bitcast(F32), g.ident[:])
                        last.then_inc(qT_done, 1)
                    pe.wait_ge(qT_kept[0], b * 2 + 2)
                    pe.wait_ge(qT_kept[1], b * 2 + 2)

                    def weigh(h, kb, n):
                        pe.wait_ge(exp_done, b * UNITS + (n + 1) * (1 if local else GQ))
                        if kb == 0:
                            pe.wait_ge(o_kept, b * KV + h)
                        for a, e in q_cols(kb):
                            first = (kb == 0 and a == 0) or (a == HALF and (kb == 3 if local else kb == 0))
                            for j in range(GQ):
                                col = a - kb * P if local else a
                                last = pe.matmul(o_ps[j * SLOT:(j + 1) * SLOT, a:e], values[:, kb, h, :],
                                                 probsT[n % 2][:, j, col:col + e - a], start=first, stop=True,
                                                 skip_group_check=True)
                        last.then_inc(pv_done, 1)

                    def turn_back(h):
                        pe.wait_ge(o_kept, b * KV + h + 1)
                        if h:
                            pe.wait_ge(att_kept, b * KV + h)
                        for blk in range(NB):
                            last = pe.transpose(x_ps[:, blk * P:(blk + 1) * P], outT[h % 2][:, blk * P:(blk + 1) * P],
                                                g.ident[:])
                        last.then_inc(back_done, 1)

                    u = 0
                    for h in range(KV):
                        for kb in range(NB):
                            n = h * NB + kb
                            for j in range(GQ):
                                if j == 0 or not local:
                                    if u >= 2:
                                        pe.wait_ge(exp_done, b * UNITS + u - 1)
                                ps = s_ps[u % 2]
                                cols = q_cols(kb)
                                off = j * 256 - kb * P if local else 0
                                for c, (a, e) in enumerate(cols):
                                    if local and c:
                                        continue
                                    if local:
                                        e = cols[-1][1]
                                    pe.matmul(ps[:, a + off:e + off], kT[h][:, kb * P:(kb + 1) * P], qT[j][:, a:e],
                                              start=not local or j % 2 == 0, stop=False, skip_group_check=True)
                                a, e = cols[0][0], cols[-1][1]
                                mw = e - a if local else P
                                last = pe.matmul(ps[:, a + off:a + off + mw], g.ident_bf[:],
                                                 (g.mask_window if local else g.mask_kq)[:, 0:mw],
                                                 start=False, stop=True, skip_group_check=True)
                                if not local or j == GQ - 1:
                                    last.then_inc(scored, 1)
                                    u += 1
                            if n:
                                weigh((n - 1) // NB, (n - 1) % NB, n - 1)
                            if n and n % NB == 1 and h:
                                turn_back(h - 1)
                    weigh(KV - 1, NB - 1, KV * NB - 1)
                    turn_back(KV - 1)
                    pe.wait_ge(att_kept, b * KV + KV)
                    for blk in range(NB):
                        last = pe.transpose(x_ps[:, blk * P:(blk + 1) * P], att[:, blk, :], g.ident[:])
                    last.then_inc(attT_done, 1)
                    pe.wait_ge(attT_kept, b + 1)
                    for blk in range(NB):
                        last = pe.matmul(o_ps[:, blk * P:(blk + 1) * P], attT[:, blk * P:(blk + 1) * P], w_o[:],
                                         start=True, stop=True)
                    last.then_inc(out_done, 1)

            @block.scalar
            def _(act):
                with act.Fori(0, BATCH) as b:
                    act.wait_ge(normedT_done, b + 1)
                    act.activation(normedT[:], x_ps[:], ACT.Copy).then_inc(normedT_kept, 1)
                    if not local:
                        act.wait_ge(lat_done, b + 1)
                        act.activation(latT[:], o_ps[0:LAT, :], ACT.Copy).then_inc(lat_kept, 1)
                    for c in range(2):
                        act.wait_ge(qkv_done, b * 2 + c + 1)
                        src = s_ps[c][:].rearrange("p (t n) -> p t n", t=4)
                        act.activation(qk[:, 4 * c:4 * c + 4, :], src[:, :, 0:QK], ACT.Copy).then_inc(qk_kept, 1)
                    act.wait_ge(qk_kept, b * 2 + 2)
                    act.activation(squares[:], qk[:], ACT.Square).then_inc(squared, 1)
                    act.wait_ge(qk_var, b + 1)
                    act.activation(rs[:], ssq[:], ACT.Sqrt).then_inc(qk_root, 1)
                    act.wait_ge(chain, b * CHAIN + CHAIN_TURNED)
                    for r in range(2):
                        act.activation(slots(k_slots)[:, :, :, r, :], k_of, ACT.Copy).then_inc(k_hi, 1)
                    for j in range(GQ):
                        for r in (0, 2):
                            act.activation(slots(q_slots[j])[:, :, :, r, :], q_of(j), ACT.Copy).then_inc(q_hi, 1)
                    act.wait_ge(kT_done, b + 1)
                    for h in range(2):
                        rows = slice(h * SLOT, (h + 1) * SLOT)
                        act.activation(kT[h][rows, :], x_ps[rows, :], ACT.Copy).then_inc(kT_kept_act, 1)
                    for j in (0, 2):
                        act.wait_ge(qT_done, b * GQ + j + 1)
                        act.activation(qT[j][:], o_ps[:], ACT.Copy).then_inc(qT_kept[0], 1)
                    u = 0
                    for n in range(KV * NB):
                        kb = n % NB
                        for j in range(1 if local else GQ):
                            act.wait_ge(scored, b * UNITS + u + 1)
                            if n >= 2 and j == 0:
                                act.wait_ge(pv_done, b * (KV * NB) + n - 1)
                            if local:
                                w = min(LOCAL_W, SEQ - kb * P)
                                out = probsT[n % 2][:, :, 0:w]
                                src = s_ps[u % 2][:].rearrange("p (j n) -> p j n", j=GQ)[:, :, 0:w]
                            else:
                                out, src = probsT[n % 2][:, j, kb * P:SEQ], s_ps[u % 2][:, kb * P:SEQ]
                            act.activation(out, src, ACT.Exp, scale=float(HD) ** -0.5).then_inc(exp_done, 1)
                            u += 1
                    act.wait_ge(attT_done, b + 1)
                    act.activation(attT[:], x_ps[:], ACT.Copy).then_inc(attT_kept, 1)

            @block.vector
            def _(dve):
                with dve.Fori(0, BATCH) as b:
                    own = Chain(dve, chain, b * CHAIN)
                    hidden = g.hidden[:, ds(b * NB, NB), :]
                    if not local:
                        norm_chain = Chain(dve, g.norm1.chain, b * NORM_STEPS)
                        layernorm(dve, norm_chain, lambda blk: g.x[:, b * NB + blk, :],
                                  lambda blk: g.hidden[:, b * NB + blk, :], g.norm1, b)
                    own.did(dve.tensor_tensor(normed[:], hidden, hidden, ALU.mult))
                    own.settle()
                    own.did(dve.tensor_reduce(ss_h[:], normed[:], AX.X, ALU.add))
                    own.settle()
                    dve.tensor_scalar(ss_h[:], ss_h[:], 1.0 / D, RMS_EPS, ALU.mult, ALU.add).then_inc(var_ready, 1)
                    dve.wait_ge(rs_ready, b + 1)
                    own.did(dve.tensor_tensor(normed[:], hidden, rs_h[:].unsqueeze(2).to_broadcast([P, NB, D]), ALU.mult))
                    assert own.n == CHAIN_NORMED
                    for c in range(2):
                        dve.wait_ge(qk_kept, b * 2 + c + 1)
                        src = s_ps[c][:].rearrange("p (t n) -> p t n", t=4)[:, :, QK:192]
                        dve.tensor_copy(values[:, 4 * c:4 * c + 4, :, 0:HD],
                                        src.rearrange("p t (s d) -> p t s d", s=KV)).then_inc(v_kept, 1)
                    own.did(dve.tensor_tensor(parts[0], even, spread(cos), ALU.mult))
                    own.did(dve.tensor_tensor(parts[1], odd, spread(sin), ALU.mult))
                    dve.wait_ge(squared, b + 1)
                    own.did(dve.tensor_reduce(ssq[:], squares[:].rearrange("p t (h d) -> p (t h) d", d=HD), AX.X, ALU.add))
                    own.settle()
                    dve.tensor_scalar(ssq[:], ssq[:], 1.0 / HD, RMS_EPS, ALU.mult, ALU.add).then_inc(qk_var, 1)
                    own.did(dve.tensor_tensor(t_even, parts[0], parts[1], ALU.subtract))
                    dve.wait_ge(half_rot, b * 2 + 2)
                    own.did(dve.tensor_tensor(t_odd, parts[2], parts[3], ALU.add))
                    dve.wait_ge(qk_root, b + 1)
                    own.did(dve.reciprocal(rs[:], rs[:]))
                    own.settle()
                    own.did(dve.tensor_tensor(newton[:], rs[:], rs[:], ALU.mult))
                    own.settle()
                    own.did(dve.scalar_tensor_tensor(newton[:], newton[:], -0.5, ssq[:], ALU.mult, ALU.mult))
                    own.settle()
                    own.did(dve.scalar_tensor_tensor(rs[:], newton[:], 1.5, rs[:], ALU.add, ALU.mult))
                    own.settle()
                    by_head = turned[:].rearrange("p t (h d) -> p (t h) d", d=HD)
                    own.did(dve.tensor_tensor(by_head, by_head, rs[:].unsqueeze(2).to_broadcast([P, NB * heads, HD]),
                                              ALU.mult))
                    assert own.n == CHAIN_TURNED, own.n
                    own.settle()
                    dve.wait_ge(k_hi, b * 2 + 2)
                    own.did(dve.tensor_tensor(slots(k_slots)[:, :, :, 2, :], k_of,
                                              slots(k_slots)[:, :, :, 0, :].bitcast(F32), ALU.subtract))
                    assert own.n == CHAIN_KEYS, own.n
                    for j in range(GQ):
                        dve.wait_ge(q_hi, b * (2 * GQ) + 2 * j + 2)
                        own.did(dve.tensor_tensor(slots(q_slots[j])[:, :, :, 1, :], q_of(j),
                                                  slots(q_slots[j])[:, :, :, 0, :].bitcast(F32), ALU.subtract))
                    dve.wait_ge(kT_kept_act, b * 2 + 2)
                    for h in range(2, KV):
                        rows = slice(h * SLOT, (h + 1) * SLOT)
                        dve.tensor_copy(kT[h][rows, :], x_ps[rows, :]).then_inc(kT_kept_dve, 1)
                    for j in (1, 3):
                        dve.wait_ge(qT_done, b * GQ + j + 1)
                        dve.tensor_copy(qT[j][:], x_ps[:]).then_inc(qT_kept[1], 1)
                    for h in range(KV):
                        dve.wait_ge(pv_done, b * (KV * NB) + h * NB + NB)
                        dve.tensor_copy(outT[h % 2][:], o_ps[:]).then_inc(o_kept, 1)
                        dve.wait_ge(back_done, b * KV + h + 1)
                        back = x_ps[:].rearrange("p (t j s) -> p t j s", t=NB, j=GQ)
                        own.did(dve.reciprocal(inv[:], back[:, :, :, HD]))
                        own.settle()
                        for j in range(GQ):
                            head = (h * GQ + j) * HD
                            ins = dve.tensor_tensor(att[:, :, head:head + HD], back[:, :, j, 0:HD],
                                                    inv[:, :, j:j + 1].to_broadcast([P, NB, HD]), ALU.mult)
                            if j < GQ - 1:
                                own.did(ins)
                        ins.then_inc(att_kept, 1)
                    dve.wait_ge(out_done, b + 1)
                    own.did(dve.tensor_tensor(hidden, hidden, o_ps[:].rearrange("p (t n) -> p t n", t=NB), ALU.add))
                    own.settle()
                    assert own.n == CHAIN, own.n


def layer1_attention(nc, g):
    with ExitStack() as ctx:
        g.hidden = ctx.enter_context(nc.sbuf_tensor("hidden", [P, NBLK, D], F32))
        g.norm1 = NormTiles(ctx, nc, "norm1")
        attention_layer1(nc, g, local=False)
        attention_layer1(nc, g, local=True)
        with nc.Block() as block:
            @block.gpsimd
            def _(pool):
                with pool.Fori(0, BATCH) as b:
                    inverse_root(pool, g.norm1, g.minus_half[:, 0:NB], b + BATCH)

            @block.vector
            def _(dve):
                with dve.Fori(0, BATCH) as b:
                    chain = Chain(dve, g.norm1.chain, BATCH * NORM_STEPS + b * (NORM_STEPS + 1))
                    y_of = lambda blk: g.hidden[:, b * NB + blk, :]
                    layernorm(dve, chain, y_of, y_of, g.norm1, b + BATCH)
                    batch = g.x[:, ds(b * NB, NB), :]
                    chain.did(dve.tensor_tensor(batch, batch, g.hidden[:, ds(b * NB, NB), :], ALU.add))
                    chain.settle()


SE, SS = 8, 64
SLOTS = SE * SS
SB = SLOTS // P
S_HID = 512
S_HB = S_HID // P
COLS = BATCH * SS
UNITS_A, UNITS_B = SB, NB // 2


def soft_mixture(nc, g, out):
    with ExitStack() as ctx:
        def sb(name, shape, dt=F32):
            return ctx.enter_context(nc.sbuf_tensor("s_" + name, shape, dt))

        def sem(name):
            return ctx.enter_context(nc.semaphore("s_" + name))

        w1 = sb("w1", [P, SE, S_HID])
        w2 = sb("w2", [P, SE, S_HB, D])
        b1 = sb("b1", [P, SE, S_HB])
        b2 = sb("b2", [P, SB, D])
        gamma, slot_gamma = sb("gamma", [P, D]), sb("slot_gamma", [P, D])
        slot_in = sb("slot_in", [P, SB, D])
        snT = [sb(f"snT{i}", [P, SLOTS], F32R) for i in range(2)]
        combine = sb("combine", [P, SB, NBLK * P])
        inv_c = sb("inv_c", [P, NBLK])
        slotsT = sb("slotsT", [P, SE, BATCH, SS])
        norm = NormTiles(ctx, nc, "s_norm")
        ss, rs = sb("ss", [P, NB]), sb("rs", [P, NB])

        loaded, chain, ss_ready, rs_ready = sem("loaded"), sem("chain"), sem("ss_ready"), sem("rs_ready")
        turned, hi_done = sem("turned"), sem("hi_done")
        root = float(D) ** 0.5

        with nc.psum_tensor("s_first_ps", [P, SLOTS], F32) as first_ps, nc.sbuf_tensor("s_sq", [P, SB, D], F32) as sq:
            with nc.Block() as block:
                @block.sync
                def _(sp):
                    sp.dma_start(slot_in[:], g.inputs["L1_ffn_slot_embeds"].rearrange("(q e) s n -> (e s) q n", e=2)
                                 ).then_inc(loaded, 16)
                    sp.dma_start(slot_gamma[:], g.inputs["L1_ffn_slot_norm_gamma"].partition_broadcast(P)).then_inc(loaded, 16)
                    sp.dma_start(gamma[:], g.inputs["L1_ffn_norm_gamma"].partition_broadcast(P)).then_inc(loaded, 16)
                    with nc.allow_non_contiguous_dma(reason="biases, one value per partition"):
                        sp.dma_start(b1[:].rearrange("p e h -> p (e h)"),
                                     g.inputs["L1_ffn_b1"].rearrange("e (h p) -> p (e h)", p=P)).then_inc(loaded, 16)
                    by_pair = g.inputs["L1_ffn_b2"].rearrange("(q e) n -> e q n", e=2)
                    for e in range(2):
                        sp.dma_start(b2[e * SS:(e + 1) * SS], by_pair[e].partition_broadcast(SS)).then_inc(loaded, 16)
                    sp.dma_start(w1[:], g.inputs["L1_ffn_w1"].rearrange("e p n -> p e n")).then_inc(loaded, 16)
                    for h in range(S_HB):
                        sp.dma_start(w2[:, :, h, :], g.inputs["L1_ffn_w2"][:, h * P:(h + 1) * P, :].rearrange("e p n -> p e n")
                                     ).then_inc(loaded, 16)

                @block.gpsimd
                def _(pool):
                    pool.wait_ge(ss_ready, 1)
                    pool.tensor_tensor(rs[:, 0:SB], ss[:, 0:SB], g.minus_half[:, 0:SB], ALU.pow).then_inc(rs_ready, 1)

                @block.tensor
                def _(pe):
                    pe.wait_ge(chain, 4 + SB)
                    for q in range(SB):
                        last = pe.transpose(first_ps[:, q * P:(q + 1) * P], sq[:, q, :], g.ident[:])
                    last.then_inc(turned, 1)

                @block.scalar
                def _(act):
                    act.wait_ge(turned, 1)
                    act.activation(snT[0][:], first_ps[:], ACT.Copy).then_inc(hi_done, 1)

                @block.vector
                def _(dve):
                    own = Chain(dve, chain)
                    dve.wait_ge(loaded, 11 * 16)
                    own.did(dve.tensor_scalar(gamma[:], gamma[:], root, None, ALU.mult))
                    own.did(dve.tensor_scalar(slot_gamma[:], slot_gamma[:], root, None, ALU.mult))
                    own.did(dve.tensor_tensor(sq[:], slot_in[:], slot_in[:], ALU.mult))
                    own.settle()
                    own.did(dve.tensor_reduce(ss[:, 0:SB], sq[:], AX.X, ALU.add))
                    own.settle()
                    dve.tensor_scalar(ss[:, 0:SB], ss[:, 0:SB], 1e-24, None, ALU.max).then_inc(ss_ready, 1)
                    dve.wait_ge(rs_ready, 1)
                    for q in range(SB):
                        own.did(dve.scalar_tensor_tensor(sq[:, q, :], slot_in[:, q, :], rs[:, q:q + 1], slot_gamma[:],
                                                         ALU.mult, ALU.mult))
                    assert own.n == 4 + SB
                    dve.wait_ge(hi_done, 1)
                    dve.tensor_tensor(snT[1][:], first_ps[:], snT[0][:].bitcast(F32), ALU.subtract)

        with ExitStack() as lctx:
            def lsb(name, shape, dt=F32):
                return lctx.enter_context(nc.sbuf_tensor("s_" + name, shape, dt))

            hidden, xn = lsb("hidden", [P, NB, D]), lsb("xn", [P, NB, D])
            xT = [lsb(f"xT{i}", [P, SEQ], F32R) for i in range(2)]
            minus_max = lsb("minus_max", [P, UNITS_A + 2 * UNITS_B])
            sums, inv_d = lsb("sums", [P, UNITS_A + 2 * UNITS_B]), lsb("inv_d", [P, UNITS_A])
            exps = [lsb(f"exps{i}", [P, SEQ]) for i in range(2)]
            dispatch = lsb("dispatch", [P, NB, SLOTS])
            logits = [lctx.enter_context(nc.psum_tensor(f"s_logits{i}", [P, SEQ], F32)) for i in range(2)]
            tr = [lctx.enter_context(nc.psum_tensor(f"s_tr{i}", [P, SEQ], F32)) for i in range(2)]
            xT_hi_done, xT_lo_done = sem("xT_hi_done"), sem("xT_lo_done")
            lg_done, max_done, exp_done, scaled = sem("lg_done"), sem("max_done"), sem("exp_done"), sem("scaled")
            tr_done, slots_done = sem("tr_done"), sem("slots_done")
            read_act, read_dve = sem("read_act"), sem("read_dve")

            UNITS = UNITS_A + UNITS_B
            CHAIN_XN = NORM_STEPS + 2 + NB
            CHAIN = CHAIN_XN + UNITS_A + UNITS_B
            READS_ACT, READS_DVE = UNITS + 1, UNITS
            EXPS = UNITS_A + 2 * UNITS_B
            exps_by = lambda u: u + 1 if u < UNITS_A else UNITS_A + 2 * (u - UNITS_A + 1)

            with nc.Block() as block:
                @block.gpsimd
                def _(pool):
                    with pool.Fori(0, BATCH) as b:
                        inverse_root(pool, norm, g.minus_half[:, 0:NB], b)
                        pool.wait_ge(ss_ready, b + 2)
                        pool.tensor_tensor(rs[:], ss[:], g.minus_half[:, 0:NB], ALU.pow).then_inc(rs_ready, 1)

                @block.tensor
                def _(pe):
                    with pe.Fori(0, BATCH) as b:
                        def tile_read(k):
                            pe.wait_ge(read_dve, b * READS_DVE + max(k - 1, 0))
                            pe.wait_ge(read_act, b * READS_ACT + max(k - 1, 0))

                        pe.wait_ge(norm.chain, b * CHAIN + CHAIN_XN)
                        tile_read(0)
                        for t in range(NB):
                            last = pe.transpose(tr[1][:, t * P:(t + 1) * P], xn[:, t, :], g.ident[:])
                        last.then_inc(tr_done, 1)
                        pe.wait_ge(xT_lo_done, b + 1)

                        def score(u):
                            if u >= 2:
                                pe.wait_ge(exp_done, b * EXPS + exps_by(u - 2))
                            for c in range(2):
                                if u < UNITS_A:
                                    a = [snT[i][:, u * P:(u + 1) * P] for i in range(2)]
                                    r = [xT[i][:, c * HALF:(c + 1) * HALF] for i in range(2)]
                                else:
                                    blk = (u - UNITS_A) * 2 + c
                                    a = [xT[i][:, blk * P:(blk + 1) * P] for i in range(2)]
                                    r = [snT[i][:] for i in range(2)]
                                for n, (l, m) in enumerate(split_passes(a, r)):
                                    last = pe.matmul(logits[u % 2][:, c * HALF:(c + 1) * HALF], l, m,
                                                     start=n == 0, stop=n == 2)
                            last.then_inc(lg_done, 1)

                        def turn(u):
                            if u < UNITS_A:
                                pe.wait_ge(scaled, b * UNITS_A + u + 1)
                            else:
                                pe.wait_ge(exp_done, b * EXPS + exps_by(u))
                            tile_read(u)
                            for t in range(NB):
                                last = pe.transpose(tr[u % 2][:, t * P:(t + 1) * P], exps[u % 2][:, t * P:(t + 1) * P],
                                                    g.ident[:])
                            last.then_inc(tr_done, 1)

                        score(0)
                        for u in range(UNITS):
                            if u + 1 < UNITS:
                                score(u + 1)
                            turn(u)
                        tile_read(UNITS)
                        for t in range(NB):
                            last = pe.matmul(tr[0][:, 0:SLOTS], xn[:, t, :], dispatch[:, t, :], start=t == 0,
                                             stop=t == NB - 1)
                        last.then_inc(slots_done, 1)

                def place(u, c):
                    src = tr[u % 2][:, c * HALF:(c + 1) * HALF].rearrange("p (t n) -> p t n", t=4)
                    if u < UNITS_A:
                        return (lambda b: dispatch[:, 4 * c:4 * c + 4, u * P:(u + 1) * P]), src
                    blk = (u - UNITS_A) * 2 + c
                    return (lambda b: combine[:, :, ds(b * SEQ + blk * P, P)]), src

                @block.scalar
                def _(act):
                    with act.Fori(0, BATCH) as b:
                        act.wait_ge(tr_done, b * (UNITS + 1) + 1)
                        act.activation(xT[0][:], tr[1][:], ACT.Copy).then_inc(xT_hi_done, 1)

                        def move(u):
                            to, src = place(u, 0)
                            act.wait_ge(tr_done, b * (UNITS + 1) + u + 2)
                            act.activation(to(b), src, ACT.Copy).then_inc(read_act, 1)

                        for u in range(UNITS):
                            act.wait_ge(max_done, b * UNITS + u + 1)
                            if u >= 2:
                                act.wait_ge(tr_done, b * (UNITS + 1) + u)
                            for i in range(1 if u < UNITS_A else 2):
                                w = SEQ if u < UNITS_A else HALF
                                n = exps_by(u) - (1 if u < UNITS_A else 2) + i
                                act.activation(exps[u % 2][:, i * w:(i + 1) * w], logits[u % 2][:, i * w:(i + 1) * w],
                                               ACT.Exp, bias=minus_max[:, n:n + 1], accum_out=sums[:, n:n + 1]
                                               ).then_inc(exp_done, 1)
                            if u:
                                move(u - 1)
                        move(UNITS - 1)
                        act.wait_ge(slots_done, b + 1)
                        act.activation(slotsT[:, :, b, :], tr[0][:, 0:SLOTS].rearrange("p (e s) -> p e s", e=SE),
                                       ACT.Copy).then_inc(read_act, 1)

                @block.vector
                def _(dve):
                    with dve.Fori(0, BATCH) as b:
                        own = Chain(dve, norm.chain, b * CHAIN)
                        layernorm(dve, own, lambda t: g.x[:, b * NB + t, :], lambda t: hidden[:, t, :], norm, b)
                        dve.wait_ge(slots_done, b)
                        own.did(dve.tensor_tensor(xn[:], hidden[:], hidden[:], ALU.mult))
                        own.settle()
                        own.did(dve.tensor_reduce(ss[:], xn[:], AX.X, ALU.add))
                        own.settle()
                        dve.tensor_scalar(ss[:], ss[:], 1e-24, None, ALU.max).then_inc(ss_ready, 1)
                        dve.wait_ge(rs_ready, b + 2)
                        for t in range(NB):
                            own.did(dve.scalar_tensor_tensor(xn[:, t, :], hidden[:, t, :], rs[:, t:t + 1], gamma[:],
                                                             ALU.mult, ALU.mult))
                        assert own.n == CHAIN_XN
                        dve.wait_ge(xT_hi_done, b + 1)
                        dve.tensor_tensor(xT[1][:], tr[1][:], xT[0][:].bitcast(F32), ALU.subtract
                                          ).then_inc(xT_lo_done, 1)

                        def move(u):
                            to, src = place(u, 1)
                            dve.wait_ge(tr_done, b * (UNITS + 1) + u + 2)
                            dve.tensor_copy(to(b), src).then_inc(read_dve, 1)

                        def largest(u):
                            dve.wait_ge(lg_done, b * UNITS + u + 1)
                            if u < UNITS_A:
                                ins = dve.tensor_reduce(minus_max[:, u:u + 1], logits[u % 2][:], AX.X, ALU.max, negate=True)
                            else:
                                n = exps_by(u) - 2
                                ins = dve.tensor_reduce(minus_max[:, n:n + 2], logits[u % 2][:].rearrange(
                                    "p (i n) -> p i n", i=2), AX.X, ALU.max, negate=True)
                            ins.then_inc(max_done, 1)

                        largest(0)
                        for u in range(UNITS):
                            if u + 1 < UNITS:
                                largest(u + 1)
                            dve.wait_ge(exp_done, b * EXPS + exps_by(u))
                            if u < UNITS_A:
                                own.did(dve.reciprocal(inv_d[:, u:u + 1], sums[:, u:u + 1]))
                                own.settle()
                                dve.tensor_scalar(exps[u % 2][:], exps[u % 2][:], inv_d[:, u:u + 1], None, ALU.mult
                                                  ).then_inc(scaled, 1)
                            else:
                                n = exps_by(u) - 2
                                own.did(dve.reciprocal(inv_c[:, ds(b * NB + 2 * (u - UNITS_A), 2)], sums[:, n:n + 2]))
                            move(u)
                        assert own.n == CHAIN, own.n

        with ExitStack() as ectx:
            def esb(name, shape, dt=F32):
                return ectx.enter_context(nc.sbuf_tensor("s_" + name, shape, dt))

            w1_e = [esb(f"w1_e{i}", [P, S_HID]) for i in range(2)]
            w2_e = [esb(f"w2_e{i}", [P, S_HB, D]) for i in range(2)]
            hT = [esb(f"hT{i}", [P, S_HB, COLS]) for i in range(2)]
            slot_out = esb("slot_out", [P, SB, BATCH, D])
            eo_b = [esb(f"eo_b{i}", [P, SB, D]) for i in range(2)]
            mixedT = esb("mixedT", [P, SEQ])
            mixed = esb("mixed", [P, NB, D])
            up = [ectx.enter_context(nc.psum_tensor(f"s_up{i}", [P, S_HB, COLS], F32)) for i in range(2)]
            down = ectx.enter_context(nc.psum_tensor("s_down", [P, BATCH * D], F32))
            w1_ready, w2_ready, up_done, gelu_done = sem("w1_ready"), sem("w2_ready"), sem("up_done"), sem("gelu_done")
            down_done, down_kept = sem("down_done"), sem("down_kept")

            with nc.Block() as block:
                @block.tensor
                def _(pe):
                    def raise_(par, e):
                        pe.wait_ge(w1_ready, e + 1)
                        for h in range(S_HB):
                            last = pe.matmul(up[par][:, h, :], w1_e[par][:, h * P:(h + 1) * P], slotsT[:, e],
                                             start=True, stop=True)
                            if h % 2:
                                last.then_inc(up_done, 1)

                    def lower(par, e, q):
                        pe.wait_ge(w2_ready, e + 1)
                        pe.wait_ge(gelu_done, (e + 1) * S_HB)
                        if par == 0:
                            pe.wait_ge(down_kept, q)
                        for b in range(BATCH):
                            for h in range(S_HB):
                                last = pe.matmul(down[par * SS:(par + 1) * SS, b * D:(b + 1) * D],
                                                 hT[par][:, h, b * SS:(b + 1) * SS], w2_e[par][:, h, :],
                                                 start=h == 0 and b == 0, stop=h == S_HB - 1, skip_group_check=True)
                        last.then_inc(down_done, 1)

                    raise_(0, 0)
                    with pe.Fori(0, SB - 1) as q:
                        for par in range(2):
                            raise_(1 - par, q * 2 + par + 1)
                            lower(par, q * 2 + par, q)
                    raise_(1, SE - 1)
                    for par in range(2):
                        lower(par, SE - 2 + par, SB - 1)

                @block.scalar
                def _(act):
                    with act.Fori(0, SB) as q:
                        for par in range(2):
                            e = q * 2 + par
                            for h in range(S_HB):
                                if h % 2 == 0:
                                    act.wait_ge(up_done, e * (S_HB // 2) + h // 2 + 1)
                                act.activation(hT[par][:, h, :], up[par][:, h, :], ACT.Gelu,
                                               bias=b1[:, e, h:h + 1]
                                               ).then_inc(gelu_done, 1)

                @block.vector
                def _(dve):
                    def take_up(par, e):
                        dve.tensor_copy(w1_e[par][:], w1[:, e, :]).then_inc(w1_ready, 1)

                    def take_down(par, e):
                        dve.tensor_copy(w2_e[par][:], w2[:, e]).then_inc(w2_ready, 1)

                    def keep(q):
                        dve.wait_ge(down_done, q * 2 + 2)
                        dve.tensor_tensor(slot_out[:, q], down[:].rearrange("p (b n) -> p b n", b=BATCH),
                                          b2[:, q, :].unsqueeze(1).to_broadcast([P, BATCH, D]), ALU.add
                                          ).then_inc(down_kept, 1)

                    for par in range(2):
                        take_up(par, par)
                        take_down(par, par)
                    with dve.Fori(0, SB - 1) as q:
                        for par in range(2):
                            dve.wait_ge(up_done, (q * 2 + par + 1) * (S_HB // 2))
                            take_up(par, q * 2 + par + 2)
                            dve.wait_ge(down_done, q * 2 + par + 1)
                            take_down(par, q * 2 + par + 2)
                        keep(q)
                    keep(SB - 1)

            eo_ready, mixT_done, mixT_kept, mix_done, mix_kept, x_done, stored = (sem(n) for n in (
                "eo_ready", "mixT_done", "mixT_kept", "mix_done", "mix_kept", "x_done", "stored"))
            mixT_ps, mix_ps = up[0], up[1]
            flat = lambda t: t[:].rearrange("p h n -> p (h n)")
            base = BATCH * CHAIN
            with nc.Block() as block:
                @block.sync
                def _(sp):
                    for b in range(BATCH):
                        sp.wait_ge(x_done, b + 1)
                        sp.dma_start(out[b].rearrange("(t p) n -> p t n", p=P), g.x[:, b * NB:(b + 1) * NB, :]
                                     ).then_inc(stored, 16)
                    sp.wait_ge(stored, BATCH * 16)

                @block.gpsimd
                def _(pool):
                    with pool.Fori(0, BATCH) as b:
                        inverse_root(pool, norm, g.minus_half[:, 0:NB], b + BATCH)

                @block.tensor
                def _(pe):
                    with pe.Fori(0, BATCH // 2) as pair:
                        for par in range(2):
                            b = pair * 2 + par
                            pe.wait_ge(eo_ready, b + 1)
                            for c in range(2):
                                for q in range(SB):
                                    last = pe.matmul(flat(mixT_ps)[:, c * HALF:(c + 1) * HALF], eo_b[par][:, q, :],
                                                     combine[:, q, ds(b * SEQ + c * HALF, HALF)], start=q == 0,
                                                     stop=q == SB - 1)
                            last.then_inc(mixT_done, 1)
                            pe.wait_ge(mixT_kept, b + 1)
                            pe.wait_ge(mix_kept, b)
                            for t in range(NB):
                                last = pe.transpose(flat(mix_ps)[:, t * P:(t + 1) * P], mixedT[:, t * P:(t + 1) * P],
                                                    g.ident[:])
                            last.then_inc(mix_done, 1)

                @block.scalar
                def _(act):
                    def take(par, b):
                        act.activation(eo_b[par][:], slot_out[:, :, b, :], ACT.Copy).then_inc(eo_ready, 1)

                    with act.Fori(0, BATCH // 2) as pair:
                        for par in range(2):
                            take(par, pair * 2 + par)
                        for par in range(2):
                            b = pair * 2 + par
                            act.wait_ge(mixT_done, b + 1)
                            act.activation(mixedT[:], flat(mixT_ps), ACT.Copy).then_inc(mixT_kept, 1)

                @block.vector
                def _(dve):
                    with dve.Fori(0, BATCH) as b:
                        own = Chain(dve, norm.chain, b * NORM_STEPS + base)
                        dve.wait_ge(x_done, b)
                        dve.wait_ge(mix_done, b + 1)
                        dve.tensor_tensor(mixed[:], flat(mix_ps).rearrange("p (t n) -> p t n", t=NB),
                                          inv_c[:, ds(b * NB, NB)].unsqueeze(2).to_broadcast([P, NB, D]),
                                          ALU.mult).then_inc(mix_kept, 1)
                        dve.wait_ge(mix_kept, b + 1)
                        layernorm(dve, own, lambda t: mixed[:, t, :], lambda t: mixed[:, t, :], norm, b + BATCH)
                        assert own.n == NORM_STEPS
                        batch = g.x[:, ds(b * NB, NB), :]
                        dve.tensor_tensor(batch, batch, mixed[:], ALU.add).then_inc(x_done, 1)


def constants():
    i = np.arange(P)
    k, q = i[:, None], np.arange(LOCAL_W)[None, :]

    def rotation(base):
        inv_freq = np.float32(1.0) / np.float32(base) ** (np.arange(0, HD, 2, dtype=np.float32) / np.float32(HD))
        angles = np.arange(SEQ, dtype=np.float32)[:, None] * inv_freq[None, :].astype(np.float32)
        return np.stack([np.cos(angles), np.sin(angles)]).astype(np.float32)

    return {
        "c_ident": np.eye(P, dtype=np.float32),
        "c_iota": np.arange(E_ROUTED, dtype=np.float32),
        "c_mask_kq": np.where(i[:, None] > i[None, :], -1e30, 0.0).astype(np.float32),
        "c_mask_window": np.where((q - k >= 0) & (q - k < WINDOW), 0.0, -1e30).astype(np.float32),
        "c_rope_g": rotation(1e6),
        "c_rope_l": rotation(1e4),
        "c_mask_qk": np.where(i[None, :] > i[:, None], -1e30, 0.0).astype(np.float32),
    }


class Shared:
    pass


def build(nc, aps, out):
    g = Shared()
    g.inputs = aps
    with ExitStack() as ctx:
        def sb(name, shape, dt=F32):
            return ctx.enter_context(nc.sbuf_tensor(name, shape, dt))

        g.x = sb("x", [P, NBLK, D])
        g.ident = sb("ident", [P, P])
        g.ident_bf = sb("ident_bf", [P, P], BF16)
        g.mask_qk = sb("mask_qk", [P, P], BF16)
        g.minus_half = sb("minus_half", [P, 256])
        g.mask_kq = sb("mask_kq", [P, P], BF16)
        g.mask_window = sb("mask_window", [P, LOCAL_W], BF16)
        staged = [sb(f"staged{i}", [P, LOCAL_W]) for i in range(3)]
        x_loaded = ctx.enter_context(nc.semaphore("x_loaded"))
        const_loaded = ctx.enter_context(nc.semaphore("const_loaded"))
        masks = ((g.inputs["c_mask_qk"], P), (g.inputs["c_mask_kq"], P), (g.inputs["c_mask_window"], LOCAL_W))
        with nc.Block() as block:
            @block.sync
            def _(sp):
                sp.dma_start(g.ident[:], g.inputs["c_ident"]).then_inc(const_loaded, 16)
                for n, (src, width) in enumerate(masks):
                    sp.dma_start(staged[n][:, 0:width], src).then_inc(const_loaded, 16)
                for b in range(BATCH):
                    sp.dma_start(g.x[:, b * NB:(b + 1) * NB, :],
                                 g.inputs["L0_attn_x"][b].rearrange("(t p) n -> p t n", p=P)).then_inc(x_loaded, 16)

            @block.gpsimd
            def _(pool):
                pool.memset(g.minus_half[:], -0.5)

            @block.vector
            def _(dve):
                dve.wait_ge(const_loaded, 4 * 16)
                dve.tensor_copy(g.ident_bf[:], g.ident[:])
                for n, (out, (_, width)) in enumerate(zip((g.mask_qk, g.mask_kq, g.mask_window), masks)):
                    dve.tensor_copy(out[:], staged[n][:, 0:width])
                dve.wait_ge(x_loaded, 64)
        attention_layer0(nc, g)
        mixture_layer0(nc, g)
        layer1_attention(nc, g)
        soft_mixture(nc, g, out)



def kernel(**inputs):
    import concourse.bacc as _bacc
    from concourse.bass_utils import run_bass_kernel_spmd as _run

    nc = _bacc.Bacc("TRN2", target_bir_lowering=False, num_devices=1)
    arrays, aps = {}, {}
    for name, a in (inputs | constants()).items():
        a = np.ascontiguousarray(a)
        arrays[f"in_{name}"] = a
        aps[name] = nc.dram_tensor(f"in_{name}", a.shape, mybir.dt.from_np(a.dtype), kind="ExternalInput").ap()
    out = nc.dram_tensor("out_x", (BATCH, SEQ, D), F32, kind="ExternalOutput").ap()
    build(nc, aps, out)
    return _run(nc, [arrays], core_ids=[0]).results[0]["out_x"]
```

```python
import numpy as np
import concourse.bass as bass
from concourse import mybir
from contextlib import ExitStack

F32 = mybir.dt.float32
F32R = mybir.dt.float32r
BF16 = mybir.dt.bfloat16
U32 = mybir.dt.uint32
ALU = mybir.AluOpType
ACT = mybir.ActivationFunctionType
AX = mybir.AxisListType
ds = bass.ds

P = 128
BATCH, SEQ, D = 4, 1024, 128
NB = SEQ // P
NBLK = BATCH * NB
HALF = 512
LN_EPS = 1e-5


class Chain:

    def __init__(self, eng, sem, base=0):
        self.eng, self.sem, self.base, self.n = eng, sem, base, 0

    def did(self, ins):
        ins.then_inc(self.sem, 1)
        self.n += 1

    def settle(self):
        self.eng.wait_ge(self.sem, self.base + self.n)


def split_passes(hi_lo_a, hi_lo_b):
    (ah, al), (bh, bl) = hi_lo_a, hi_lo_b
    return [(ah, bh), (ah, bl), (al, bh)]




NORM_STEPS = 2 * NB + 5


def layernorm_parts(dve, chain, x_of, out_of, t, count):
    def statistics(blks):
        for blk in blks:
            chain.did(dve.bn_stats(t.stats[:, blk, :], x_of(blk)))

    def variance():
        chain.settle()
        mean_e, sq_e, mean_o, sq_o = (t.stats[:, :, c] for c in (1, 2, 4, 5))
        chain.did(dve.scalar_tensor_tensor(t.square[:], sq_e, D * LN_EPS, sq_o, ALU.add, ALU.add))
        chain.did(dve.tensor_tensor(t.gap[:], mean_e, mean_o, ALU.subtract))
        chain.did(dve.tensor_tensor(t.twice[:], mean_e, mean_o, ALU.add))
        chain.settle()
        chain.did(dve.scalar_tensor_tensor(t.gap[:], t.gap[:], 0.25, t.gap[:], ALU.mult, ALU.mult))
        chain.did(dve.tensor_scalar(t.mean[:], t.twice[:], 0.5, None, ALU.mult))
        chain.settle()
        dve.scalar_tensor_tensor(t.var[:], t.square[:], 1.0 / D, t.gap[:], ALU.mult, ALU.add).then_inc(t.var_ready, 1)

    def normalize(blks):
        dve.wait_ge(t.rstd_ready, count + 1)
        for blk in blks:
            chain.did(dve.tensor_scalar(out_of(blk), x_of(blk), t.mean[:, blk:blk + 1], t.rstd[:, blk:blk + 1],
                                        ALU.subtract, ALU.mult))

    quarters = [range(blk, blk + 2) for blk in range(0, NB, 2)]
    return [*(lambda q=q: statistics(q) for q in quarters), variance,
            *(lambda q=q: normalize(q) for q in (range(0, 4), range(4, NB))), chain.settle]


def layernorm(*args):
    for part in layernorm_parts(*args):
        part()


def inverse_root(pool, t, minus_half, count):
    pool.wait_ge(t.var_ready, count + 1)
    pool.tensor_tensor(t.rstd[:], t.var[:], minus_half, ALU.pow).then_inc(t.rstd_ready, 1)


class NormTiles:

    def __init__(self, ctx, nc, name):
        sb = lambda n, shape: ctx.enter_context(nc.sbuf_tensor(f"{name}_{n}", shape, F32))
        sem = lambda n: ctx.enter_context(nc.semaphore(f"{name}_{n}"))
        self.stats = sb("stats", [P, NB, 6])
        self.square, self.gap, self.twice, self.mean, self.var, self.rstd = (
            sb(n, [P, NB]) for n in ("square", "gap", "twice", "mean", "var", "rstd"))
        self.var_ready, self.rstd_ready, self.chain = sem("var_ready"), sem("rstd_ready"), sem("chain")


A_HEADS, A_HD = 16, 64
PAIRS = A_HEADS // 2
QK_GROUPS, V_GROUPS = 8, 2
GROUPS = QK_GROUPS + V_GROUPS
KEYS_SCALE = 1.0 / A_HD
BANK_TURNS = sum((i + 4) // 4 for i in range(NB))
GROUPS_OF_STEP = [(0, 1)] + [(k + 1,) for k in range(1, NB - 1)] + [(QK_GROUPS, QK_GROUPS + 1)]


def first_pair(run, b, extra=()):
    run(0, 0, 1, True, True, b, extra)


def other_pairs(eng, run, b, extra=()):
    with eng.Fori(0, PAIRS // 2 - 1) as q:
        for par, pair in ((1, q * 2 + 1), (0, q * 2 + 2)):
            run(par, pair, q + 2, False, True, b, ())
    run(1, PAIRS - 1, 0, False, False, b, extra)


def attention_layer0(nc, g):
    with ExitStack() as ctx:
        def sb(name, shape, dt=F32):
            return ctx.enter_context(nc.sbuf_tensor("a_" + name, shape, dt))

        def pb(name, shape):
            return ctx.enter_context(nc.psum_tensor("a_" + name, shape, F32))

        def sem(name):
            sems.append(nc.alloc_semaphore(name="a_" + name))
            return sems[-1]

        sems = []

        w_hl = sb("w_hl", [P, 6, D * 8], F32R)
        w_u = sb("w_u", [P, PAIRS, D])
        b_u = sb("b_u", [P, D])
        w_pair = [sb(f"w_pair{i}", [P, 4, 2, P], F32R) for i in range(2)]
        wv_pair = [sb(f"wv_pair{i}", [P, 2, P], F32R) for i in range(2)]
        x_norm = sb("x_norm", [P, NB, D])
        y = sb("y", [P, NB, D])
        xT_hi = sb("xT_hi", [P, SEQ], F32R)
        xT_lo = sb("xT_lo", [P, SEQ], F32R)
        q_st = [[sb(f"q_st{i}{h}", [P, SEQ], F32R) for h in range(2)] for i in range(2)]
        k_hh = [[sb(f"k_hh{i}{h}", [P, SEQ], F32R) for h in range(2)] for i in range(2)]
        k_ll = [[sb(f"k_ll{i}{h}", [P, SEQ], F32R) for h in range(2)] for i in range(2)]
        v_sb = [sb(f"v{i}", [P, NB, P]) for i in range(2)]
        probs = [sb(f"probs{i}", [P, 2, SEQ]) for i in range(2)]
        probsT = [sb(f"probsT{i}", [P, 2, SEQ]) for i in range(2)]
        outT = sb("outT", [P, PAIRS, SEQ])
        r_bc = [sb(f"r_bc{i}", [P, P]) for i in range(2)]
        neg_max, row_sum, row_inv = (sb(n, [P, NB, 2]) for n in ("neg_max", "row_sum", "row_inv"))
        norm = NormTiles(ctx, nc, "a_norm")

        scores = [pb(f"scores{h}", [P, SEQ]) for h in range(2)]
        tr = [pb(f"tr{i}", [P, HALF]) for i in range(2)]
        o_ps = pb("o_ps", [P, HALF])
        p_ps = pb("p_ps", [P, HALF])
        raw = outT

        loaded, split_hi, split_lo = sem("loaded"), sem("split_hi"), sem("split_lo")
        pair_loaded = [sem(f"pair_loaded{i}") for i in range(2)]
        xT_done, xT_hi_done, xT_lo_done = sem("xT_done"), sem("xT_hi_done"), sem("xT_lo_done")
        proj_done, proj_hi, proj_lo = sem("proj_done"), sem("proj_hi"), sem("proj_lo")
        scored, max_ready, exp_done = sem("scored"), sem("max_ready"), sem("exp_done")
        tr_done, tr_out = sem("tr_done"), [sem("tr_out_act"), sem("tr_out_dve")]
        inv_ready, inv_bc, inv_sb = sem("inv_ready"), sem("inv_bc"), sem("inv_sb")
        pv_done, out_kept = sem("pv_done"), sem("out_kept")
        y_done, y_used = sem("y_done"), sem("y_used")

        with nc.Block() as block:
            @block.sync
            def _(sp):
                for n, w in enumerate((g.inputs["L0_attn_w_q"], g.inputs["L0_attn_w_k"], g.inputs["L0_attn_w_v"])):
                    sp.dma_start(raw[:, n, :], w).then_inc(loaded, 16)
                sp.dma_start(w_u[:], g.inputs["L0_attn_w_u"].rearrange("(t p) n -> p t n", p=P)).then_inc(loaded, 16)
                sp.dma_start(b_u[:], g.inputs["L0_attn_b_u"].partition_broadcast(P)).then_inc(loaded, 16)

            @block.scalar
            def _(act):
                act.wait_ge(loaded, 5 * 16)
                for n in range(3):
                    act.activation(w_hl[:, 2 * n, :], raw[:, n, :], ACT.Copy).then_inc(split_hi, 1)

            @block.vector
            def _(dve):
                for n in range(3):
                    dve.wait_ge(split_hi, n + 1)
                    dve.tensor_tensor(w_hl[:, 2 * n + 1, :], raw[:, n, :],
                                      w_hl[:, 2 * n, :].bitcast(F32), ALU.subtract).then_inc(split_lo, 1)
                dve.wait_ge(split_lo, 3)

        CHAIN = 2 * NORM_STEPS + 1

        LAST_TURN = BANK_TURNS - 1

        with nc.Block() as block:
            @block.sync
            def _(sp):
                def fetch(par, pair, b, q, projected):
                    sp.wait_ge(proj_done, projected)
                    for n in range(4):
                        head_cols = w_hl[:, n, ds(pair * P, P)].bitcast(F32).rearrange("p (h c) -> p h c", h=2)
                        for t in range(2):
                            sp.dma_start(w_pair[par][:, n, :, t * A_HD:(t + 1) * A_HD].bitcast(F32),
                                         head_cols).then_inc(pair_loaded[par], 16)
                    sp.dma_start(wv_pair[par][:].bitcast(F32),
                                 w_hl[:, 4:6, ds(pair * P, P)].bitcast(F32)).then_inc(pair_loaded[par], 16)

                with sp.Fori(0, BATCH) as b:
                    base = b * (PAIRS * GROUPS)
                    fetch(0, 0, b, 0, base)
                    fetch(1, 1, b, 0, base)
                    with sp.Fori(0, PAIRS // 2 - 1) as q:
                        fetch(0, q * 2 + 2, b, q, base + (q * 2 + 1) * GROUPS)
                        fetch(1, q * 2 + 3, b, q, base + (q * 2 + 2) * GROUPS)

            @block.gpsimd
            def _(pool):
                with pool.Fori(0, 2 * BATCH) as n:
                    inverse_root(pool, norm, g.minus_half[:, 0:NB], n)

            @block.tensor
            def _(pe):
                def project(par, k, loads, before):
                    if k == 0:
                        pe.wait_ge(pair_loaded[par], loads * (9 * 16))
                    pe.wait_ge(proj_hi, before * GROUPS + k)
                    pe.wait_ge(proj_lo, before * QK_GROUPS + min(k, QK_GROUPS))
                    w = w_pair[par]
                    if k < QK_GROUPS:
                        qk, head, half = k // 4, k // 2 % 2, k % 2
                        cols = slice(half * HALF, (half + 1) * HALF)
                        w_hi, w_lo = (w[:, 2 * qk + part, head, :] for part in range(2))
                        todo = split_passes((w_hi, w_lo), (xT_hi[:, cols], xT_lo[:, cols]))
                        for n, (a, r) in enumerate(todo):
                            last = pe.matmul(p_ps[:], a, r, start=n == 0, stop=n == len(todo) - 1)
                    else:
                        for t in range(4):
                            blk = (k - QK_GROUPS) * 4 + t
                            toks = slice(blk * P, (blk + 1) * P)
                            todo = split_passes((xT_hi[:, toks], xT_lo[:, toks]), (wv_pair[par][:, 0, :], wv_pair[par][:, 1, :]))
                            for n, (a, r) in enumerate(todo):
                                last = pe.matmul(p_ps[:, t * P:(t + 1) * P], a, r,
                                                 start=n == 0, stop=n == len(todo) - 1)
                    last.then_inc(proj_done, 1)

                def score(par, i, n, k, h):
                    width = (i + 1) * P
                    pe.wait_ge(exp_done, n * (2 * NB) + (2 * k - 1 + h if k else 0))
                    q = q_st[par][h][:, i * P:(i + 1) * P]
                    for c in range(0, width, HALF):
                        e = min(c + HALF, width)
                        pe.matmul(scores[h][:, c:e], q, k_hh[par][h][:, c:e], start=True, stop=False)
                        last = pe.matmul(scores[h][:, c:e], q, k_ll[par][h][:, c:e], start=False,
                                         stop=e < width)
                    last = pe.matmul(scores[h][:, i * P:width], g.ident_bf[:], g.mask_qk[:],
                                     start=False, stop=True)
                    last.then_inc(scored, 1)

                def turn(i, n, k, turns, h):
                    m = h * ((i + 4) // 4)
                    pe.wait_ge(exp_done, n * (2 * NB) + 2 * k + 1 + h)
                    for c in range(0, i + 1, 4):
                        pe.wait_ge(tr_out[m % 2], n * BANK_TURNS + turns + m // 2)
                        for j in range(c, min(c + 4, i + 1)):
                            last = pe.transpose(tr[m % 2][:, (j - c) * P:(j - c + 1) * P],
                                                probs[i % 2][:, h, j * P:(j + 1) * P], g.ident[:])
                        last.then_inc(tr_done, 1)
                        m += 1

                def spread(i, step):
                    pe.wait_ge(out_kept, step)
                    pe.wait_ge(inv_ready, step + 1)
                    for h in range(2):
                        last = pe.matmul(o_ps[h * A_HD:(h + 1) * A_HD, P:2 * P],
                                         row_inv[:, i, h:h + 1].to_broadcast([P, A_HD]), g.ident[:],
                                         start=True, stop=True)
                    last.then_inc(inv_bc, 1)

                def weigh(par, i, n, step, turns):
                    pe.wait_ge(inv_sb, step + 1)
                    pe.wait_ge(tr_out[0], n * BANK_TURNS + turns)
                    pe.wait_ge(tr_out[1], n * BANK_TURNS + turns)
                    for j in range(i + 1):
                        for h in range(2):
                            rows = slice(h * A_HD, (h + 1) * A_HD)
                            last = pe.matmul(o_ps[rows, 0:P], v_sb[par][:, j, rows],
                                             probsT[i % 2][:, h, j * P:(j + 1) * P], start=j == 0, stop=j == i)
                    last.then_inc(pv_done, 1)

                def attend(par, pair, loads, first, more, b, extra):
                    n = b * PAIRS + pair
                    turns = 0

                    def projections(groups):
                        for k in groups if more else ():
                            project(1 - par, k, b * (PAIRS // 2) + loads, n + 1)

                    pe.wait_ge(proj_hi, n * GROUPS + GROUPS)
                    pe.wait_ge(proj_lo, n * QK_GROUPS + QK_GROUPS)
                    for k in range(NB):
                        i = NB - 1 - k
                        if k:
                            turn(i + 1, n, k - 1, turns, 0)
                        score(par, i, n, k, 0)
                        if k:
                            turn(i + 1, n, k - 1, turns, 1)
                            turns += (i + 5) // 4
                            spread(i + 1, n * NB + k - 1)
                        elif not first:
                            turn_last(n - 1)
                        if k == 0:
                            projections(GROUPS_OF_STEP[k][:1])
                        score(par, i, n, k, 1)
                        if k:
                            projections(GROUPS_OF_STEP[k][:1])
                            weigh(par, i + 1, n, n * NB + k - 1, turns)
                        elif not first:
                            weigh_last(1 - par, n - 1)
                        projections(GROUPS_OF_STEP[k][1:])

                def turn_last(n):
                    for h in range(2):
                        turn(0, n, NB - 1, LAST_TURN, h)
                    spread(0, n * NB + NB - 1)

                def weigh_last(par, n):
                    weigh(par, 0, n, n * NB + NB - 1, BANK_TURNS)

                def input_turned(b, chained):
                    pe.wait_ge(norm.chain, chained)
                    for c in range(2):
                        pe.wait_ge(tr_out[c], b * (PAIRS * BANK_TURNS))
                        for t in range(4):
                            last = pe.transpose(tr[c][:, t * P:(t + 1) * P], x_norm[:, c * 4 + t, :], g.ident[:])
                        last.then_inc(xT_done, 1)

                def output_block(blk):
                    c, t = blk // 4, blk % 4
                    for hp in range(PAIRS):
                        last = pe.matmul(scores[0][:, blk * P:(blk + 1) * P], outT[:, hp, blk * P:(blk + 1) * P],
                                         w_u[:, hp, :], start=hp == 0, stop=hp == PAIRS - 1)
                    if t == 3:
                        last.then_inc(y_done, 1)

                def input_projected(b, between):
                    between(0)
                    pe.wait_ge(xT_hi_done, b * 2 + 2)
                    pe.wait_ge(xT_lo_done, b * 2 + 2)
                    for k in range(GROUPS):
                        project(0, k, b * (PAIRS // 2) + 1, b * PAIRS)
                        between(k + 1)

                input_turned(0, NORM_STEPS)
                input_projected(0, lambda k: None)
                first_pair(attend, 0)
                with pe.Fori(0, BATCH - 1) as b:
                    other_pairs(pe, attend, b)
                    turn_last(b * PAIRS + PAIRS - 1)
                    weigh_last(1, b * PAIRS + PAIRS - 1)
                    input_turned(b + 1, b * CHAIN + 2 * NORM_STEPS)
                    pe.wait_ge(out_kept, b * (PAIRS * NB) + PAIRS * NB)
                    input_projected(b + 1, lambda k: output_block(k) if k < NB else None)
                    pe.wait_ge(y_used, b * 2 + 2)
                    first_pair(attend, b + 1)
                other_pairs(pe, attend, BATCH - 1)
                turn_last(BATCH * PAIRS - 1)
                weigh_last(1, BATCH * PAIRS - 1)
                pe.wait_ge(out_kept, BATCH * PAIRS * NB)
                for blk in range(NB):
                    output_block(blk)

            def keep_turned_groups(eng, bank, i, n, turns, h):
                m = h * ((i + 4) // 4)
                for c in range(0, i + 1, 4):
                    if m % 2 == bank:
                        width = min(4, i + 1 - c) * P
                        eng.wait_ge(tr_done, n * (2 * BANK_TURNS) + 2 * turns + m + 1)
                        out = probsT[i % 2][:, h, c * P:c * P + width]
                        if bank:
                            ins = eng.tensor_copy(out, tr[bank][:, 0:width])
                        else:
                            ins = eng.activation(out, tr[bank][:, 0:width], ACT.Copy)
                        ins.then_inc(tr_out[bank], 1)
                    m += 1

            @block.scalar
            def _(act):
                def keep_projection(par, k, before):
                    act.wait_ge(proj_done, before * GROUPS + k + 1)
                    if k < QK_GROUPS:
                        qk, head, half = k // 4, k // 2 % 2, k % 2
                        out = (q_st, k_hh)[qk][par][head][:, half * HALF:(half + 1) * HALF]
                        act.activation(out, p_ps[:], ACT.Copy,
                                       scale=KEYS_SCALE if qk else 1.0).then_inc(proj_hi, 1)
                    else:
                        t = (k - QK_GROUPS) * 4
                        act.activation(v_sb[par][:, t:t + 4, :], p_ps[:].rearrange("p (t n) -> p t n", t=4),
                                       ACT.Copy).then_inc(proj_hi, 1)

                def exponentials(i, n, k, h):
                    act.wait_ge(max_ready, n * (2 * NB) + 2 * k + h + 1)
                    width = (i + 1) * P
                    act.activation(probs[i % 2][:, h, 0:width], scores[h][:, 0:width], ACT.Exp,
                                   bias=neg_max[:, i, h:h + 1],
                                   accum_out=row_sum[:, i, h:h + 1]).then_inc(exp_done, 1)

                def attend(par, pair, loads, first, more, b, extra):
                    n = b * PAIRS + pair
                    turns = 0

                    def projections(groups):
                        for k in groups if more else ():
                            keep_projection(1 - par, k, n + 1)

                    for k in range(NB):
                        i = NB - 1 - k
                        if k:
                            keep_turned(i + 1, n, turns)
                            turns += (i + 5) // 4
                            keep_inverse(i + 1, n * NB + k - 1)
                        if k == 0:
                            if not first:
                                keep_last(n - 1)
                            projections(GROUPS_OF_STEP[k][:1])
                        exponentials(i, n, k, 0)
                        if k:
                            projections(GROUPS_OF_STEP[k][:1])
                        exponentials(i, n, k, 1)
                        projections(GROUPS_OF_STEP[k][1:])

                def keep_turned(i, n, turns):
                    for h in range(2):
                        keep_turned_groups(act, 0, i, n, turns, h)

                def keep_inverse(i, step):
                    act.wait_ge(inv_bc, step + 1)
                    act.activation(r_bc[i % 2][:], o_ps[:, P:2 * P], ACT.Copy).then_inc(inv_sb, 1)

                def keep_last(n):
                    keep_turned(0, n, LAST_TURN)
                    keep_inverse(0, n * NB + NB - 1)

                def keep_input(b):
                    for c in range(2):
                        act.wait_ge(xT_done, b * 2 + c + 1)
                        act.activation(xT_hi[:, c * HALF:(c + 1) * HALF], tr[c][:], ACT.Copy).then_inc(xT_hi_done, 1)
                    for k in range(GROUPS):
                        keep_projection(0, k, b * PAIRS)

                keep_input(0)
                first_pair(attend, 0)
                with act.Fori(0, BATCH - 1) as b:
                    other_pairs(act, attend, b)
                    keep_last(b * PAIRS + PAIRS - 1)
                    keep_input(b + 1)
                    first_pair(attend, b + 1)
                other_pairs(act, attend, BATCH - 1)
                keep_last(BATCH * PAIRS - 1)

            @block.vector
            def _(dve):
                def keep_low_part(par, k, before):
                    if k >= QK_GROUPS:
                        return
                    qk, head, half = k // 4, k // 2 % 2, k % 2
                    cols = slice(half * HALF, (half + 1) * HALF)
                    dve.wait_ge(proj_hi, before * GROUPS + k + 1)
                    if qk:
                        dve.scalar_tensor_tensor(k_ll[par][head][:, cols], p_ps[:], KEYS_SCALE,
                                                 k_hh[par][head][:, cols].bitcast(F32), ALU.mult,
                                                 ALU.subtract).then_inc(proj_lo, 1)
                    else:
                        low = q_st[par][head][A_HD:P, cols]
                        dve.tensor_tensor(low, p_ps[A_HD:P, :], low.bitcast(F32), ALU.subtract).then_inc(proj_lo, 1)

                def maximum(i, n, k, h):
                    dve.wait_ge(scored, n * (2 * NB) + 2 * k + h + 1)
                    dve.tensor_reduce(neg_max[:, i, h:h + 1], scores[h][:, 0:(i + 1) * P], AX.X, ALU.max,
                                      negate=True).then_inc(max_ready, 1)

                def attend(par, pair, loads, first, more, b, extra):
                    n = b * PAIRS + pair
                    turns = 0

                    def projections(groups):
                        for k in groups if more else ():
                            keep_low_part(1 - par, k, n + 1)

                    for k in range(NB):
                        i = NB - 1 - k
                        if k:
                            invert(i + 1, n, k - 1)
                            keep_turned_groups(dve, 1, i + 1, n, turns, 0)
                        elif not first:
                            invert(0, n - 1, NB - 1)
                        maximum(i, n, k, 0)
                        if k == 0:
                            if not first:
                                keep_last(n - 1)
                            projections(GROUPS_OF_STEP[k][:1])
                        if k:
                            keep_turned_groups(dve, 1, i + 1, n, turns, 1)
                            turns += (i + 5) // 4
                        maximum(i, n, k, 1)
                        if k:
                            projections(GROUPS_OF_STEP[k][:1])
                        elif not first:
                            keep_output(0, pair - 1, n * NB - 1)
                        projections(GROUPS_OF_STEP[k][1:])
                        if k:
                            keep_output(i + 1, pair, n * NB + k - 1)
                        if extra:
                            extra[k]()

                def invert(i, n, k):
                    dve.wait_ge(exp_done, n * (2 * NB) + 2 * k + 2)
                    dve.reciprocal(row_inv[:, i, :], row_sum[:, i, :]).then_inc(inv_ready, 1)

                def keep_output(i, pair, step):
                    dve.wait_ge(pv_done, step + 1)
                    dve.tensor_tensor(outT[:, pair, i * P:(i + 1) * P], o_ps[:, 0:P], r_bc[i % 2][:],
                                      ALU.mult).then_inc(out_kept, 1)

                def keep_last(n):
                    for h in range(2):
                        keep_turned_groups(dve, 1, 0, n, LAST_TURN, h)

                def keep_input(b):
                    for c in range(2):
                        cols = slice(c * HALF, (c + 1) * HALF)
                        dve.wait_ge(xT_hi_done, b * 2 + c + 1)
                        dve.tensor_tensor(xT_lo[:, cols], tr[c][:], xT_hi[:, cols].bitcast(F32),
                                          ALU.subtract).then_inc(xT_lo_done, 1)
                    for k in range(GROUPS):
                        keep_low_part(0, k, b * PAIRS)

                def finish_pairs(b):
                    invert(0, b * PAIRS + PAIRS - 1, NB - 1)
                    keep_last(b * PAIRS + PAIRS - 1)
                    keep_output(0, PAIRS - 1, b * (PAIRS * NB) + PAIRS * NB - 1)

                def normalized(b, chain, count):
                    return layernorm_parts(dve, chain, lambda blk: g.x[:, b * NB + blk, :],
                                           lambda blk: x_norm[:, blk, :], norm, count)

                def add_bias(b):
                    for c in range(2):
                        dve.wait_ge(y_done, b * 2 + c + 1)
                        src = scores[0][:, c * HALF:(c + 1) * HALF].rearrange("p (t n) -> p t n", t=4)
                        dve.tensor_tensor(y[:, 4 * c:4 * c + 4, :], src, b_u[:].unsqueeze(1).to_broadcast([P, 4, D]),
                                          ALU.add).then_inc(y_used, 1)
                    dve.wait_ge(y_used, b * 2 + 2)

                def finish_batch(b, chain, count):
                    y_of = lambda blk: y[:, blk, :]
                    x_all = g.x[:, ds(b * NB, NB), :]

                    def residual():
                        chain.settle()
                        chain.did(dve.tensor_tensor(x_all, x_all, y[:], ALU.add))
                        chain.settle()

                    return layernorm_parts(dve, chain, y_of, y_of, norm, count)[:-1] + [residual]

                for part in normalized(0, Chain(dve, norm.chain), 0):
                    part()
                keep_input(0)
                first_pair(attend, 0)
                with dve.Fori(0, BATCH - 1) as b:
                    chain = Chain(dve, norm.chain, b * CHAIN + NORM_STEPS)
                    other_pairs(dve, attend, b, normalized(b + 1, chain, b * 2 + 1))
                    finish_pairs(b)
                    keep_input(b + 1)
                    add_bias(b)
                    first_pair(attend, b + 1, finish_batch(b, chain, b * 2 + 2))
                    assert chain.n == CHAIN
                chain = Chain(dve, norm.chain, (BATCH - 1) * CHAIN + NORM_STEPS)
                other_pairs(dve, attend, BATCH - 1)
                finish_pairs(BATCH - 1)
                add_bias(BATCH - 1)
                for part in finish_batch(BATCH - 1, chain, BATCH * 2 - 1):
                    part()

        nc.clear_and_free_semaphores(sems)
        nc.all_engine_barrier()


E_ROUTED, E_SHARED = 8, 2
EXPERTS = E_ROUTED + E_SHARED
HID = 256
HB = HID // P
CHUNKS = NBLK * P // HALF
TOP = 8


def mixture_layer0(nc, g):
    with ExitStack() as ctx:
        def sb(name, shape, dt=F32):
            return ctx.enter_context(nc.sbuf_tensor("m_" + name, shape, dt))

        def sem(name):
            return ctx.enter_context(nc.semaphore("m_" + name))

        w12 = sb("w12", [P, EXPERTS, 2, HID])
        w3 = sb("w3", [P, EXPERTS, HB, D])
        w_hl = [sb(f"w_hl{i}", [P, 2, 2, HID], F32R) for i in range(2)]
        b12 = sb("b12", [P, 2, EXPERTS, HB])
        b3 = sb("b3", [EXPERTS, D])
        gate_hl = sb("gate_hl", [P, 2, E_ROUTED], F32R)
        gate_w = sb("gate_w", [P, E_ROUTED])
        gate_b = sb("gate_b", [E_ROUTED, 1])
        iota = sb("iota", [P, E_ROUTED])
        x_norm = sb("x_norm", [P, NB, D])
        xT_hi = sb("xT_hi", [P, NBLK * P], F32R)
        xT_lo = sb("xT_lo", [P, NBLK * P], F32R)
        acc = sb("acc", [P, NBLK, D])
        gates = sb("gates", [P, NBLK, EXPERTS])
        norm = NormTiles(ctx, nc, "m_norm")

        loaded, prepared = sem("loaded"), sem("prepared")
        xT_done, xT_hi_done, xT_lo_done = sem("xT_done"), sem("xT_hi_done"), sem("xT_lo_done")
        lg_done, lgT_kept, turned, gexp_ready, gexp_done = (sem(n) for n in (
            "lg_done", "lgT_kept", "turned", "gexp_ready", "gexp_done"))
        gates_turned, gatesT_kept, b3_done, b3_kept = (sem(n) for n in (
            "gates_turned", "gatesT_kept", "b3_done", "b3_kept"))
        w_free, w_hi_done, w_split = sem("w_free"), sem("w_hi_done"), sem("w_split")
        up_done, silu_done, glu_done = sem("up_done"), sem("silu_done"), sem("glu_done")
        down_done, weighed, added = sem("down_done"), sem("weighed"), sem("added")

        with ExitStack() as pctx:
            def psb(name, shape, dt=F32):
                return pctx.enter_context(nc.sbuf_tensor("m_" + name, shape, dt))

            lgT = psb("lgT", [E_ROUTED, SEQ])
            first = psb("first", [P, 1])
            lg = psb("lg", [P, NB, E_ROUTED])
            top = psb("top", [P, NB, TOP])
            idx = psb("idx", [P, NB, TOP], U32)
            idx_f = psb("idx_f", [P, NB, 2])
            diff = psb("diff", [P, NB, E_ROUTED + 1])
            g_exp = psb("g_exp", [P, NB, E_ROUTED + 1])
            g_sum = psb("g_sum", [P, NB])
            weight = psb("weight", [P, NB, 2])
            hot = [psb(f"hot{i}", [P, NB, E_ROUTED]) for i in range(2)]
            gates_b = psb("gates_b", [P, NB, EXPERTS])
            gatesT = psb("gatesT", [EXPERTS, SEQ])
            tr = [pctx.enter_context(nc.psum_tensor(f"m_tr{i}", [P, HALF], F32)) for i in range(2)]
            lg_ps = pctx.enter_context(nc.psum_tensor("m_lg_ps", [E_ROUTED, SEQ], F32))
            lgt_ps = pctx.enter_context(nc.psum_tensor("m_lgt_ps", [P, HALF], F32))
            gt_ps = pctx.enter_context(nc.psum_tensor("m_gt_ps", [EXPERTS, SEQ], F32))

            CHAIN = NORM_STEPS + 2 * NB + 13

            with nc.Block() as block:
                @block.sync
                def _(sp):
                    small = ((gate_w[:], g.inputs["L0_ffn_gate_w"]), (gate_b[:], g.inputs["L0_ffn_gate_b"].rearrange("(e a) -> e a", a=1)),
                             (iota[:], g.inputs["c_iota"].partition_broadcast(P)),
                             (b3[0:E_ROUTED, :], g.inputs["L0_ffn_rb3"]), (b3[E_ROUTED:EXPERTS, :], g.inputs["L0_ffn_sb3"]))
                    for out, src in small:
                        sp.dma_start(out, src).then_inc(loaded, 16)
                    with nc.allow_non_contiguous_dma(reason="biases, one value per partition"):
                        for e0, n, letter in ((0, E_ROUTED, "r"), (E_ROUTED, E_SHARED, "s")):
                            for j in range(2):
                                src = g.inputs[f"L0_ffn_{letter}b{j + 1}"].rearrange("e (h p) -> p (e h)", p=P)
                                sp.dma_start(b12[:, j, e0:e0 + n, :].rearrange("p e h -> p (e h)"),
                                             src).then_inc(loaded, 16)
                                sp.dma_start(w12[:, e0:e0 + n, j, :], g.inputs[f"L0_ffn_{letter}w{j + 1}"]
                                             .rearrange("e p n -> p e n")).then_inc(loaded, 16)
                            for h in range(HB):
                                sp.dma_start(w3[:, e0:e0 + n, h, :], g.inputs[f"L0_ffn_{letter}w3"]
                                             [:, h * P:(h + 1) * P, :].rearrange("e p n -> p e n")).then_inc(loaded, 16)
                    sp.wait_ge(loaded, 17 * 16)

                @block.gpsimd
                def _(pool):
                    pool.memset(gates[:, :, E_ROUTED:EXPERTS], 1.0 / E_SHARED).then_inc(prepared, 1)
                    with pool.Fori(0, BATCH) as n:
                        inverse_root(pool, norm, g.minus_half[:, 0:NB], n)

                @block.tensor
                def _(pe):
                    with pe.Fori(0, BATCH) as b:
                        pe.wait_ge(norm.chain, b * CHAIN + NORM_STEPS)
                        pe.wait_ge(b3_kept, b * 2)
                        for c in range(2):
                            for t in range(4):
                                last = pe.transpose(tr[c][:, t * P:(t + 1) * P], x_norm[:, c * 4 + t, :], g.ident[:])
                            last.then_inc(xT_done, 1)
                        pe.wait_ge(prepared, 4)
                        for c in range(2):
                            pe.wait_ge(xT_lo_done, b * 2 + c + 1)
                            cols = ds(b * SEQ + c * HALF, HALF)
                            todo = split_passes((gate_hl[:, 0, :], gate_hl[:, 1, :]), (xT_hi[:, cols], xT_lo[:, cols]))
                            for n, (a, r) in enumerate(todo):
                                last = pe.matmul(lg_ps[:, c * HALF:(c + 1) * HALF], a, r, start=n == 0, stop=n == 2)
                        last.then_inc(lg_done, 1)
                        pe.wait_ge(lgT_kept, b + 1)
                        for t in range(NB):
                            last = pe.matmul(lgt_ps[:, t * E_ROUTED:(t + 1) * E_ROUTED], lgT[:, t * P:(t + 1) * P],
                                             g.ident[0:E_ROUTED, 0:E_ROUTED], start=True, stop=True)
                        last.then_inc(turned, 1)
                        pe.wait_ge(norm.chain, b * CHAIN + CHAIN)
                        for t in range(NB):
                            last = pe.transpose(gt_ps[:, t * P:(t + 1) * P], gates_b[:, t, :], g.ident[:])
                        last.then_inc(gates_turned, 1)
                        pe.wait_ge(gatesT_kept, b + 1)
                        for c in range(2):
                            for t in range(4):
                                blk = c * 4 + t
                                last = pe.matmul(tr[c][:, t * P:(t + 1) * P], gatesT[:, blk * P:(blk + 1) * P],
                                                 b3[:], start=True, stop=True)
                            last.then_inc(b3_done, 1)

                @block.scalar
                def _(act):
                    act.wait_ge(loaded, 17 * 16)
                    act.activation(gate_hl[:, 0, :], gate_w[:], ACT.Copy).then_inc(prepared, 1)
                    with act.Fori(0, BATCH) as b:
                        for c in range(2):
                            act.wait_ge(xT_done, b * 2 + c + 1)
                            act.activation(xT_hi[:, ds(b * SEQ + c * HALF, HALF)], tr[c][:],
                                           ACT.Copy).then_inc(xT_hi_done, 1)
                        act.wait_ge(lg_done, b + 1)
                        act.activation(lgT[:], lg_ps[:], ACT.Identity, bias=gate_b[:]).then_inc(lgT_kept, 1)
                        act.wait_ge(gexp_ready, b + 1)
                        act.activation(g_exp[:], diff[:], ACT.Exp).then_inc(gexp_done, 1)
                        act.wait_ge(gates_turned, b + 1)
                        act.activation(gatesT[:], gt_ps[:], ACT.Copy).then_inc(gatesT_kept, 1)

                @block.vector
                def _(dve):
                    dve.wait_ge(prepared, 2)
                    dve.tensor_tensor(gate_hl[:, 1, :], gate_w[:], gate_hl[:, 0, :].bitcast(F32),
                                      ALU.subtract).then_inc(prepared, 1)
                    dve.tensor_copy(gates_b[:, :, E_ROUTED:EXPERTS], gates[:, 0:NB, E_ROUTED:EXPERTS]
                                    ).then_inc(prepared, 1)
                    with dve.Fori(0, BATCH) as b:
                        chain = Chain(dve, norm.chain, b * CHAIN)
                        layernorm(dve, chain, lambda blk: g.x[:, b * NB + blk, :], lambda blk: x_norm[:, blk, :], norm, b)
                        for c in range(2):
                            cols = ds(b * SEQ + c * HALF, HALF)
                            dve.wait_ge(xT_hi_done, b * 2 + c + 1)
                            dve.tensor_tensor(xT_lo[:, cols], tr[c][:], xT_hi[:, cols].bitcast(F32),
                                              ALU.subtract).then_inc(xT_lo_done, 1)
                        dve.wait_ge(turned, b + 1)
                        chain.did(dve.tensor_copy(lg[:], lgt_ps[:, 0:NB * E_ROUTED].rearrange("p (t e) -> p t e", t=NB)))
                        chain.settle()
                        chain.did(dve.tensor_copy(first[:], lg[:, 0, 0:1]))
                        for t in range(NB):
                            chain.did(dve.max(top[:, t, :], lg[:, t, :]))
                        chain.settle()
                        largest = top[:, :, 0:1]
                        chain.did(dve.tensor_tensor(diff[:, :, 0:E_ROUTED], lg[:],
                                                    largest.to_broadcast([P, NB, E_ROUTED]), ALU.subtract))
                        dve.tensor_tensor(diff[:, :, E_ROUTED:], top[:, :, 1:2], largest, ALU.subtract
                                          ).then_inc(gexp_ready, 1)
                        for t in range(NB):
                            chain.did(dve.max_index(idx[:, t, :], top[:, t, :], lg[:, t, :]))
                        chain.settle()
                        chain.did(dve.tensor_copy(idx_f[:], idx[:, :, 0:2]))
                        dve.wait_ge(gexp_done, b + 1)
                        chain.did(dve.tensor_reduce(g_sum[:], g_exp[:, :, 0:E_ROUTED], AX.X, ALU.add))
                        chain.settle()
                        chain.did(dve.reciprocal(weight[:, :, 0], g_sum[:]))
                        for j in range(2):
                            chain.did(dve.tensor_tensor(hot[j][:], iota[:].unsqueeze(1).to_broadcast([P, NB, E_ROUTED]),
                                                        idx_f[:, :, j:j + 1].to_broadcast([P, NB, E_ROUTED]),
                                                        ALU.is_equal))
                        chain.settle()
                        chain.did(dve.tensor_tensor(weight[:, :, 1:2], weight[:, :, 0:1], g_exp[:, :, E_ROUTED:],
                                                    ALU.mult))
                        chain.settle()
                        for j in range(2):
                            chain.did(dve.tensor_tensor(hot[j][:], hot[j][:],
                                                        weight[:, :, j:j + 1].to_broadcast([P, NB, E_ROUTED]), ALU.mult))
                        chain.settle()
                        chain.did(dve.tensor_tensor(gates[:, ds(b * NB, NB), 0:E_ROUTED], hot[0][:], hot[1][:], ALU.add))
                        chain.did(dve.tensor_tensor(gates_b[:, :, 0:E_ROUTED], hot[0][:], hot[1][:], ALU.add))
                        chain.settle()
                        assert chain.n == CHAIN, chain.n
                        for c in range(2):
                            dve.wait_ge(b3_done, b * 2 + c + 1)
                            dve.tensor_copy(acc[:, ds(b * NB + c * 4, 4), :],
                                            tr[c][:].rearrange("p (t n) -> p t n", t=4)).then_inc(b3_kept, 1)

        with ExitStack() as ectx:
            def esb(name, shape, dt=F32):
                return ectx.enter_context(nc.sbuf_tensor("m_" + name, shape, dt))

            silu = [esb(f"silu{i}", [P, HALF]) for i in range(2)]
            glu = [[esb(f"glu{i}{h}", [P, HALF]) for h in range(HB)] for i in range(2)]
            bias = [esb(f"bias{i}", [P, 2, HB]) for i in range(2)]
            taken = esb("taken", [P, 1])
            part = [esb(f"part{i}", [P, 4, D]) for i in range(2)]
            up = [[ectx.enter_context(nc.psum_tensor(f"m_up{i}{j}", [P, HALF], F32)) for j in range(2)]
                  for i in range(2)]
            down = [ectx.enter_context(nc.psum_tensor(f"m_down{i}", [P, HALF], F32)) for i in range(2)]

            def experts(eng, run):
                with eng.Fori(0, EXPERTS // 2 - 1) as q:
                    for par in range(2):
                        run(par, q, True)
                for par in range(2):
                    run(par, EXPERTS // 2 - 1, par == 0)

            def chunk_pairs(eng, par, q, run):
                with eng.Fori(0, CHUNKS // 2) as t:
                    run(t, (q * 2 + par) * CHUNKS + t * 2)

            with nc.Block() as block:
                @block.gpsimd
                def _(pool):
                    def split_hi(par, e):
                        pool.tensor_copy(w_hl[par][:, 0], w12[:, e]).then_inc(w_hi_done, 1)
                        pool.tensor_copy(bias[par][:], b12[:, :, e, :]).then_inc(w_hi_done, 1)

                    def expert(par, q, more):
                        if more:
                            pool.wait_ge(glu_done, (q * 2 + par) * (CHUNKS * HB))
                            pool.tensor_tensor(taken[:], norm.mean[:, 0:1], norm.mean[:, 0:1], ALU.add
                                               ).then_inc(w_free, 1)
                            split_hi(1 - par, q * 2 + par + 1)

                    split_hi(0, 0)
                    experts(pool, expert)

                @block.tensor
                def _(pe):
                    def expert(par, q, more):
                        e = q * 2 + par

                        def chunks(t, before):
                            pe.wait_ge(w_split, e + 1)

                            def raise_(c, h):
                                cols = ds(t * (2 * HALF) + c * HALF, HALF)
                                pe.wait_ge(glu_done, before * HB + max(c * HB + h - 1, 0))
                                for j in range(2):
                                    w = [w_hl[par][:, s, j, h * P:(h + 1) * P] for s in range(2)]
                                    todo = split_passes(w, (xT_hi[:, cols], xT_lo[:, cols]))
                                    for n, (a, r) in enumerate(todo):
                                        last = pe.matmul(up[h][j][:], a, r, start=n == 0, stop=n == 2)
                                last.then_inc(up_done, 1)

                            def lower(c):
                                n = before + c
                                pe.wait_ge(weighed, before)
                                for h in range(HB):
                                    pe.wait_ge(glu_done, n * HB + h + 1)
                                    for b in range(4):
                                        last = pe.matmul(down[c][:, b * P:(b + 1) * P], glu[c][h][:, b * P:(b + 1) * P],
                                                         w3[:, e, h, :], start=h == 0 and b == 0, stop=h == HB - 1,
                                                         skip_group_check=True)
                                last.then_inc(down_done, 1)

                            raise_(0, 0)
                            raise_(0, 1)
                            raise_(1, 0)
                            lower(0)
                            raise_(1, 1)
                            lower(1)

                        chunk_pairs(pe, par, q, chunks)

                    experts(pe, expert)

                @block.scalar
                def _(act):
                    def expert(par, q, more):
                        def chunks(t, before):
                            for u in range(2 * HB):
                                h = u % HB
                                act.wait_ge(up_done, before * HB + u + 1)
                                act.activation(silu[h][:], up[h][0][:], ACT.Silu,
                                               bias=bias[par][:, 0, h:h + 1]).then_inc(silu_done, 1)

                        chunk_pairs(act, par, q, chunks)

                    experts(act, expert)

                @block.vector
                def _(dve):
                    def expert(par, q, more):
                        e = q * 2 + par

                        def chunks(t, before):
                            def gate_up(c, h):
                                dve.wait_ge(silu_done, before * HB + c * HB + h + 1)
                                dve.scalar_tensor_tensor(glu[c][h][:], up[h][1][:], bias[par][:, 1, h:h + 1], silu[h][:],
                                                         ALU.add, ALU.mult).then_inc(glu_done, 1)

                            def weigh(c):
                                dve.wait_ge(down_done, before + c + 1)
                                dve.wait_ge(added, before)
                                dve.tensor_tensor(part[c][:], down[c][:].rearrange("p (t n) -> p t n", t=4),
                                                  gates[:, ds(t * 8 + c * 4, 4), e].unsqueeze(2).to_broadcast([P, 4, D]),
                                                  ALU.mult).then_inc(weighed, 1)
                                sums = acc[:, ds(t * 8 + c * 4, 4), :]
                                dve.wait_ge(weighed, before + c + 1)
                                dve.tensor_tensor(sums, sums, part[c][:], ALU.add).then_inc(added, 1)

                            gate_up(0, 0)
                            gate_up(0, 1)
                            gate_up(1, 0)
                            weigh(0)
                            gate_up(1, 1)
                            weigh(1)

                        if more:
                            split_lo(1 - par, e + 1)
                        chunk_pairs(dve, par, q, chunks)

                    def split_lo(par, e):
                        dve.wait_ge(w_hi_done, e * 2 + 2)
                        dve.tensor_tensor(w_hl[par][:, 1], w12[:, e], w_hl[par][:, 0].bitcast(F32),
                                          ALU.subtract).then_inc(w_split, 1)

                    split_lo(0, 0)
                    experts(dve, expert)

            with nc.Block() as block:
                @block.gpsimd
                def _(pool):
                    with pool.Fori(0, BATCH) as n:
                        inverse_root(pool, norm, g.minus_half[:, 0:NB], n + BATCH)

                @block.vector
                def _(dve):
                    with dve.Fori(0, BATCH) as b:
                        chain = Chain(dve, norm.chain, BATCH * CHAIN + b * (NORM_STEPS + 1))
                        y_of = lambda blk: acc[:, b * NB + blk, :]
                        layernorm(dve, chain, y_of, y_of, norm, b + BATCH)
                        batch = g.x[:, ds(b * NB, NB), :]
                        chain.did(dve.tensor_tensor(batch, batch, acc[:, ds(b * NB, NB), :], ALU.add))
                        chain.settle()


HEADS, KV, HD = 16, 4, 8
GQ = HEADS // KV
LAT = 32
WINDOW = 32
QK = (HEADS + KV) * HD
SLOT = 32
REPS = SLOT // HD
LOCAL_W = P + WINDOW
RMS_EPS = 1e-6
STEPS = KV * NB


def attention_layer1(nc, g, local):
    tag = "l_" if local else "g_"
    with ExitStack() as ctx:
        def sb(name, shape, dt=F32):
            return ctx.enter_context(nc.sbuf_tensor(tag + name, shape, dt))

        def sem(name):
            return ctx.enter_context(nc.semaphore(tag + name))

        w_in = sb("w_in", [P, 192])
        w_up = sb("w_up", [LAT, 2 * KV * HD])
        w_o = sb("w_o", [P, D])
        norm_w = sb("norm_w", [P, 1])
        cos, sin = sb("cos", [P, NB, HD // 2]), sb("sin", [P, NB, HD // 2])
        normed = sb("normed", [P, NB, D])
        normedT = sb("normedT", [P, SEQ])
        latT = sb("latT", [LAT, SEQ])
        qk = sb("qk", [P, NB, QK])
        squares = sb("squares", [P, NB, QK])
        part = [sb(f"part{i}", [P, NB * QK // 2]) for i in range(4)]
        turned = sb("turned", [P, NB, QK])
        ssq, rs = sb("ssq", [P, NB * (HEADS + KV)]), sb("rs", [P, NB * (HEADS + KV)])
        newton = sb("newton", [P, NB * (HEADS + KV)])
        ss_h, rs_h = sb("ss_h", [P, NB]), sb("rs_h", [P, NB])
        q_slots = [sb(f"q_slots{j}", [P, NB, P], F32R) for j in range(GQ)]
        k_slots = sb("k_slots", [P, NB, P], F32R)
        v_next = sb("v_next", [P, NB, KV * HD])
        values = sb("values", [P, NB, KV, SLOT])
        qT = [sb(f"qT{j}", [P, SEQ], F32R) for j in range(GQ)]
        kT = [sb(f"kT{h}", [P, SEQ], F32R) for h in range(KV)]
        PW = LOCAL_W if local else SEQ
        probsT = [sb(f"probsT{i}", [P, GQ, PW]) for i in range(2)]
        outT = [sb(f"outT{i}", [P, SEQ]) for i in range(2)]
        inv = sb("inv", [P, NB, GQ])
        att = sb("att", [P, NB, D])
        attT = sb("attT", [P, SEQ])

        s_ps = [ctx.enter_context(nc.psum_tensor(f"{tag}s_ps{i}", [P, SEQ], F32)) for i in range(2)]
        o_ps = ctx.enter_context(nc.psum_tensor(f"{tag}o_ps", [P, SEQ], F32))
        x_ps = ctx.enter_context(nc.psum_tensor(f"{tag}x_ps", [P, SEQ], F32))

        loaded, scaled, zeroed = sem("loaded"), sem("scaled"), sem("zeroed")
        chain, var_ready, rs_ready = sem("chain"), sem("var_ready"), sem("rs_ready")
        normedT_done, normedT_kept, lat_done, lat_kept = (sem(n) for n in (
            "normedT_done", "normedT_kept", "lat_done", "lat_kept"))
        qkv_done, qk_kept, v_kept, squared = sem("qkv_done"), sem("qk_kept"), sem("v_kept"), sem("squared")
        qk_var, qk_root = sem("qk_var"), sem("qk_root")
        half_rot, q_hi, k_hi = sem("half_rot"), sem("q_hi"), sem("k_hi")
        kT_done, kT_kept = sem("kT_done"), [sem("kT_kept_act"), sem("kT_kept_dve")]
        qT_done, qT_kept = sem("qT_done"), [sem("qT_kept_act"), sem("qT_kept_dve")]
        scored, exp_done, pv_done, o_kept = sem("scored"), sem("exp_done"), sem("pv_done"), sem("o_kept")
        back_done, att_kept, attT_done, attT_kept, out_done = (sem(n) for n in (
            "back_done", "att_kept", "attT_done", "attT_kept", "out_done"))

        names = {False: ("g_wq", "g_kv_down", "g_wo", "norm1_w", "c_rope_g"),
                 True: ("l_wq", "l_wk", "l_wo", "norm2_w", "c_rope_l")}[local]
        wq, wk, wo, nw = (g.inputs[f"L1_attn_{n}"] for n in names[:4])
        rope = g.inputs[names[4]]
        CHAIN_NORMED, CHAIN_TURNED = 3, 13
        CHAIN_PREPARED = CHAIN_TURNED + 1 + GQ
        CHAIN = CHAIN_PREPARED + KV * GQ + 1
        TURN_INPUT, PROJECT, ROOT = (5 if local else 3), (11, 13), 22

        with nc.Block() as block:
            @block.sync
            def _(sp):
                sp.dma_start(w_in[:, 0:D], wq).then_inc(loaded, 16)
                sp.dma_start(w_in[:, D:D + 32], wk).then_inc(loaded, 16)
                if local:
                    sp.dma_start(w_in[:, D + 32:D + 64], g.inputs["L1_attn_l_wv"]).then_inc(loaded, 16)
                    sp.dma_start(w_up[:, 0:32], g.inputs["L1_attn_g_k_up"]).then_inc(loaded, 16)
                else:
                    sp.dma_start(w_up[:, 0:32], g.inputs["L1_attn_g_k_up"]).then_inc(loaded, 16)
                    sp.dma_start(w_up[:, 32:64], g.inputs["L1_attn_g_v_up"]).then_inc(loaded, 16)
                sp.dma_start(w_o[:], wo).then_inc(loaded, 16)
                sp.dma_start(norm_w[:], nw.rearrange("(p a) -> p a", a=1)).then_inc(loaded, 16)
                sp.dma_start(cos[:], rope[0].rearrange("(t p) n -> p t n", p=P)).then_inc(loaded, 16)
                sp.dma_start(sin[:], rope[1].rearrange("(t p) n -> p t n", p=P)).then_inc(loaded, 16)

            @block.gpsimd
            def _(pool):
                for j in range(GQ):
                    pool.memset(q_slots[j][:].bitcast(F32), 0.0)
                pool.memset(k_slots[:].bitcast(F32), 0.0)
                pool.memset(values[:], 0.0).then_inc(zeroed, 1)
                pool.wait_ge(zeroed, 1)
                pool.memset(values[:, :, :, HD:HD + 1], 1.0)

            @block.vector
            def _(dve):
                for h in range(KV):
                    dve.memset(kT[h][:].bitcast(F32), 0.0)
                dve.wait_ge(loaded, 8 * 16)
                width = 192 if local else 160
                dve.tensor_scalar(w_in[:, 0:width], w_in[:, 0:width], norm_w[:], None, ALU.mult)

        heads = QK // HD
        as_pairs = lambda t: t[:].rearrange("p t (h n two) -> p t h n two", h=heads, two=2)
        even, odd = (as_pairs(qk)[:, :, :, :, c] for c in range(2))
        t_even, t_odd = (as_pairs(turned)[:, :, :, :, c] for c in range(2))
        parts = [p[:].rearrange("p (t h n) -> p t h n", t=NB, h=heads) for p in part]
        spread = lambda t: t[:].unsqueeze(2).to_broadcast([P, NB, heads, HD // 2])
        slots = lambda t: t[:].rearrange("p t (s r d) -> p t s r d", s=KV, r=REPS)
        q_of = lambda j: turned[:, :, 0:HEADS * HD].rearrange("p t (s j d) -> p t s j d", s=KV, j=GQ)[:, :, :, j, :]
        k_of = turned[:, :, HEADS * HD:QK].rearrange("p t (s d) -> p t s d", s=KV)

        def query_cols(kb):
            lo, hi = kb * P, min(kb * P + LOCAL_W, SEQ) if local else SEQ
            starts = [lo] + ([HALF] if lo < HALF < hi else [])
            return [(a, min(hi, a // HALF * HALF + HALF)) for a in starts]

        def heads_at_once(kb):
            width = query_cols(kb)[-1][1] - kb * P
            return max(n for n in (1, 2, GQ) if n * 256 * -(-width // 256) <= SEQ)

        def units_before(n):
            a_head = [GQ // heads_at_once(kb) for kb in range(NB)]
            return n // NB * sum(a_head) + sum(a_head[:n % NB])

        UNITS = units_before(STEPS)

        def batches(eng, prepare, run):
            prepare(0)
            run(0, True, False)
            with eng.Fori(0, BATCH - 2) as i:
                run(i + 1, False, False)
            run(BATCH - 1, False, True)

        with nc.Block() as block:
            @block.gpsimd
            def _(pool):
                def prepare(x):
                    if not local:
                        inverse_root(pool, g.norm1, g.minus_half[:, 0:NB], x)
                    pool.wait_ge(var_ready, x + 1)
                    pool.tensor_tensor(rs_h[:], ss_h[:], g.minus_half[:, 0:NB], ALU.pow).then_inc(rs_ready, 1)
                    pool.wait_ge(qk_kept, x * 2 + 2)
                    pool.tensor_tensor(parts[2], even, spread(sin), ALU.mult).then_inc(half_rot, 1)
                    pool.tensor_tensor(parts[3], odd, spread(cos), ALU.mult).then_inc(half_rot, 1)

                def attend(b, first, last):
                    if not last:
                        prepare(b + 1)
                    if local and not first:
                        inverse_root(pool, g.norm1, g.minus_half[:, 0:NB], b - 1 + BATCH)

                batches(pool, prepare, attend)
                if local:
                    inverse_root(pool, g.norm1, g.minus_half[:, 0:NB], 2 * BATCH - 1)

            @block.tensor
            def _(pe):
                def turn_input(x, chained):
                    pe.wait_ge(chain, chained)
                    for blk in range(NB):
                        last = pe.transpose(x_ps[:, blk * P:(blk + 1) * P], normed[:, blk, :], g.ident[:])
                    last.then_inc(normedT_done, 1)

                def project_latent(x):
                    pe.wait_ge(normedT_kept, x + 1)
                    for c in range(2):
                        last = pe.matmul(x_ps[0:LAT, c * HALF:(c + 1) * HALF], w_in[:, D:D + LAT],
                                         normedT[:, c * HALF:(c + 1) * HALF], start=True, stop=True)
                    last.then_inc(lat_done, 1)

                def input_read(x):
                    if local:
                        pe.wait_ge(normedT_kept, x + 1)
                    else:
                        pe.wait_ge(lat_kept, x + 1)

                def projection_read(x, c):
                    pe.wait_ge(qk_kept, x * 2 + c + 1)
                    pe.wait_ge(v_kept, x * 2 + c + 1)

                def project(x, c):
                    input_read(x)
                    if c:
                        projection_read(x, 0)
                    for t in range(NB // 2):
                        blk = c * (NB // 2) + t
                        out = x_ps[:, t * 256:t * 256 + 192]
                        rows = slice(blk * P, (blk + 1) * P)
                        if local:
                            last = pe.matmul(out, normedT[:, rows], w_in[:], start=True, stop=True)
                        else:
                            pe.matmul(out[:, 0:D], normedT[:, rows], w_in[:, 0:D], start=True, stop=True)
                            last = pe.matmul(out[:, D:], latT[:, rows], w_up[:], start=True, stop=True)
                    last.then_inc(qkv_done, 1)

                def prepare(x):
                    turn_input(x, CHAIN_NORMED)
                    if not local:
                        project_latent(x)
                    project(x, 0)
                    project(x, 1)
                    projection_read(x, 1)

                def attend(b, first, last_batch):
                    done = CHAIN_PREPARED + b * CHAIN
                    pe.wait_ge(chain, done - (0 if first else 1))
                    for blk in range(NB):
                        last = pe.transpose(x_ps[:, blk * P:(blk + 1) * P], k_slots[:, blk, :].bitcast(F32), g.ident[:])
                    last.then_inc(kT_done, 1)
                    for j in range(GQ):
                        if j == 0:
                            pe.wait_ge(chain, done)
                        if j == 1:
                            pe.wait_ge(kT_kept[0], b + 1)
                            pe.wait_ge(kT_kept[1], b + 1)
                        if j >= 2:
                            pe.wait_ge(qT_kept[0], b * GQ + j - 1)
                            pe.wait_ge(qT_kept[1], b * GQ + j - 1)
                        for blk in range(NB):
                            last = pe.transpose((o_ps, x_ps)[j % 2][:, blk * P:(blk + 1) * P],
                                                q_slots[j][:, blk, :].bitcast(F32), g.ident[:])
                        last.then_inc(qT_done, 1)
                    pe.wait_ge(qT_kept[0], b * GQ + GQ)
                    pe.wait_ge(qT_kept[1], b * GQ + GQ)

                    def score(n, unit):
                        h, kb = n // NB, n % NB
                        u = units_before(n) + unit
                        if u >= 2:
                            pe.wait_ge(exp_done, b * UNITS + u - 1)
                        together = heads_at_once(kb)
                        cols = query_cols(kb) if together == 1 else [(kb * P, query_cols(kb)[-1][1])]
                        for i in range(together):
                            off = i * (SEQ // together) - kb * P if together > 1 else 0
                            clears = together < GQ or i % 2 == 0
                            for a, e in cols:
                                pe.matmul(s_ps[u % 2][:, a + off:e + off], kT[h][:, kb * P:(kb + 1) * P],
                                          qT[unit * together + i][:, a:e], start=clears, stop=False,
                                          skip_group_check=True)
                            a = kb * P
                            width = cols[-1][1] - a if local else P
                            last = pe.matmul(s_ps[u % 2][:, a + off:a + off + width], g.ident_bf[:],
                                             (g.mask_window if local else g.mask_kq)[:, 0:width],
                                             start=False, stop=True, skip_group_check=True)
                        last.then_inc(scored, 1)

                    def weigh(n, chunks):
                        h, kb = n // NB, n % NB
                        cols = query_cols(kb)
                        for c in chunks:
                            if c >= len(cols):
                                continue
                            if c == 0:
                                pe.wait_ge(exp_done, b * UNITS + units_before(n + 1))
                                if kb == 0:
                                    pe.wait_ge(o_kept, b * KV + h)
                            a, e = cols[c]
                            first = (kb == 0 and a == 0) or (a == HALF and (kb == 3 if local else kb == 0))
                            for j in range(GQ):
                                col = a - kb * P if local else a
                                last = pe.matmul(o_ps[j * SLOT:(j + 1) * SLOT, a:e], values[:, kb, h, :],
                                                 probsT[n % 2][:, j, col:col + e - a], start=first, stop=True,
                                                 skip_group_check=True)
                            if c == len(cols) - 1:
                                last.then_inc(pv_done, 1)

                    def turn_back(h):
                        pe.wait_ge(o_kept, b * KV + h + 1)
                        if h:
                            pe.wait_ge(att_kept, b * KV + h)
                        if h == 0 and not last_batch:
                            input_read(b + 1)
                        if h == 1 and not last_batch:
                            projection_read(b + 1, 1)
                        for blk in range(NB):
                            last = pe.transpose(x_ps[:, blk * P:(blk + 1) * P], outT[h % 2][:, blk * P:(blk + 1) * P],
                                                g.ident[:])
                        last.then_inc(back_done, 1)

                    def project_next(c):
                        pe.wait_ge(att_kept, b * KV + 1)
                        project(b + 1, c)

                    pieces = {} if last_batch else {
                        TURN_INPUT: lambda: turn_input(b + 1, done + CHAIN_NORMED),
                        PROJECT[0]: lambda: project_next(0), PROJECT[1]: lambda: project_next(1)}
                    if not (last_batch or local):
                        pieces[TURN_INPUT + 1] = lambda: project_latent(b + 1)
                    for n in range(STEPS):
                        units = GQ // heads_at_once(n % NB)
                        for unit in range(units):
                            score(n, unit)
                            if n and unit == (units - 1) // 2:
                                weigh(n - 1, (0,) if units > 1 else (0, 1))
                        if n and units > 1:
                            weigh(n - 1, (1,))
                        if n > NB and n % NB == 1:
                            turn_back(n // NB - 1)
                        if n in pieces:
                            pieces[n]()
                    weigh(STEPS - 1, (0, 1))
                    turn_back(KV - 1)
                    pe.wait_ge(att_kept, b * KV + KV)
                    for blk in range(NB):
                        last = pe.transpose(x_ps[:, blk * P:(blk + 1) * P], att[:, blk, :], g.ident[:])
                    last.then_inc(attT_done, 1)
                    pe.wait_ge(attT_kept, b + 1)
                    for blk in range(NB):
                        last = pe.matmul(o_ps[:, blk * P:(blk + 1) * P], attT[:, blk * P:(blk + 1) * P], w_o[:],
                                         start=True, stop=True)
                    last.then_inc(out_done, 1)

                batches(pe, prepare, attend)

            def keep_qT_kT(eng, bank, b):
                cols = slice(bank * HALF, (bank + 1) * HALF)

                def keep(out, src):
                    return eng.tensor_copy(out, src) if bank else eng.activation(out, src, ACT.Copy)

                eng.wait_ge(kT_done, b + 1)
                for h in range(KV):
                    rows = slice(h * SLOT, (h + 1) * SLOT)
                    last = keep(kT[h][rows, cols], x_ps[rows, cols])
                last.then_inc(kT_kept[bank], 1)
                for j in range(GQ):
                    eng.wait_ge(qT_done, b * GQ + j + 1)
                    keep(qT[j][:, cols], (o_ps, x_ps)[j % 2][:, cols]).then_inc(qT_kept[bank], 1)

            @block.scalar
            def _(act):
                def keep_input(x):
                    act.wait_ge(normedT_done, x + 1)
                    act.activation(normedT[:], x_ps[:], ACT.Copy).then_inc(normedT_kept, 1)

                def keep_latent(x):
                    act.wait_ge(lat_done, x + 1)
                    act.activation(latT[:], x_ps[0:LAT, :], ACT.Copy).then_inc(lat_kept, 1)

                def keep_qk(x, c):
                    act.wait_ge(qkv_done, x * 2 + c + 1)
                    src = x_ps[:].rearrange("p (t n) -> p t n", t=NB // 2)
                    act.activation(qk[:, 4 * c:4 * c + 4, :], src[:, :, 0:QK], ACT.Copy).then_inc(qk_kept, 1)

                def square(x):
                    act.wait_ge(qk_kept, x * 2 + 2)
                    act.activation(squares[:], qk[:], ACT.Square).then_inc(squared, 1)

                def root(x):
                    act.wait_ge(qk_var, x + 1)
                    act.activation(rs[:], ssq[:], ACT.Sqrt).then_inc(qk_root, 1)

                def high_parts(x, chained):
                    def k_part(r):
                        act.wait_ge(chain, chained)
                        act.activation(slots(k_slots)[:, :, :, r, :], k_of, ACT.Copy).then_inc(k_hi, 1)

                    def q_part(j, r):
                        act.activation(slots(q_slots[j])[:, :, :, r, :], q_of(j), ACT.Copy).then_inc(q_hi, 1)

                    return [*(lambda r=r: k_part(r) for r in range(2)),
                            *(lambda j=j, r=r: q_part(j, r) for j in range(GQ) for r in (0, 2))]

                def prepare(x):
                    keep_input(x)
                    if not local:
                        keep_latent(x)
                    keep_qk(x, 0)
                    keep_qk(x, 1)
                    square(x)
                    root(x)
                    for part in high_parts(x, CHAIN_TURNED):
                        part()

                def attend(b, first, last):
                    keep_qT_kT(act, 0, b)
                    pieces = {}
                    if not last:
                        pieces = {TURN_INPUT + 1: lambda: keep_input(b + 1), PROJECT[0] + 1: lambda: keep_qk(b + 1, 0),
                                  PROJECT[1] + 1: lambda: keep_qk(b + 1, 1), PROJECT[1] + 2: lambda: square(b + 1),
                                  ROOT: lambda: root(b + 1)}
                        if not local:
                            pieces[TURN_INPUT + 2] = lambda: keep_latent(b + 1)
                    for n in range(STEPS):
                        kb = n % NB
                        together = heads_at_once(kb)
                        for unit in range(GQ // together):
                            u = units_before(n) + unit
                            act.wait_ge(scored, b * UNITS + u + 1)
                            if n >= 2 and unit == 0:
                                act.wait_ge(pv_done, b * STEPS + n - 1)
                            width = min(LOCAL_W if local else SEQ, SEQ - kb * P)
                            at = 0 if local else kb * P
                            out = probsT[n % 2][:, unit * together:(unit + 1) * together, at:at + width]
                            src = s_ps[u % 2][:, kb * P:SEQ].unsqueeze(1)
                            if together > 1:
                                src = s_ps[u % 2][:].rearrange("p (j n) -> p j n", j=together)[:, :, 0:width]
                            act.activation(out, src, ACT.Exp, scale=float(HD) ** -0.5).then_inc(exp_done, 1)
                        if n in pieces:
                            pieces[n]()
                    if not last:
                        for part in high_parts(b + 1, CHAIN_PREPARED + b * CHAIN + CHAIN_TURNED + 3 * GQ):
                            part()
                    act.wait_ge(attT_done, b + 1)
                    act.activation(attT[:], x_ps[:], ACT.Copy).then_inc(attT_kept, 1)

                batches(act, prepare, attend)

            @block.vector
            def _(dve):
                def normalize(x, own):
                    hidden = g.hidden[:, ds(x * NB, NB), :]
                    if not local:
                        norm_chain = Chain(dve, g.norm1.chain, x * NORM_STEPS)
                        layernorm(dve, norm_chain, lambda blk: g.x[:, x * NB + blk, :],
                                  lambda blk: g.hidden[:, x * NB + blk, :], g.norm1, x)
                    own.did(dve.tensor_tensor(normed[:], hidden, hidden, ALU.mult))
                    own.settle()
                    own.did(dve.tensor_reduce(ss_h[:], normed[:], AX.X, ALU.add))
                    own.settle()
                    dve.tensor_scalar(ss_h[:], ss_h[:], 1.0 / D, RMS_EPS, ALU.mult, ALU.add).then_inc(var_ready, 1)
                    dve.wait_ge(rs_ready, x + 1)
                    own.did(dve.tensor_tensor(normed[:], hidden, rs_h[:].unsqueeze(2).to_broadcast([P, NB, D]), ALU.mult))

                def rotate(x, own):
                    for c in range(2):
                        dve.wait_ge(qk_kept, x * 2 + c + 1)
                        src = x_ps[:].rearrange("p (t n) -> p t n", t=NB // 2)[:, :, QK:192]
                        dve.tensor_copy(v_next[:, 4 * c:4 * c + 4, :], src).then_inc(v_kept, 1)
                    own.did(dve.tensor_tensor(parts[0], even, spread(cos), ALU.mult))
                    own.did(dve.tensor_tensor(parts[1], odd, spread(sin), ALU.mult))

                def sum_rotation(x, own):
                    dve.wait_ge(squared, x + 1)
                    own.did(dve.tensor_reduce(ssq[:], squares[:].rearrange("p t (h d) -> p (t h) d", d=HD), AX.X, ALU.add))
                    own.settle()
                    dve.tensor_scalar(ssq[:], ssq[:], 1.0 / HD, RMS_EPS, ALU.mult, ALU.add).then_inc(qk_var, 1)
                    own.did(dve.tensor_tensor(t_even, parts[0], parts[1], ALU.subtract))
                    dve.wait_ge(half_rot, x * 2 + 2)
                    own.did(dve.tensor_tensor(t_odd, parts[2], parts[3], ALU.add))

                def scale_heads(x, own):
                    dve.wait_ge(qk_root, x + 1)
                    own.did(dve.reciprocal(rs[:], rs[:]))
                    own.settle()
                    own.did(dve.tensor_tensor(newton[:], rs[:], rs[:], ALU.mult))
                    own.settle()
                    own.did(dve.scalar_tensor_tensor(newton[:], newton[:], -0.5, ssq[:], ALU.mult, ALU.mult))
                    own.settle()
                    own.did(dve.scalar_tensor_tensor(rs[:], newton[:], 1.5, rs[:], ALU.add, ALU.mult))
                    own.settle()
                    by_head = turned[:].rearrange("p t (h d) -> p (t h) d", d=HD)
                    own.did(dve.tensor_tensor(by_head, by_head, rs[:].unsqueeze(2).to_broadcast([P, NB * heads, HD]),
                                              ALU.mult))
                    own.settle()

                def low_parts(x, own):
                    dve.wait_ge(k_hi, x * 2 + 2)
                    own.did(dve.tensor_tensor(slots(k_slots)[:, :, :, 2, :], k_of,
                                              slots(k_slots)[:, :, :, 0, :].bitcast(F32), ALU.subtract))
                    for j in range(GQ):
                        dve.wait_ge(q_hi, x * (2 * GQ) + 2 * j + 2)
                        own.did(dve.tensor_tensor(slots(q_slots[j])[:, :, :, 1, :], q_of(j),
                                                  slots(q_slots[j])[:, :, :, 0, :].bitcast(F32), ALU.subtract))

                def prepare(x):
                    own = Chain(dve, chain)
                    normalize(x, own)
                    assert own.n == CHAIN_NORMED
                    rotate(x, own)
                    sum_rotation(x, own)
                    scale_heads(x, own)
                    assert own.n == CHAIN_TURNED
                    low_parts(x, own)
                    assert own.n == CHAIN_PREPARED

                def residual(x, count):
                    norm_chain = Chain(dve, g.norm1.chain, BATCH * NORM_STEPS + x * (NORM_STEPS + 1))
                    y_of = lambda blk: g.hidden[:, x * NB + blk, :]

                    def add():
                        norm_chain.settle()
                        batch = g.x[:, ds(x * NB, NB), :]
                        norm_chain.did(dve.tensor_tensor(batch, batch, g.hidden[:, ds(x * NB, NB), :], ALU.add))
                        norm_chain.settle()

                    return layernorm_parts(dve, norm_chain, y_of, y_of, g.norm1, count)[:-1] + [add]

                def attend(b, first, last):
                    own = Chain(dve, chain, CHAIN_PREPARED + b * CHAIN)
                    dve.tensor_copy(values[:, :, :, 0:HD], v_next[:].rearrange("p t (s d) -> p t s d", s=KV))
                    keep_qT_kT(dve, 1, b)
                    nexts = [rotate, sum_rotation, scale_heads, low_parts]
                    ends = residual(b - 1, b - 1 + BATCH) if local and not first else []
                    ends_by_head = [ends[0:4], ends[4:5], ends[5:6], ends[6:]]
                    if not last:
                        normalize(b + 1, own)
                    for h in range(KV):
                        dve.wait_ge(pv_done, b * STEPS + h * NB + NB)
                        dve.tensor_copy(outT[h % 2][:], o_ps[:]).then_inc(o_kept, 1)
                        dve.wait_ge(back_done, b * KV + h + 1)
                        back = x_ps[:].rearrange("p (t j s) -> p t j s", t=NB, j=GQ)
                        own.did(dve.reciprocal(inv[:], back[:, :, :, HD]))
                        own.settle()
                        for j in range(GQ):
                            head = (h * GQ + j) * HD
                            ins = dve.tensor_tensor(att[:, :, head:head + HD], back[:, :, j, 0:HD],
                                                    inv[:, :, j:j + 1].to_broadcast([P, NB, HD]), ALU.mult)
                            if j < GQ - 1:
                                own.did(ins)
                        ins.then_inc(att_kept, 1)
                        if not last:
                            nexts[h](b + 1, own)
                        for part in ends_by_head[h]:
                            part()
                    dve.wait_ge(out_done, b + 1)
                    hidden = g.hidden[:, ds(b * NB, NB), :]
                    own.did(dve.tensor_tensor(hidden, hidden, o_ps[:].rearrange("p (t n) -> p t n", t=NB), ALU.add))
                    own.settle()
                    assert last or own.n == CHAIN, own.n

                batches(dve, prepare, attend)
                if local:
                    for part in residual(BATCH - 1, 2 * BATCH - 1):
                        part()


def layer1_attention(nc, g):
    with ExitStack() as ctx:
        g.hidden = ctx.enter_context(nc.sbuf_tensor("hidden", [P, NBLK, D], F32))
        g.norm1 = NormTiles(ctx, nc, "norm1")
        attention_layer1(nc, g, local=False)
        attention_layer1(nc, g, local=True)


SE, SS = 8, 64
SLOTS = SE * SS
SB = SLOTS // P
S_HID = 512
S_HB = S_HID // P
COLS = BATCH * SS
UNITS_A, UNITS_B = SB, NB // 2


def soft_mixture(nc, g, out):
    with ExitStack() as ctx:
        def sb(name, shape, dt=F32):
            return ctx.enter_context(nc.sbuf_tensor("s_" + name, shape, dt))

        def sem(name):
            return ctx.enter_context(nc.semaphore("s_" + name))

        w1 = sb("w1", [P, SE, S_HID])
        w2 = sb("w2", [P, SE, S_HB, D])
        b1 = sb("b1", [P, SE, S_HB])
        b2 = sb("b2", [P, SB, D])
        gamma, slot_gamma = sb("gamma", [P, D]), sb("slot_gamma", [P, D])
        slot_in = sb("slot_in", [P, SB, D])
        snT = [sb(f"snT{i}", [P, SLOTS], F32R) for i in range(2)]
        combine = sb("combine", [P, SB, NBLK * P])
        inv_c = sb("inv_c", [P, NBLK])
        slotsT = sb("slotsT", [P, SE, BATCH, SS])
        norm = NormTiles(ctx, nc, "s_norm")
        ss, rs = sb("ss", [P, NB]), sb("rs", [P, NB])

        loaded, chain, ss_ready, rs_ready = sem("loaded"), sem("chain"), sem("ss_ready"), sem("rs_ready")
        turned, hi_done = sem("turned"), sem("hi_done")
        root = float(D) ** 0.5

        with nc.psum_tensor("s_first_ps", [P, SLOTS], F32) as first_ps, nc.sbuf_tensor("s_sq", [P, SB, D], F32) as sq:
            with nc.Block() as block:
                @block.sync
                def _(sp):
                    sp.dma_start(slot_in[:], g.inputs["L1_ffn_slot_embeds"].rearrange("(q e) s n -> (e s) q n", e=2)
                                 ).then_inc(loaded, 16)
                    sp.dma_start(slot_gamma[:], g.inputs["L1_ffn_slot_norm_gamma"].partition_broadcast(P)).then_inc(loaded, 16)
                    sp.dma_start(gamma[:], g.inputs["L1_ffn_norm_gamma"].partition_broadcast(P)).then_inc(loaded, 16)
                    with nc.allow_non_contiguous_dma(reason="biases, one value per partition"):
                        sp.dma_start(b1[:].rearrange("p e h -> p (e h)"),
                                     g.inputs["L1_ffn_b1"].rearrange("e (h p) -> p (e h)", p=P)).then_inc(loaded, 16)
                    by_pair = g.inputs["L1_ffn_b2"].rearrange("(q e) n -> e q n", e=2)
                    for e in range(2):
                        sp.dma_start(b2[e * SS:(e + 1) * SS], by_pair[e].partition_broadcast(SS)).then_inc(loaded, 16)
                    sp.dma_start(w1[:], g.inputs["L1_ffn_w1"].rearrange("e p n -> p e n")).then_inc(loaded, 16)
                    for h in range(S_HB):
                        sp.dma_start(w2[:, :, h, :], g.inputs["L1_ffn_w2"][:, h * P:(h + 1) * P, :].rearrange("e p n -> p e n")
                                     ).then_inc(loaded, 16)

                @block.gpsimd
                def _(pool):
                    pool.wait_ge(ss_ready, 1)
                    pool.tensor_tensor(rs[:, 0:SB], ss[:, 0:SB], g.minus_half[:, 0:SB], ALU.pow).then_inc(rs_ready, 1)

                @block.tensor
                def _(pe):
                    pe.wait_ge(chain, 4 + SB)
                    for q in range(SB):
                        last = pe.transpose(first_ps[:, q * P:(q + 1) * P], sq[:, q, :], g.ident[:])
                    last.then_inc(turned, 1)

                @block.scalar
                def _(act):
                    act.wait_ge(turned, 1)
                    act.activation(snT[0][:], first_ps[:], ACT.Copy).then_inc(hi_done, 1)

                @block.vector
                def _(dve):
                    own = Chain(dve, chain)
                    dve.wait_ge(loaded, 11 * 16)
                    own.did(dve.tensor_scalar(gamma[:], gamma[:], root, None, ALU.mult))
                    own.did(dve.tensor_scalar(slot_gamma[:], slot_gamma[:], root, None, ALU.mult))
                    own.did(dve.tensor_tensor(sq[:], slot_in[:], slot_in[:], ALU.mult))
                    own.settle()
                    own.did(dve.tensor_reduce(ss[:, 0:SB], sq[:], AX.X, ALU.add))
                    own.settle()
                    dve.tensor_scalar(ss[:, 0:SB], ss[:, 0:SB], 1e-24, None, ALU.max).then_inc(ss_ready, 1)
                    dve.wait_ge(rs_ready, 1)
                    for q in range(SB):
                        own.did(dve.scalar_tensor_tensor(sq[:, q, :], slot_in[:, q, :], rs[:, q:q + 1], slot_gamma[:],
                                                         ALU.mult, ALU.mult))
                    assert own.n == 4 + SB
                    dve.wait_ge(hi_done, 1)
                    dve.tensor_tensor(snT[1][:], first_ps[:], snT[0][:].bitcast(F32), ALU.subtract)

        with ExitStack() as lctx:
            def lsb(name, shape, dt=F32):
                return lctx.enter_context(nc.sbuf_tensor("s_" + name, shape, dt))

            hidden, xn = lsb("hidden", [P, NB, D]), lsb("xn", [P, NB, D])
            xT = [lsb(f"xT{i}", [P, SEQ], F32R) for i in range(2)]
            minus_max = lsb("minus_max", [P, UNITS_A + 2 * UNITS_B])
            sums, inv_d = lsb("sums", [P, UNITS_A + 2 * UNITS_B]), lsb("inv_d", [P, UNITS_A])
            exps = [lsb(f"exps{i}", [P, SEQ]) for i in range(2)]
            dispatch = lsb("dispatch", [P, NB, SLOTS])
            logits = [lctx.enter_context(nc.psum_tensor(f"s_logits{i}", [P, SEQ], F32)) for i in range(2)]
            tr = [lctx.enter_context(nc.psum_tensor(f"s_tr{i}", [P, SEQ], F32)) for i in range(2)]
            xT_hi_done, xT_lo_done = sem("xT_hi_done"), sem("xT_lo_done")
            lg_done, max_done, exp_done, scaled = sem("lg_done"), sem("max_done"), sem("exp_done"), sem("scaled")
            tr_done, slots_done = sem("tr_done"), sem("slots_done")
            read_act, read_dve = sem("read_act"), sem("read_dve")

            UNITS = UNITS_A + UNITS_B
            CHAIN_XN = NORM_STEPS + 2 + NB
            CHAIN = CHAIN_XN + UNITS_A + UNITS_B
            READS_ACT, READS_DVE = UNITS + 1, UNITS
            EXPS = UNITS_A + 2 * UNITS_B
            exps_by = lambda u: u + 1 if u < UNITS_A else UNITS_A + 2 * (u - UNITS_A + 1)

            with nc.Block() as block:
                @block.gpsimd
                def _(pool):
                    with pool.Fori(0, BATCH) as b:
                        inverse_root(pool, norm, g.minus_half[:, 0:NB], b)
                        pool.wait_ge(ss_ready, b + 2)
                        pool.tensor_tensor(rs[:], ss[:], g.minus_half[:, 0:NB], ALU.pow).then_inc(rs_ready, 1)

                @block.tensor
                def _(pe):
                    with pe.Fori(0, BATCH) as b:
                        def tile_read(k):
                            pe.wait_ge(read_dve, b * READS_DVE + max(k - 1, 0))
                            pe.wait_ge(read_act, b * READS_ACT + max(k - 1, 0))

                        pe.wait_ge(norm.chain, b * CHAIN + CHAIN_XN)
                        tile_read(0)
                        for t in range(NB):
                            last = pe.transpose(tr[1][:, t * P:(t + 1) * P], xn[:, t, :], g.ident[:])
                        last.then_inc(tr_done, 1)
                        pe.wait_ge(xT_lo_done, b + 1)

                        def score(u):
                            if u >= 2:
                                pe.wait_ge(exp_done, b * EXPS + exps_by(u - 2))
                            for c in range(2):
                                if u < UNITS_A:
                                    a = [snT[i][:, u * P:(u + 1) * P] for i in range(2)]
                                    r = [xT[i][:, c * HALF:(c + 1) * HALF] for i in range(2)]
                                else:
                                    blk = (u - UNITS_A) * 2 + c
                                    a = [xT[i][:, blk * P:(blk + 1) * P] for i in range(2)]
                                    r = [snT[i][:] for i in range(2)]
                                for n, (l, m) in enumerate(split_passes(a, r)):
                                    last = pe.matmul(logits[u % 2][:, c * HALF:(c + 1) * HALF], l, m,
                                                     start=n == 0, stop=n == 2)
                            last.then_inc(lg_done, 1)

                        def turn(u):
                            if u < UNITS_A:
                                pe.wait_ge(scaled, b * UNITS_A + u + 1)
                            else:
                                pe.wait_ge(exp_done, b * EXPS + exps_by(u))
                            tile_read(u)
                            for t in range(NB):
                                last = pe.transpose(tr[u % 2][:, t * P:(t + 1) * P], exps[u % 2][:, t * P:(t + 1) * P],
                                                    g.ident[:])
                            last.then_inc(tr_done, 1)

                        score(0)
                        for u in range(UNITS):
                            if u + 1 < UNITS:
                                score(u + 1)
                            turn(u)
                        tile_read(UNITS)
                        for t in range(NB):
                            last = pe.matmul(tr[0][:, 0:SLOTS], xn[:, t, :], dispatch[:, t, :], start=t == 0,
                                             stop=t == NB - 1)
                        last.then_inc(slots_done, 1)

                def place(u, c):
                    src = tr[u % 2][:, c * HALF:(c + 1) * HALF].rearrange("p (t n) -> p t n", t=4)
                    if u < UNITS_A:
                        return (lambda b: dispatch[:, 4 * c:4 * c + 4, u * P:(u + 1) * P]), src
                    blk = (u - UNITS_A) * 2 + c
                    return (lambda b: combine[:, :, ds(b * SEQ + blk * P, P)]), src

                @block.scalar
                def _(act):
                    with act.Fori(0, BATCH) as b:
                        act.wait_ge(tr_done, b * (UNITS + 1) + 1)
                        act.activation(xT[0][:], tr[1][:], ACT.Copy).then_inc(xT_hi_done, 1)

                        def move(u):
                            to, src = place(u, 0)
                            act.wait_ge(tr_done, b * (UNITS + 1) + u + 2)
                            act.activation(to(b), src, ACT.Copy).then_inc(read_act, 1)

                        for u in range(UNITS):
                            act.wait_ge(max_done, b * UNITS + u + 1)
                            if u >= 2:
                                act.wait_ge(tr_done, b * (UNITS + 1) + u)
                            for i in range(1 if u < UNITS_A else 2):
                                w = SEQ if u < UNITS_A else HALF
                                n = exps_by(u) - (1 if u < UNITS_A else 2) + i
                                act.activation(exps[u % 2][:, i * w:(i + 1) * w], logits[u % 2][:, i * w:(i + 1) * w],
                                               ACT.Exp, bias=minus_max[:, n:n + 1], accum_out=sums[:, n:n + 1]
                                               ).then_inc(exp_done, 1)
                            if u:
                                move(u - 1)
                        move(UNITS - 1)
                        act.wait_ge(slots_done, b + 1)
                        act.activation(slotsT[:, :, b, :], tr[0][:, 0:SLOTS].rearrange("p (e s) -> p e s", e=SE),
                                       ACT.Copy).then_inc(read_act, 1)

                @block.vector
                def _(dve):
                    with dve.Fori(0, BATCH) as b:
                        own = Chain(dve, norm.chain, b * CHAIN)
                        layernorm(dve, own, lambda t: g.x[:, b * NB + t, :], lambda t: hidden[:, t, :], norm, b)
                        dve.wait_ge(slots_done, b)
                        own.did(dve.tensor_tensor(xn[:], hidden[:], hidden[:], ALU.mult))
                        own.settle()
                        own.did(dve.tensor_reduce(ss[:], xn[:], AX.X, ALU.add))
                        own.settle()
                        dve.tensor_scalar(ss[:], ss[:], 1e-24, None, ALU.max).then_inc(ss_ready, 1)
                        dve.wait_ge(rs_ready, b + 2)
                        for t in range(NB):
                            own.did(dve.scalar_tensor_tensor(xn[:, t, :], hidden[:, t, :], rs[:, t:t + 1], gamma[:],
                                                             ALU.mult, ALU.mult))
                        assert own.n == CHAIN_XN
                        dve.wait_ge(xT_hi_done, b + 1)
                        dve.tensor_tensor(xT[1][:], tr[1][:], xT[0][:].bitcast(F32), ALU.subtract
                                          ).then_inc(xT_lo_done, 1)

                        def move(u):
                            to, src = place(u, 1)
                            dve.wait_ge(tr_done, b * (UNITS + 1) + u + 2)
                            dve.tensor_copy(to(b), src).then_inc(read_dve, 1)

                        def largest(u):
                            dve.wait_ge(lg_done, b * UNITS + u + 1)
                            if u < UNITS_A:
                                ins = dve.tensor_reduce(minus_max[:, u:u + 1], logits[u % 2][:], AX.X, ALU.max, negate=True)
                            else:
                                n = exps_by(u) - 2
                                ins = dve.tensor_reduce(minus_max[:, n:n + 2], logits[u % 2][:].rearrange(
                                    "p (i n) -> p i n", i=2), AX.X, ALU.max, negate=True)
                            ins.then_inc(max_done, 1)

                        largest(0)
                        for u in range(UNITS):
                            if u + 1 < UNITS:
                                largest(u + 1)
                            dve.wait_ge(exp_done, b * EXPS + exps_by(u))
                            if u < UNITS_A:
                                own.did(dve.reciprocal(inv_d[:, u:u + 1], sums[:, u:u + 1]))
                                own.settle()
                                dve.tensor_scalar(exps[u % 2][:], exps[u % 2][:], inv_d[:, u:u + 1], None, ALU.mult
                                                  ).then_inc(scaled, 1)
                            else:
                                n = exps_by(u) - 2
                                own.did(dve.reciprocal(inv_c[:, ds(b * NB + 2 * (u - UNITS_A), 2)], sums[:, n:n + 2]))
                            move(u)
                        assert own.n == CHAIN, own.n

        with ExitStack() as ectx:
            def esb(name, shape, dt=F32):
                return ectx.enter_context(nc.sbuf_tensor("s_" + name, shape, dt))

            w1_e = [esb(f"w1_e{i}", [P, S_HID]) for i in range(2)]
            w2_e = [esb(f"w2_e{i}", [P, S_HB, D]) for i in range(2)]
            hT = [esb(f"hT{i}", [P, S_HB, COLS]) for i in range(2)]
            slot_out = esb("slot_out", [P, SB, BATCH, D])
            eo_b = [esb(f"eo_b{i}", [P, SB, D]) for i in range(2)]
            mixedT = esb("mixedT", [P, SEQ])
            mixed = esb("mixed", [P, NB, D])
            up = [ectx.enter_context(nc.psum_tensor(f"s_up{i}", [P, S_HB, COLS], F32)) for i in range(2)]
            down = ectx.enter_context(nc.psum_tensor("s_down", [P, BATCH * D], F32))
            w1_ready, w2_ready, up_done, gelu_done = sem("w1_ready"), sem("w2_ready"), sem("up_done"), sem("gelu_done")
            down_done, down_kept = sem("down_done"), sem("down_kept")

            with nc.Block() as block:
                @block.tensor
                def _(pe):
                    def raise_(par, e):
                        pe.wait_ge(w1_ready, e + 1)
                        for h in range(S_HB):
                            last = pe.matmul(up[par][:, h, :], w1_e[par][:, h * P:(h + 1) * P], slotsT[:, e],
                                             start=True, stop=True)
                            if h % 2:
                                last.then_inc(up_done, 1)

                    def lower(par, e, q):
                        pe.wait_ge(w2_ready, e + 1)
                        pe.wait_ge(gelu_done, (e + 1) * S_HB)
                        if par == 0:
                            pe.wait_ge(down_kept, q)
                        for b in range(BATCH):
                            for h in range(S_HB):
                                last = pe.matmul(down[par * SS:(par + 1) * SS, b * D:(b + 1) * D],
                                                 hT[par][:, h, b * SS:(b + 1) * SS], w2_e[par][:, h, :],
                                                 start=h == 0 and b == 0, stop=h == S_HB - 1, skip_group_check=True)
                        last.then_inc(down_done, 1)

                    raise_(0, 0)
                    with pe.Fori(0, SB - 1) as q:
                        for par in range(2):
                            raise_(1 - par, q * 2 + par + 1)
                            lower(par, q * 2 + par, q)
                    raise_(1, SE - 1)
                    for par in range(2):
                        lower(par, SE - 2 + par, SB - 1)

                @block.scalar
                def _(act):
                    with act.Fori(0, SB) as q:
                        for par in range(2):
                            e = q * 2 + par
                            for h in range(S_HB):
                                if h % 2 == 0:
                                    act.wait_ge(up_done, e * (S_HB // 2) + h // 2 + 1)
                                act.activation(hT[par][:, h, :], up[par][:, h, :], ACT.Gelu,
                                               bias=b1[:, e, h:h + 1]
                                               ).then_inc(gelu_done, 1)

                @block.vector
                def _(dve):
                    def take_up(par, e):
                        dve.tensor_copy(w1_e[par][:], w1[:, e, :]).then_inc(w1_ready, 1)

                    def take_down(par, e):
                        dve.tensor_copy(w2_e[par][:], w2[:, e]).then_inc(w2_ready, 1)

                    def keep(q):
                        dve.wait_ge(down_done, q * 2 + 2)
                        dve.tensor_tensor(slot_out[:, q], down[:].rearrange("p (b n) -> p b n", b=BATCH),
                                          b2[:, q, :].unsqueeze(1).to_broadcast([P, BATCH, D]), ALU.add
                                          ).then_inc(down_kept, 1)

                    for par in range(2):
                        take_up(par, par)
                        take_down(par, par)
                    with dve.Fori(0, SB - 1) as q:
                        for par in range(2):
                            dve.wait_ge(up_done, (q * 2 + par + 1) * (S_HB // 2))
                            take_up(par, q * 2 + par + 2)
                            dve.wait_ge(down_done, q * 2 + par + 1)
                            take_down(par, q * 2 + par + 2)
                        keep(q)
                    keep(SB - 1)

            eo_ready, mixT_done, mixT_kept, mix_done, mix_kept, x_done, stored = (sem(n) for n in (
                "eo_ready", "mixT_done", "mixT_kept", "mix_done", "mix_kept", "x_done", "stored"))
            mixT_ps, mix_ps = up[0], up[1]
            flat = lambda t: t[:].rearrange("p h n -> p (h n)")
            base = BATCH * CHAIN
            with nc.Block() as block:
                @block.sync
                def _(sp):
                    for b in range(BATCH):
                        sp.wait_ge(x_done, b + 1)
                        sp.dma_start(out[b].rearrange("(t p) n -> p t n", p=P), g.x[:, b * NB:(b + 1) * NB, :]
                                     ).then_inc(stored, 16)
                    sp.wait_ge(stored, BATCH * 16)

                @block.gpsimd
                def _(pool):
                    with pool.Fori(0, BATCH) as b:
                        inverse_root(pool, norm, g.minus_half[:, 0:NB], b + BATCH)

                @block.tensor
                def _(pe):
                    with pe.Fori(0, BATCH // 2) as pair:
                        for par in range(2):
                            b = pair * 2 + par
                            pe.wait_ge(eo_ready, b + 1)
                            for c in range(2):
                                for q in range(SB):
                                    last = pe.matmul(flat(mixT_ps)[:, c * HALF:(c + 1) * HALF], eo_b[par][:, q, :],
                                                     combine[:, q, ds(b * SEQ + c * HALF, HALF)], start=q == 0,
                                                     stop=q == SB - 1)
                            last.then_inc(mixT_done, 1)
                            pe.wait_ge(mixT_kept, b + 1)
                            pe.wait_ge(mix_kept, b)
                            for t in range(NB):
                                last = pe.transpose(flat(mix_ps)[:, t * P:(t + 1) * P], mixedT[:, t * P:(t + 1) * P],
                                                    g.ident[:])
                            last.then_inc(mix_done, 1)

                @block.scalar
                def _(act):
                    def take(par, b):
                        act.activation(eo_b[par][:], slot_out[:, :, b, :], ACT.Copy).then_inc(eo_ready, 1)

                    with act.Fori(0, BATCH // 2) as pair:
                        for par in range(2):
                            take(par, pair * 2 + par)
                        for par in range(2):
                            b = pair * 2 + par
                            act.wait_ge(mixT_done, b + 1)
                            act.activation(mixedT[:], flat(mixT_ps), ACT.Copy).then_inc(mixT_kept, 1)

                @block.vector
                def _(dve):
                    with dve.Fori(0, BATCH) as b:
                        own = Chain(dve, norm.chain, b * NORM_STEPS + base)
                        dve.wait_ge(x_done, b)
                        dve.wait_ge(mix_done, b + 1)
                        dve.tensor_tensor(mixed[:], flat(mix_ps).rearrange("p (t n) -> p t n", t=NB),
                                          inv_c[:, ds(b * NB, NB)].unsqueeze(2).to_broadcast([P, NB, D]),
                                          ALU.mult).then_inc(mix_kept, 1)
                        dve.wait_ge(mix_kept, b + 1)
                        layernorm(dve, own, lambda t: mixed[:, t, :], lambda t: mixed[:, t, :], norm, b + BATCH)
                        assert own.n == NORM_STEPS
                        batch = g.x[:, ds(b * NB, NB), :]
                        dve.tensor_tensor(batch, batch, mixed[:], ALU.add).then_inc(x_done, 1)


def constants():
    i = np.arange(P)
    k, q = i[:, None], np.arange(LOCAL_W)[None, :]

    def rotation(base):
        inv_freq = np.float32(1.0) / np.float32(base) ** (np.arange(0, HD, 2, dtype=np.float32) / np.float32(HD))
        angles = np.arange(SEQ, dtype=np.float32)[:, None] * inv_freq[None, :].astype(np.float32)
        return np.stack([np.cos(angles), np.sin(angles)]).astype(np.float32)

    return {
        "c_ident": np.eye(P, dtype=np.float32),
        "c_iota": np.arange(E_ROUTED, dtype=np.float32),
        "c_mask_kq": np.where(i[:, None] > i[None, :], -1e30, 0.0).astype(np.float32),
        "c_mask_window": np.where((q - k >= 0) & (q - k < WINDOW), 0.0, -1e30).astype(np.float32),
        "c_rope_g": rotation(1e6),
        "c_rope_l": rotation(1e4),
        "c_mask_qk": np.where(i[None, :] > i[:, None], -1e30, 0.0).astype(np.float32),
    }


class Shared:
    pass


def build(nc, aps, out):
    g = Shared()
    g.inputs = aps
    with ExitStack() as ctx:
        def sb(name, shape, dt=F32):
            return ctx.enter_context(nc.sbuf_tensor(name, shape, dt))

        g.x = sb("x", [P, NBLK, D])
        g.ident = sb("ident", [P, P])
        g.ident_bf = sb("ident_bf", [P, P], BF16)
        g.mask_qk = sb("mask_qk", [P, P], BF16)
        g.minus_half = sb("minus_half", [P, 256])
        g.mask_kq = sb("mask_kq", [P, P], BF16)
        g.mask_window = sb("mask_window", [P, LOCAL_W], BF16)
        staged = [sb(f"staged{i}", [P, LOCAL_W]) for i in range(3)]
        x_loaded = ctx.enter_context(nc.semaphore("x_loaded"))
        const_loaded = ctx.enter_context(nc.semaphore("const_loaded"))
        masks = ((g.inputs["c_mask_qk"], P), (g.inputs["c_mask_kq"], P), (g.inputs["c_mask_window"], LOCAL_W))
        with nc.Block() as block:
            @block.sync
            def _(sp):
                sp.dma_start(g.ident[:], g.inputs["c_ident"]).then_inc(const_loaded, 16)
                for n, (src, width) in enumerate(masks):
                    sp.dma_start(staged[n][:, 0:width], src).then_inc(const_loaded, 16)
                for b in range(BATCH):
                    sp.dma_start(g.x[:, b * NB:(b + 1) * NB, :],
                                 g.inputs["L0_attn_x"][b].rearrange("(t p) n -> p t n", p=P)).then_inc(x_loaded, 16)

            @block.gpsimd
            def _(pool):
                pool.memset(g.minus_half[:], -0.5)

            @block.vector
            def _(dve):
                dve.wait_ge(const_loaded, 4 * 16)
                dve.tensor_copy(g.ident_bf[:], g.ident[:])
                for n, (out, (_, width)) in enumerate(zip((g.mask_qk, g.mask_kq, g.mask_window), masks)):
                    dve.tensor_copy(out[:], staged[n][:, 0:width])
                dve.wait_ge(x_loaded, 64)
        attention_layer0(nc, g)
        mixture_layer0(nc, g)
        layer1_attention(nc, g)
        soft_mixture(nc, g, out)



def kernel(**inputs):
    import concourse.bacc as _bacc
    from concourse.bass_utils import run_bass_kernel_spmd as _run

    nc = _bacc.Bacc("TRN2", target_bir_lowering=False, num_devices=1)
    arrays, aps = {}, {}
    for name, a in (inputs | constants()).items():
        a = np.ascontiguousarray(a)
        arrays[f"in_{name}"] = a
        aps[name] = nc.dram_tensor(f"in_{name}", a.shape, mybir.dt.from_np(a.dtype), kind="ExternalInput").ap()
    out = nc.dram_tensor("out_x", (BATCH, SEQ, D), F32, kind="ExternalOutput").ap()
    build(nc, aps, out)
    return _run(nc, [arrays], core_ids=[0]).results[0]["out_x"]
```

```python
import numpy as np
import concourse.bass as bass
from concourse import mybir
from contextlib import ExitStack

F32 = mybir.dt.float32
F32R = mybir.dt.float32r
BF16 = mybir.dt.bfloat16
U32 = mybir.dt.uint32
ALU = mybir.AluOpType
ACT = mybir.ActivationFunctionType
AX = mybir.AxisListType
ds = bass.ds

P = 128
BATCH, SEQ, D = 4, 1024, 128
NB = SEQ // P
NBLK = BATCH * NB
HALF = 512
LN_EPS = 1e-5


class Chain:

    def __init__(self, eng, sem, base=0):
        self.eng, self.sem, self.base, self.n = eng, sem, base, 0

    def did(self, ins):
        ins.then_inc(self.sem, 1)
        self.n += 1

    def settle(self):
        self.eng.wait_ge(self.sem, self.base + self.n)


def split_passes(hi_lo_a, hi_lo_b):
    (ah, al), (bh, bl) = hi_lo_a, hi_lo_b
    return [(ah, bh), (ah, bl), (al, bh)]




NORM_STEPS = 2 * NB + 5


def layernorm_parts(dve, chain, x_of, out_of, t, count):
    def statistics(blks):
        for blk in blks:
            chain.did(dve.bn_stats(t.stats[:, blk, :], x_of(blk)))

    def variance():
        chain.settle()
        mean_e, sq_e, mean_o, sq_o = (t.stats[:, :, c] for c in (1, 2, 4, 5))
        chain.did(dve.scalar_tensor_tensor(t.square[:], sq_e, D * LN_EPS, sq_o, ALU.add, ALU.add))
        chain.did(dve.tensor_tensor(t.gap[:], mean_e, mean_o, ALU.subtract))
        chain.did(dve.tensor_tensor(t.twice[:], mean_e, mean_o, ALU.add))
        chain.settle()
        chain.did(dve.scalar_tensor_tensor(t.gap[:], t.gap[:], 0.25, t.gap[:], ALU.mult, ALU.mult))
        chain.did(dve.tensor_scalar(t.mean[:], t.twice[:], 0.5, None, ALU.mult))
        chain.settle()
        dve.scalar_tensor_tensor(t.var[:], t.square[:], 1.0 / D, t.gap[:], ALU.mult, ALU.add).then_inc(t.var_ready, 1)

    def normalize(blks):
        dve.wait_ge(t.rstd_ready, count + 1)
        for blk in blks:
            chain.did(dve.tensor_scalar(out_of(blk), x_of(blk), t.mean[:, blk:blk + 1], t.rstd[:, blk:blk + 1],
                                        ALU.subtract, ALU.mult))

    quarters = [range(blk, blk + 2) for blk in range(0, NB, 2)]
    return [*(lambda q=q: statistics(q) for q in quarters), variance,
            *(lambda q=q: normalize(q) for q in (range(0, 4), range(4, NB))), chain.settle]


def layernorm(*args):
    for part in layernorm_parts(*args):
        part()


def inverse_root(pool, t, minus_half, count):
    pool.wait_ge(t.var_ready, count + 1)
    pool.tensor_tensor(t.rstd[:], t.var[:], minus_half, ALU.pow).then_inc(t.rstd_ready, 1)


class NormTiles:

    def __init__(self, ctx, nc, name):
        sb = lambda n, shape: ctx.enter_context(nc.sbuf_tensor(f"{name}_{n}", shape, F32))
        sem = lambda n: ctx.enter_context(nc.semaphore(f"{name}_{n}"))
        self.stats = sb("stats", [P, NB, 6])
        self.square, self.gap, self.twice, self.mean, self.var, self.rstd = (
            sb(n, [P, NB]) for n in ("square", "gap", "twice", "mean", "var", "rstd"))
        self.var_ready, self.rstd_ready, self.chain = sem("var_ready"), sem("rstd_ready"), sem("chain")


A_HEADS, A_HD = 16, 64
PAIRS = A_HEADS // 2
QK_GROUPS, V_GROUPS = 4, 2
GROUPS = QK_GROUPS + V_GROUPS
KEYS_SCALE = 1.0 / A_HD
BANK_TURNS = sum((i + 4) // 4 for i in range(NB))
GROUPS_OF_STEP = [(k - 1,) if 1 <= k <= GROUPS else () for k in range(NB)]


def first_pair(run, b, extra=()):
    run(0, 0, 1, True, True, b, extra)


def other_pairs(eng, run, b, extra=()):
    with eng.Fori(0, PAIRS // 2 - 1) as q:
        for par, pair in ((1, q * 2 + 1), (0, q * 2 + 2)):
            run(par, pair, q + 2, False, True, b, ())
    run(1, PAIRS - 1, 0, False, False, b, extra)


def attention_layer0(nc, g):
    with ExitStack() as ctx:
        def sb(name, shape, dt=F32):
            return ctx.enter_context(nc.sbuf_tensor("a_" + name, shape, dt))

        def pb(name, shape):
            return ctx.enter_context(nc.psum_tensor("a_" + name, shape, F32))

        def sem(name):
            sems.append(nc.alloc_semaphore(name="a_" + name))
            return sems[-1]

        sems = []

        w_hl = sb("w_hl", [P, 6, D * 8], F32R)
        w_u = sb("w_u", [P, PAIRS, D])
        b_u = sb("b_u", [P, D])
        w_pair = [sb(f"w_pair{i}", [P, 6, P], F32R) for i in range(2)]
        q_lo = sb("q_lo", [P, SEQ], F32R)
        x_norm = sb("x_norm", [P, NB, D])
        y = sb("y", [P, NB, D])
        xT_hi = sb("xT_hi", [P, SEQ], F32R)
        xT_lo = sb("xT_lo", [P, SEQ], F32R)
        q_st = [[sb(f"q_st{i}{h}", [P, SEQ], F32R) for h in range(2)] for i in range(2)]
        k_hh = [[sb(f"k_hh{i}{h}", [P, SEQ], F32R) for h in range(2)] for i in range(2)]
        k_ll = [[sb(f"k_ll{i}{h}", [P, SEQ], F32R) for h in range(2)] for i in range(2)]
        v_sb = [sb(f"v{i}", [P, NB, P]) for i in range(2)]
        probs = [sb(f"probs{i}", [P, 2, SEQ]) for i in range(2)]
        probsT = [sb(f"probsT{i}", [P, 2, SEQ]) for i in range(2)]
        outT = sb("outT", [P, PAIRS, SEQ])
        r_bc = [sb(f"r_bc{i}", [P, P]) for i in range(2)]
        neg_max, row_sum, row_inv = (sb(n, [P, NB, 2]) for n in ("neg_max", "row_sum", "row_inv"))
        norm = NormTiles(ctx, nc, "a_norm")

        scores = [pb(f"scores{h}", [P, SEQ]) for h in range(2)]
        tr = [pb(f"tr{i}", [P, HALF]) for i in range(2)]
        o_ps = pb("o_ps", [P, HALF])
        p_ps = pb("p_ps", [P, HALF])
        raw = outT

        first_x_loaded, x_loaded = sem("first_x_loaded"), sem("x_loaded")
        loaded, split_hi, split_lo = sem("loaded"), sem("split_hi"), sem("split_lo")
        moved = sem("moved")
        pair_loaded = [sem(f"pair_loaded{i}") for i in range(2)]
        xT_done, xT_hi_done, xT_lo_done = sem("xT_done"), sem("xT_hi_done"), sem("xT_lo_done")
        proj_done, proj_hi, proj_lo = sem("proj_done"), sem("proj_hi"), sem("proj_lo")
        scored, max_ready, exp_done = sem("scored"), sem("max_ready"), sem("exp_done")
        tr_done, tr_out = sem("tr_done"), [sem("tr_out_act"), sem("tr_out_dve")]
        inv_ready, inv_bc, inv_sb = sem("inv_ready"), sem("inv_bc"), sem("inv_sb")
        pv_done, out_kept = sem("pv_done"), sem("out_kept")
        y_done, y_used = sem("y_done"), sem("y_used")

        with nc.Block() as block:
            @block.sync
            def _(sp):
                def fetch(batches, signal):
                    src = g.inputs["L0_attn_x"][batches[0]:batches[-1] + 1].rearrange("b (t p) n -> p (b t) n", p=P)
                    sp.dma_start(g.x[:, batches[0] * NB:(batches[-1] + 1) * NB, :], src).then_inc(signal, 16)

                fetch([0], first_x_loaded)
                for n, w in enumerate((g.inputs["L0_attn_w_q"], g.inputs["L0_attn_w_k"], g.inputs["L0_attn_w_v"])):
                    sp.dma_start(raw[:, n, :], w).then_inc(loaded, 16)
                fetch(range(1, BATCH), x_loaded)
                sp.dma_start(w_u[:], g.inputs["L0_attn_w_u"].rearrange("(t p) n -> p t n", p=P)).then_inc(x_loaded, 16)
                sp.dma_start(b_u[:], g.inputs["L0_attn_b_u"].partition_broadcast(P)).then_inc(x_loaded, 16)

            @block.scalar
            def _(act):
                act.wait_ge(loaded, 3 * 16)
                for n in range(3):
                    act.activation(w_hl[:, 2 * n, :], raw[:, n, :], ACT.Copy).then_inc(split_hi, 1)

            @block.gpsimd
            def _(pool):
                inverse_root(pool, norm, g.minus_half[:, 0:NB], 0)

            @block.vector
            def _(dve):
                dve.wait_ge(first_x_loaded, 16)
                layernorm(dve, Chain(dve, norm.chain), lambda blk: g.x[:, blk, :], lambda blk: x_norm[:, blk, :], norm, 0)
                for n in range(3):
                    dve.wait_ge(split_hi, n + 1)
                    dve.tensor_tensor(w_hl[:, 2 * n + 1, :], raw[:, n, :],
                                      w_hl[:, 2 * n, :].bitcast(F32), ALU.subtract).then_inc(split_lo, 1)
                dve.wait_ge(split_lo, 3)

        CHAIN = 2 * NORM_STEPS + 1

        LAST_TURN = BANK_TURNS - 1

        with nc.Block() as block:
            @block.sync
            def _(sp):
                def fetch(par, pair, b, q, projected):
                    sp.wait_ge(proj_done, projected)
                    sp.dma_start(w_pair[par][:].bitcast(F32), w_hl[:, :, ds(pair * P, P)].bitcast(F32)
                                 ).then_inc(pair_loaded[par], 16)

                def move(par, n):
                    def to_other_half(h, out, src):
                        own, other = (slice(t * A_HD, (t + 1) * A_HD) for t in (h, 1 - h))
                        sp.dma_start(out[other, :].bitcast(F32), src[own, :].bitcast(F32)).then_inc(moved, 16)

                    sp.wait_ge(proj_lo, n * QK_GROUPS + QK_GROUPS // 2)
                    for h in range(2):
                        to_other_half(h, q_st[par][h], q_lo)
                    sp.wait_ge(proj_lo, n * QK_GROUPS + QK_GROUPS)
                    for h in range(2):
                        for stack in (k_hh, k_ll):
                            to_other_half(h, stack[par][h], stack[par][h])

                with sp.Fori(0, BATCH) as b:
                    base = b * (PAIRS * GROUPS)
                    fetch(0, 0, b, 0, base)
                    fetch(1, 1, b, 0, base)
                    move(0, b * PAIRS)
                    with sp.Fori(0, PAIRS // 2 - 1) as q:
                        fetch(0, q * 2 + 2, b, q, base + (q * 2 + 1) * GROUPS)
                        move(1, b * PAIRS + q * 2 + 1)
                        fetch(1, q * 2 + 3, b, q, base + (q * 2 + 2) * GROUPS)
                        move(0, b * PAIRS + q * 2 + 2)
                    move(1, b * PAIRS + PAIRS - 1)

            @block.gpsimd
            def _(pool):
                with pool.Fori(0, 2 * BATCH - 1) as n:
                    inverse_root(pool, norm, g.minus_half[:, 0:NB], n + 1)

            @block.tensor
            def _(pe):
                def project(par, k, loads, before):
                    if k == 0:
                        pe.wait_ge(pair_loaded[par], loads * 16)
                    pe.wait_ge(proj_hi, before * GROUPS + k)
                    pe.wait_ge(proj_lo, before * QK_GROUPS + min(k, QK_GROUPS))
                    w = w_pair[par]
                    if k < QK_GROUPS:
                        qk, half = k // 2, k % 2
                        cols = slice(half * HALF, (half + 1) * HALF)
                        w_hi, w_lo = (w[:, 2 * qk + part, :] for part in range(2))
                        todo = split_passes((w_hi, w_lo), (xT_hi[:, cols], xT_lo[:, cols]))
                        for n, (a, r) in enumerate(todo):
                            last = pe.matmul(p_ps[:], a, r, start=n == 0, stop=n == len(todo) - 1)
                    else:
                        for t in range(4):
                            blk = (k - QK_GROUPS) * 4 + t
                            toks = slice(blk * P, (blk + 1) * P)
                            todo = split_passes((xT_hi[:, toks], xT_lo[:, toks]), (w[:, 4, :], w[:, 5, :]))
                            for n, (a, r) in enumerate(todo):
                                last = pe.matmul(p_ps[:, t * P:(t + 1) * P], a, r,
                                                 start=n == 0, stop=n == len(todo) - 1)
                    last.then_inc(proj_done, 1)

                def score(par, i, n, k, h):
                    width = (i + 1) * P
                    pe.wait_ge(exp_done, n * (2 * NB) + (2 * k - 1 + h if k else 0))
                    q = q_st[par][h][:, i * P:(i + 1) * P]
                    for c in range(0, width, HALF):
                        e = min(c + HALF, width)
                        pe.matmul(scores[h][:, c:e], q, k_hh[par][h][:, c:e], start=True, stop=False)
                        last = pe.matmul(scores[h][:, c:e], q, k_ll[par][h][:, c:e], start=False,
                                         stop=e < width)
                    last = pe.matmul(scores[h][:, i * P:width], g.ident_bf[:], g.mask_qk[:],
                                     start=False, stop=True)
                    last.then_inc(scored, 1)

                def turn(i, n, k, turns, h):
                    m = h * ((i + 4) // 4)
                    pe.wait_ge(exp_done, n * (2 * NB) + 2 * k + 1 + h)
                    for c in range(0, i + 1, 4):
                        pe.wait_ge(tr_out[m % 2], n * BANK_TURNS + turns + m // 2)
                        for j in range(c, min(c + 4, i + 1)):
                            last = pe.transpose(tr[m % 2][:, (j - c) * P:(j - c + 1) * P],
                                                probs[i % 2][:, h, j * P:(j + 1) * P], g.ident[:])
                        last.then_inc(tr_done, 1)
                        m += 1

                def spread(i, step):
                    pe.wait_ge(out_kept, step)
                    pe.wait_ge(inv_ready, step + 1)
                    for h in range(2):
                        last = pe.matmul(o_ps[h * A_HD:(h + 1) * A_HD, P:2 * P],
                                         row_inv[:, i, h:h + 1].to_broadcast([P, A_HD]), g.ident[:],
                                         start=True, stop=True)
                    last.then_inc(inv_bc, 1)

                def weigh(par, i, n, step, turns):
                    pe.wait_ge(inv_sb, step + 1)
                    pe.wait_ge(tr_out[0], n * BANK_TURNS + turns)
                    pe.wait_ge(tr_out[1], n * BANK_TURNS + turns)
                    for j in range(i + 1):
                        for h in range(2):
                            rows = slice(h * A_HD, (h + 1) * A_HD)
                            last = pe.matmul(o_ps[rows, 0:P], v_sb[par][:, j, rows],
                                             probsT[i % 2][:, h, j * P:(j + 1) * P], start=j == 0, stop=j == i)
                    last.then_inc(pv_done, 1)

                def attend(par, pair, loads, first, more, b, extra):
                    n = b * PAIRS + pair
                    turns = 0

                    def projections(groups):
                        for k in groups if more else ():
                            project(1 - par, k, b * (PAIRS // 2) + loads, n + 1)

                    pe.wait_ge(moved, n * (6 * 16) + 6 * 16)
                    pe.wait_ge(proj_hi, n * GROUPS + QK_GROUPS)
                    pe.wait_ge(proj_lo, n * QK_GROUPS + QK_GROUPS)
                    for k in range(NB):
                        i = NB - 1 - k
                        if k:
                            turn(i + 1, n, k - 1, turns, 0)
                        score(par, i, n, k, 0)
                        if k:
                            turn(i + 1, n, k - 1, turns, 1)
                            turns += (i + 5) // 4
                            spread(i + 1, n * NB + k - 1)
                        elif not first:
                            turn_last(n - 1)
                        if k == 0:
                            projections(GROUPS_OF_STEP[k][:1])
                        score(par, i, n, k, 1)
                        if k:
                            projections(GROUPS_OF_STEP[k][:1])
                            if k == 1:
                                pe.wait_ge(proj_hi, n * GROUPS + GROUPS)
                            weigh(par, i + 1, n, n * NB + k - 1, turns)
                        elif not first:
                            weigh_last(1 - par, n - 1)
                        projections(GROUPS_OF_STEP[k][1:])

                def turn_last(n):
                    for h in range(2):
                        turn(0, n, NB - 1, LAST_TURN, h)
                    spread(0, n * NB + NB - 1)

                def weigh_last(par, n):
                    weigh(par, 0, n, n * NB + NB - 1, BANK_TURNS)

                def input_turned(b, chained):
                    pe.wait_ge(norm.chain, chained)
                    for c in range(2):
                        pe.wait_ge(tr_out[c], b * (PAIRS * BANK_TURNS))
                        for t in range(4):
                            last = pe.transpose(tr[c][:, t * P:(t + 1) * P], x_norm[:, c * 4 + t, :], g.ident[:])
                        last.then_inc(xT_done, 1)

                def output_blocks(blks):
                    for blk in blks:
                        for hp in range(PAIRS):
                            last = pe.matmul(scores[0][:, blk * P:(blk + 1) * P], outT[:, hp, blk * P:(blk + 1) * P],
                                             w_u[:, hp, :], start=hp == 0, stop=hp == PAIRS - 1)
                        if blk % 4 == 3:
                            last.then_inc(y_done, 1)

                def input_projected(b, between):
                    between(0)
                    pe.wait_ge(xT_hi_done, b * 2 + 2)
                    pe.wait_ge(xT_lo_done, b * 2 + 2)
                    for k in range(GROUPS):
                        project(0, k, b * (PAIRS // 2) + 1, b * PAIRS)
                        between(k + 1)

                input_turned(0, NORM_STEPS)
                input_projected(0, lambda k: None)
                first_pair(attend, 0)
                with pe.Fori(0, BATCH - 1) as b:
                    other_pairs(pe, attend, b)
                    turn_last(b * PAIRS + PAIRS - 1)
                    weigh_last(1, b * PAIRS + PAIRS - 1)
                    input_turned(b + 1, b * CHAIN + 2 * NORM_STEPS)
                    pe.wait_ge(out_kept, b * (PAIRS * NB) + PAIRS * NB)
                    input_projected(b + 1, lambda k: output_blocks(range(k, k + 1) if k < GROUPS else range(k, NB)))
                    pe.wait_ge(y_used, b * 2 + 2)
                    first_pair(attend, b + 1)
                other_pairs(pe, attend, BATCH - 1)
                turn_last(BATCH * PAIRS - 1)
                weigh_last(1, BATCH * PAIRS - 1)
                pe.wait_ge(out_kept, BATCH * PAIRS * NB)
                output_blocks(range(NB))

            def keep_turned_groups(eng, bank, i, n, turns, h):
                m = h * ((i + 4) // 4)
                for c in range(0, i + 1, 4):
                    if m % 2 == bank:
                        width = min(4, i + 1 - c) * P
                        eng.wait_ge(tr_done, n * (2 * BANK_TURNS) + 2 * turns + m + 1)
                        out = probsT[i % 2][:, h, c * P:c * P + width]
                        if bank:
                            ins = eng.tensor_copy(out, tr[bank][:, 0:width])
                        else:
                            ins = eng.activation(out, tr[bank][:, 0:width], ACT.Copy)
                        ins.then_inc(tr_out[bank], 1)
                    m += 1

            @block.scalar
            def _(act):
                def keep_projection(par, k, before):
                    act.wait_ge(proj_done, before * GROUPS + k + 1)
                    if k < QK_GROUPS:
                        qk, half = k // 2, k % 2
                        for head in range(2):
                            rows = slice(head * A_HD, (head + 1) * A_HD)
                            out = (q_st, k_hh)[qk][par][head][rows, half * HALF:(half + 1) * HALF]
                            last = act.activation(out, p_ps[rows, :], ACT.Copy, scale=KEYS_SCALE if qk else 1.0)
                        last.then_inc(proj_hi, 1)
                    else:
                        t = (k - QK_GROUPS) * 4
                        act.activation(v_sb[par][:, t:t + 4, :], p_ps[:].rearrange("p (t n) -> p t n", t=4),
                                       ACT.Copy).then_inc(proj_hi, 1)

                def exponentials(i, n, k, h):
                    act.wait_ge(max_ready, n * (2 * NB) + 2 * k + h + 1)
                    width = (i + 1) * P
                    act.activation(probs[i % 2][:, h, 0:width], scores[h][:, 0:width], ACT.Exp,
                                   bias=neg_max[:, i, h:h + 1],
                                   accum_out=row_sum[:, i, h:h + 1]).then_inc(exp_done, 1)

                def attend(par, pair, loads, first, more, b, extra):
                    n = b * PAIRS + pair
                    turns = 0

                    def projections(groups):
                        for k in groups if more else ():
                            keep_projection(1 - par, k, n + 1)

                    for k in range(NB):
                        i = NB - 1 - k
                        if k:
                            keep_turned(i + 1, n, turns)
                            turns += (i + 5) // 4
                            keep_inverse(i + 1, n * NB + k - 1)
                        if k == 0:
                            if not first:
                                keep_last(n - 1)
                            projections(GROUPS_OF_STEP[k][:1])
                        exponentials(i, n, k, 0)
                        if k:
                            projections(GROUPS_OF_STEP[k][:1])
                        exponentials(i, n, k, 1)
                        projections(GROUPS_OF_STEP[k][1:])

                def keep_turned(i, n, turns):
                    for h in range(2):
                        keep_turned_groups(act, 0, i, n, turns, h)

                def keep_inverse(i, step):
                    act.wait_ge(inv_bc, step + 1)
                    act.activation(r_bc[i % 2][:], o_ps[:, P:2 * P], ACT.Copy).then_inc(inv_sb, 1)

                def keep_last(n):
                    keep_turned(0, n, LAST_TURN)
                    keep_inverse(0, n * NB + NB - 1)

                def keep_input(b):
                    for c in range(2):
                        act.wait_ge(xT_done, b * 2 + c + 1)
                        act.activation(xT_hi[:, c * HALF:(c + 1) * HALF], tr[c][:], ACT.Copy).then_inc(xT_hi_done, 1)
                    for k in range(GROUPS):
                        keep_projection(0, k, b * PAIRS)

                keep_input(0)
                first_pair(attend, 0)
                with act.Fori(0, BATCH - 1) as b:
                    other_pairs(act, attend, b)
                    keep_last(b * PAIRS + PAIRS - 1)
                    keep_input(b + 1)
                    first_pair(attend, b + 1)
                other_pairs(act, attend, BATCH - 1)
                keep_last(BATCH * PAIRS - 1)

            @block.vector
            def _(dve):
                def keep_low_part(par, k, before):
                    if k >= QK_GROUPS:
                        return
                    qk, half = k // 2, k % 2
                    cols = slice(half * HALF, (half + 1) * HALF)
                    dve.wait_ge(proj_hi, before * GROUPS + k + 1)
                    for head in range(2):
                        rows = slice(head * A_HD, (head + 1) * A_HD)
                        if qk:
                            last = dve.scalar_tensor_tensor(k_ll[par][head][rows, cols], p_ps[rows, :], KEYS_SCALE,
                                                            k_hh[par][head][rows, cols].bitcast(F32), ALU.mult,
                                                            ALU.subtract)
                        else:
                            last = dve.tensor_tensor(q_lo[rows, cols], p_ps[rows, :],
                                                     q_st[par][head][rows, cols].bitcast(F32), ALU.subtract)
                    last.then_inc(proj_lo, 1)

                def maximum(i, n, k, h):
                    dve.wait_ge(scored, n * (2 * NB) + 2 * k + h + 1)
                    dve.tensor_reduce(neg_max[:, i, h:h + 1], scores[h][:, 0:(i + 1) * P], AX.X, ALU.max,
                                      negate=True).then_inc(max_ready, 1)

                def attend(par, pair, loads, first, more, b, extra):
                    n = b * PAIRS + pair
                    turns = 0

                    def projections(groups):
                        for k in groups if more else ():
                            keep_low_part(1 - par, k, n + 1)

                    for k in range(NB):
                        i = NB - 1 - k
                        if k:
                            invert(i + 1, n, k - 1)
                            keep_turned_groups(dve, 1, i + 1, n, turns, 0)
                        elif not first:
                            invert(0, n - 1, NB - 1)
                        maximum(i, n, k, 0)
                        if k == 0:
                            if not first:
                                keep_last(n - 1)
                            projections(GROUPS_OF_STEP[k][:1])
                        if k:
                            keep_turned_groups(dve, 1, i + 1, n, turns, 1)
                            turns += (i + 5) // 4
                        maximum(i, n, k, 1)
                        if k:
                            projections(GROUPS_OF_STEP[k][:1])
                        elif not first:
                            keep_output(0, pair - 1, n * NB - 1)
                        projections(GROUPS_OF_STEP[k][1:])
                        if k:
                            keep_output(i + 1, pair, n * NB + k - 1)
                        if extra:
                            extra[k]()

                def invert(i, n, k):
                    dve.wait_ge(exp_done, n * (2 * NB) + 2 * k + 2)
                    dve.reciprocal(row_inv[:, i, :], row_sum[:, i, :]).then_inc(inv_ready, 1)

                def keep_output(i, pair, step):
                    dve.wait_ge(pv_done, step + 1)
                    dve.tensor_tensor(outT[:, pair, i * P:(i + 1) * P], o_ps[:, 0:P], r_bc[i % 2][:],
                                      ALU.mult).then_inc(out_kept, 1)

                def keep_last(n):
                    for h in range(2):
                        keep_turned_groups(dve, 1, 0, n, LAST_TURN, h)

                def keep_input(b):
                    for c in range(2):
                        cols = slice(c * HALF, (c + 1) * HALF)
                        dve.wait_ge(xT_hi_done, b * 2 + c + 1)
                        dve.tensor_tensor(xT_lo[:, cols], tr[c][:], xT_hi[:, cols].bitcast(F32),
                                          ALU.subtract).then_inc(xT_lo_done, 1)
                    for k in range(GROUPS):
                        keep_low_part(0, k, b * PAIRS)

                def finish_pairs(b):
                    invert(0, b * PAIRS + PAIRS - 1, NB - 1)
                    keep_last(b * PAIRS + PAIRS - 1)
                    keep_output(0, PAIRS - 1, b * (PAIRS * NB) + PAIRS * NB - 1)

                def normalized(b, chain, count):
                    dve.wait_ge(x_loaded, 3 * 16)
                    return layernorm_parts(dve, chain, lambda blk: g.x[:, b * NB + blk, :],
                                           lambda blk: x_norm[:, blk, :], norm, count)

                def add_bias(b):
                    for c in range(2):
                        dve.wait_ge(y_done, b * 2 + c + 1)
                        src = scores[0][:, c * HALF:(c + 1) * HALF].rearrange("p (t n) -> p t n", t=4)
                        dve.tensor_tensor(y[:, 4 * c:4 * c + 4, :], src, b_u[:].unsqueeze(1).to_broadcast([P, 4, D]),
                                          ALU.add).then_inc(y_used, 1)
                    dve.wait_ge(y_used, b * 2 + 2)

                def finish_batch(b, chain, count):
                    y_of = lambda blk: y[:, blk, :]
                    x_all = g.x[:, ds(b * NB, NB), :]

                    def residual():
                        chain.settle()
                        chain.did(dve.tensor_tensor(x_all, x_all, y[:], ALU.add))
                        chain.settle()

                    return layernorm_parts(dve, chain, y_of, y_of, norm, count)[:-1] + [residual]

                keep_input(0)
                first_pair(attend, 0)
                with dve.Fori(0, BATCH - 1) as b:
                    chain = Chain(dve, norm.chain, b * CHAIN + NORM_STEPS)
                    other_pairs(dve, attend, b, normalized(b + 1, chain, b * 2 + 1))
                    finish_pairs(b)
                    keep_input(b + 1)
                    add_bias(b)
                    first_pair(attend, b + 1, finish_batch(b, chain, b * 2 + 2))
                    assert chain.n == CHAIN
                chain = Chain(dve, norm.chain, (BATCH - 1) * CHAIN + NORM_STEPS)
                other_pairs(dve, attend, BATCH - 1)
                finish_pairs(BATCH - 1)
                add_bias(BATCH - 1)
                for part in finish_batch(BATCH - 1, chain, BATCH * 2 - 1):
                    part()

        nc.clear_and_free_semaphores(sems)
        nc.all_engine_barrier()


E_ROUTED, E_SHARED = 8, 2
EXPERTS = E_ROUTED + E_SHARED
HID = 256
HB = HID // P
CHUNKS = NBLK * P // HALF
TOP = 8


def mixture_layer0(nc, g):
    with ExitStack() as ctx:
        def sb(name, shape, dt=F32):
            return ctx.enter_context(nc.sbuf_tensor("m_" + name, shape, dt))

        def sem(name):
            return ctx.enter_context(nc.semaphore("m_" + name))

        w12 = sb("w12", [P, EXPERTS, 2, HID])
        w3 = sb("w3", [P, EXPERTS, HB, D])
        w_hl = [sb(f"w_hl{i}", [P, 2, 2, HID], F32R) for i in range(2)]
        b12 = sb("b12", [P, 2, EXPERTS, HB])
        b3 = sb("b3", [EXPERTS, D])
        gate_hl = sb("gate_hl", [P, 2, E_ROUTED], F32R)
        gate_w = sb("gate_w", [P, E_ROUTED])
        gate_b = sb("gate_b", [E_ROUTED, 1])
        iota = sb("iota", [P, E_ROUTED])
        x_norm = sb("x_norm", [P, NB, D])
        xT_hi = sb("xT_hi", [P, NBLK * P], F32R)
        xT_lo = sb("xT_lo", [P, NBLK * P], F32R)
        acc = sb("acc", [P, NBLK, D])
        gates = sb("gates", [P, NBLK, EXPERTS])
        norm = NormTiles(ctx, nc, "m_norm")

        loaded, prepared = sem("loaded"), sem("prepared")
        lg_kept, small_loaded = sem("lg_kept"), sem("small_loaded")
        xT_done, xT_hi_done, xT_lo_done = sem("xT_done"), sem("xT_hi_done"), sem("xT_lo_done")
        lg_done, lgT_kept, turned, gexp_ready, gexp_done = (sem(n) for n in (
            "lg_done", "lgT_kept", "turned", "gexp_ready", "gexp_done"))
        gates_turned, gatesT_kept, b3_done, b3_kept = (sem(n) for n in (
            "gates_turned", "gatesT_kept", "b3_done", "b3_kept"))
        w_free, w_hi_done, w_split = sem("w_free"), sem("w_hi_done"), sem("w_split")
        up_done, silu_done, glu_done = sem("up_done"), sem("silu_done"), sem("glu_done")
        down_done, weighed, added = sem("down_done"), sem("weighed"), sem("added")

        with ExitStack() as pctx:
            def psb(name, shape, dt=F32):
                return pctx.enter_context(nc.sbuf_tensor("m_" + name, shape, dt))

            lgT = psb("lgT", [E_ROUTED, SEQ])
            lg = psb("lg", [P, NBLK, E_ROUTED])
            top = psb("top", [P, NBLK, TOP])
            idx = psb("idx", [P, NBLK, TOP], U32)
            idx_f = psb("idx_f", [P, NBLK, 2])
            diff = psb("diff", [P, NBLK, E_ROUTED + 1])
            g_exp = psb("g_exp", [P, NBLK, E_ROUTED + 1])
            g_sum = psb("g_sum", [P, NBLK])
            weight = psb("weight", [P, NBLK, 2])
            hot = [psb(f"hot{i}", [P, NBLK, E_ROUTED]) for i in range(2)]
            gatesT = [psb(f"gatesT{i}", [EXPERTS, SEQ]) for i in range(2)]
            tr = [pctx.enter_context(nc.psum_tensor(f"m_tr{i}", [P, HALF], F32)) for i in range(2)]
            lg_ps = pctx.enter_context(nc.psum_tensor("m_lg_ps", [EXPERTS, SEQ], F32))
            lgt_ps = pctx.enter_context(nc.psum_tensor("m_lgt_ps", [P, HALF], F32))
            gt_ps = [pctx.enter_context(nc.psum_tensor("m_gt_ps", [EXPERTS, SEQ], F32)), lg_ps]

            NORMS = BATCH * NORM_STEPS
            GATES = 2 * NBLK + 10

            with nc.Block() as block:
                @block.sync
                def _(sp):
                    small = ((gate_w[:], g.inputs["L0_ffn_gate_w"]),
                             (gate_b[:], g.inputs["L0_ffn_gate_b"].rearrange("(e a) -> e a", a=1)),
                             (iota[:], g.inputs["c_iota"].partition_broadcast(P)),
                             (b3[0:E_ROUTED, :], g.inputs["L0_ffn_rb3"]), (b3[E_ROUTED:EXPERTS, :], g.inputs["L0_ffn_sb3"]))
                    for out, src in small:
                        sp.dma_start(out, src).then_inc(small_loaded, 16)
                    with nc.allow_non_contiguous_dma(reason="biases, one value per partition"):
                        for e0, n, letter in ((0, E_ROUTED, "r"), (E_ROUTED, E_SHARED, "s")):
                            for j in range(2):
                                src = g.inputs[f"L0_ffn_{letter}b{j + 1}"].rearrange("e (h p) -> p (e h)", p=P)
                                sp.dma_start(b12[:, j, e0:e0 + n, :].rearrange("p e h -> p (e h)"),
                                             src).then_inc(loaded, 16)
                                sp.dma_start(w12[:, e0:e0 + n, j, :], g.inputs[f"L0_ffn_{letter}w{j + 1}"]
                                             .rearrange("e p n -> p e n")).then_inc(loaded, 16)
                            for h in range(HB):
                                sp.dma_start(w3[:, e0:e0 + n, h, :], g.inputs[f"L0_ffn_{letter}w3"]
                                             [:, h * P:(h + 1) * P, :].rearrange("e p n -> p e n")).then_inc(loaded, 16)
                    sp.wait_ge(loaded, 12 * 16)

                @block.gpsimd
                def _(pool):
                    pool.memset(gates[:, :, E_ROUTED:EXPERTS], 1.0 / E_SHARED).then_inc(prepared, 1)
                    with pool.Fori(0, BATCH) as n:
                        inverse_root(pool, norm, g.minus_half[:, 0:NB], n)

                @block.tensor
                def _(pe):
                    with pe.Fori(0, BATCH) as b:
                        pe.wait_ge(norm.chain, b * NORM_STEPS + NORM_STEPS)
                        for c in range(2):
                            for t in range(4):
                                last = pe.transpose(tr[c][:, t * P:(t + 1) * P], x_norm[:, c * 4 + t, :], g.ident[:])
                            last.then_inc(xT_done, 1)
                        pe.wait_ge(prepared, 3)
                        for c in range(2):
                            pe.wait_ge(xT_lo_done, b * 2 + c + 1)
                            cols = ds(b * SEQ + c * HALF, HALF)
                            todo = split_passes((gate_hl[:, 0, :], gate_hl[:, 1, :]), (xT_hi[:, cols], xT_lo[:, cols]))
                            for n, (a, r) in enumerate(todo):
                                last = pe.matmul(lg_ps[0:E_ROUTED, c * HALF:(c + 1) * HALF], a, r, start=n == 0, stop=n == 2)
                        last.then_inc(lg_done, 1)
                        pe.wait_ge(lgT_kept, b + 1)
                        for t in range(NB):
                            last = pe.matmul(lgt_ps[:, t * E_ROUTED:(t + 1) * E_ROUTED], lgT[:, t * P:(t + 1) * P],
                                             g.ident[0:E_ROUTED, 0:E_ROUTED], start=True, stop=True)
                        last.then_inc(turned, 1)
                    pe.wait_ge(norm.chain, NORMS + GATES)
                    for b in range(BATCH):
                        for t in range(NB):
                            last = pe.transpose(gt_ps[b % 2][:, t * P:(t + 1) * P], gates[:, b * NB + t, :], g.ident[:])
                        last.then_inc(gates_turned, 1)
                        pe.wait_ge(gatesT_kept, b + 1)
                        if b:
                            pe.wait_ge(b3_kept, b * 2)
                        for c in range(2):
                            for t in range(4):
                                blk = c * 4 + t
                                last = pe.matmul(tr[c][:, t * P:(t + 1) * P], gatesT[b % 2][:, blk * P:(blk + 1) * P],
                                                 b3[:], start=True, stop=True)
                            last.then_inc(b3_done, 1)

                @block.scalar
                def _(act):
                    act.wait_ge(small_loaded, 5 * 16)
                    act.activation(gate_hl[:, 0, :], gate_w[:], ACT.Copy).then_inc(prepared, 1)
                    with act.Fori(0, BATCH) as b:
                        for c in range(2):
                            act.wait_ge(xT_done, b * 2 + c + 1)
                            act.activation(xT_hi[:, ds(b * SEQ + c * HALF, HALF)], tr[c][:],
                                           ACT.Copy).then_inc(xT_hi_done, 1)
                        act.wait_ge(lg_done, b + 1)
                        act.activation(lgT[:], lg_ps[0:E_ROUTED, :], ACT.Identity, bias=gate_b[:]).then_inc(lgT_kept, 1)
                        act.wait_ge(turned, b + 1)
                        act.activation(lg[:, ds(b * NB, NB), :], lgt_ps[:, 0:NB * E_ROUTED].rearrange(
                            "p (t e) -> p t e", t=NB), ACT.Copy).then_inc(lg_kept, 1)
                    act.wait_ge(gexp_ready, 1)
                    act.activation(g_exp[:], diff[:], ACT.Exp).then_inc(gexp_done, 1)
                    for b in range(BATCH):
                        act.wait_ge(gates_turned, b + 1)
                        act.activation(gatesT[b % 2][:], gt_ps[b % 2][:], ACT.Copy).then_inc(gatesT_kept, 1)

                @block.vector
                def _(dve):
                    dve.wait_ge(prepared, 2)
                    dve.tensor_tensor(gate_hl[:, 1, :], gate_w[:], gate_hl[:, 0, :].bitcast(F32),
                                      ALU.subtract).then_inc(prepared, 1)
                    with dve.Fori(0, BATCH) as b:
                        chain = Chain(dve, norm.chain, b * NORM_STEPS)
                        layernorm(dve, chain, lambda blk: g.x[:, b * NB + blk, :], lambda blk: x_norm[:, blk, :], norm, b)
                        for c in range(2):
                            cols = ds(b * SEQ + c * HALF, HALF)
                            dve.wait_ge(xT_hi_done, b * 2 + c + 1)
                            dve.tensor_tensor(xT_lo[:, cols], tr[c][:], xT_hi[:, cols].bitcast(F32),
                                              ALU.subtract).then_inc(xT_lo_done, 1)
                    chain = Chain(dve, norm.chain, NORMS)
                    dve.wait_ge(lg_kept, BATCH)
                    for t in range(NBLK):
                        chain.did(dve.max(top[:, t, :], lg[:, t, :]))
                    chain.settle()
                    largest = top[:, :, 0:1]
                    chain.did(dve.tensor_tensor(diff[:, :, 0:E_ROUTED], lg[:],
                                                largest.to_broadcast([P, NBLK, E_ROUTED]), ALU.subtract))
                    dve.tensor_tensor(diff[:, :, E_ROUTED:], top[:, :, 1:2], largest, ALU.subtract
                                      ).then_inc(gexp_ready, 1)
                    for t in range(NBLK):
                        chain.did(dve.max_index(idx[:, t, :], top[:, t, :], lg[:, t, :]))
                    chain.settle()
                    chain.did(dve.tensor_copy(idx_f[:], idx[:, :, 0:2]))
                    dve.wait_ge(gexp_done, 1)
                    chain.did(dve.tensor_reduce(g_sum[:], g_exp[:, :, 0:E_ROUTED], AX.X, ALU.add))
                    chain.settle()
                    chain.did(dve.reciprocal(weight[:, :, 0], g_sum[:]))
                    for j in range(2):
                        chain.did(dve.tensor_tensor(hot[j][:], iota[:].unsqueeze(1).to_broadcast([P, NBLK, E_ROUTED]),
                                                    idx_f[:, :, j:j + 1].to_broadcast([P, NBLK, E_ROUTED]), ALU.is_equal))
                    chain.settle()
                    chain.did(dve.tensor_tensor(weight[:, :, 1:2], weight[:, :, 0:1], g_exp[:, :, E_ROUTED:], ALU.mult))
                    chain.settle()
                    for j in range(2):
                        chain.did(dve.tensor_tensor(hot[j][:], hot[j][:],
                                                    weight[:, :, j:j + 1].to_broadcast([P, NBLK, E_ROUTED]), ALU.mult))
                    chain.settle()
                    chain.did(dve.tensor_tensor(gates[:, :, 0:E_ROUTED], hot[0][:], hot[1][:], ALU.add))
                    assert chain.n == GATES, chain.n
                    for b in range(BATCH):
                        for c in range(2):
                            dve.wait_ge(b3_done, b * 2 + c + 1)
                            blk = b * NB + c * 4
                            dve.tensor_copy(acc[:, blk:blk + 4, :],
                                            tr[c][:].rearrange("p (t n) -> p t n", t=4)).then_inc(b3_kept, 1)

        with ExitStack() as ectx:
            def esb(name, shape, dt=F32):
                return ectx.enter_context(nc.sbuf_tensor("m_" + name, shape, dt))

            silu = [esb(f"silu{i}", [P, HALF]) for i in range(2 * HB)]
            glu = [[esb(f"glu{i}{h}", [P, HALF]) for h in range(HB)] for i in range(2)]
            bias = [esb(f"bias{i}", [P, 2, HB]) for i in range(2)]
            taken = esb("taken", [P, 1])
            part = [esb(f"part{i}", [P, 4, D]) for i in range(2)]
            up = [[ectx.enter_context(nc.psum_tensor(f"m_up{i}{j}", [P, HALF], F32)) for j in range(2)]
                  for i in range(3)]
            up_of = (0, 1, 2, 0)
            down = [ectx.enter_context(nc.psum_tensor(f"m_down{i}", [P, HALF], F32)) for i in range(2)]

            def experts(eng, run):
                with eng.Fori(0, EXPERTS // 2 - 1) as q:
                    for par in range(2):
                        run(par, q, True)
                for par in range(2):
                    run(par, EXPERTS // 2 - 1, par == 0)

            assert CHUNKS // 2 == BATCH
            SPREAD = (0, 3, 5, 6, 7, 8, 9)

            def chunk_pairs(eng, par, q, run):
                with eng.Fori(0, CHUNKS // 2) as t:
                    run(t, (q * 2 + par) * CHUNKS + t * 2)

            with nc.Block() as block:
                @block.gpsimd
                def _(pool):
                    def split_hi(par, e):
                        pool.tensor_copy(w_hl[par][:, 0], w12[:, e]).then_inc(w_hi_done, 1)
                        pool.tensor_copy(bias[par][:], b12[:, :, e, :]).then_inc(w_hi_done, 1)

                    def expert(par, q, more):
                        if more:
                            pool.wait_ge(glu_done, (q * 2 + par) * (CHUNKS * HB))
                            pool.tensor_tensor(taken[:], norm.mean[:, 0:1], norm.mean[:, 0:1], ALU.add
                                               ).then_inc(w_free, 1)
                            split_hi(1 - par, q * 2 + par + 1)

                    split_hi(0, 0)
                    experts(pool, expert)
                    with pool.Fori(0, BATCH) as n:
                        inverse_root(pool, norm, g.minus_half[:, 0:NB], n + BATCH)

                @block.tensor
                def _(pe):
                    def expert(par, q, more):
                        e = q * 2 + par

                        def chunks(t, before):
                            pe.wait_ge(w_split, e + 1)

                            def raise_(c, h):
                                cols = ds(t * (2 * HALF) + c * HALF, HALF)
                                unit = c * HB + h
                                pe.wait_ge(glu_done, before * HB + (1 if unit == 3 else 0))
                                for j in range(2):
                                    w = [w_hl[par][:, s, j, h * P:(h + 1) * P] for s in range(2)]
                                    todo = split_passes(w, (xT_hi[:, cols], xT_lo[:, cols]))
                                    for n, (a, r) in enumerate(todo):
                                        last = pe.matmul(up[up_of[unit]][j][:], a, r, start=n == 0, stop=n == 2)
                                last.then_inc(up_done, 1)

                            def lower(c):
                                n = before + c
                                pe.wait_ge(weighed, before)
                                for h in range(HB):
                                    pe.wait_ge(glu_done, n * HB + h + 1)
                                    for b in range(4):
                                        last = pe.matmul(down[c][:, b * P:(b + 1) * P], glu[c][h][:, b * P:(b + 1) * P],
                                                         w3[:, e, h, :], start=h == 0 and b == 0, stop=h == HB - 1,
                                                         skip_group_check=True)
                                last.then_inc(down_done, 1)

                            raise_(0, 0)
                            raise_(0, 1)
                            raise_(1, 0)
                            raise_(1, 1)
                            lower(0)
                            lower(1)

                        chunk_pairs(pe, par, q, chunks)

                    experts(pe, expert)

                @block.scalar
                def _(act):
                    def expert(par, q, more):
                        def chunks(t, before):
                            for u in range(2 * HB):
                                h = u % HB
                                act.wait_ge(up_done, before * HB + u + 1)
                                act.activation(silu[u][:], up[up_of[u]][0][:], ACT.Silu,
                                               bias=bias[par][:, 0, h:h + 1]).then_inc(silu_done, 1)

                        chunk_pairs(act, par, q, chunks)

                    experts(act, expert)

                @block.vector
                def _(dve):
                    def expert(par, q, more):
                        e = q * 2 + par

                        def chunks(t, before, ends=()):
                            def gate_up(c, h):
                                unit = c * HB + h
                                dve.wait_ge(silu_done, before * HB + unit + 1)
                                dve.scalar_tensor_tensor(glu[c][h][:], up[up_of[unit]][1][:], bias[par][:, 1, h:h + 1],
                                                         silu[unit][:],
                                                         ALU.add, ALU.mult).then_inc(glu_done, 1)

                            def weigh(c):
                                dve.wait_ge(down_done, before + c + 1)
                                dve.wait_ge(added, before)
                                dve.tensor_tensor(part[c][:], down[c][:].rearrange("p (t n) -> p t n", t=4),
                                                  gates[:, ds(t * 8 + c * 4, 4), e].unsqueeze(2).to_broadcast([P, 4, D]),
                                                  ALU.mult).then_inc(weighed, 1)
                                sums = acc[:, ds(t * 8 + c * 4, 4), :]
                                dve.wait_ge(weighed, before + c + 1)
                                dve.tensor_tensor(sums, sums, part[c][:], ALU.add).then_inc(added, 1)

                            steps = [lambda: gate_up(0, 0), lambda: gate_up(0, 1), lambda: gate_up(1, 0),
                                     lambda: gate_up(1, 1), lambda: weigh(0), lambda: weigh(1)]
                            for n, step in enumerate(steps):
                                step()
                                for piece in ends[SPREAD[n]:SPREAD[n + 1]]:
                                    piece()

                        if more:
                            split_lo(1 - par, e + 1)
                            chunk_pairs(dve, par, q, chunks)
                        else:
                            before = e * CHUNKS
                            for t in range(BATCH):
                                chunks(t, before + 2 * t, residual(t - 1, before + 2 * t) if t else ())
                            for piece in residual(BATCH - 1, before + CHUNKS):
                                piece()

                    def residual(t, chunks_added):
                        chain = Chain(dve, norm.chain, NORMS + GATES + t * (NORM_STEPS + 1))
                        y_of = lambda blk: acc[:, t * NB + blk, :]

                        def add():
                            chain.settle()
                            batch = g.x[:, t * NB:(t + 1) * NB, :]
                            chain.did(dve.tensor_tensor(batch, batch, acc[:, t * NB:(t + 1) * NB, :], ALU.add))
                            chain.settle()

                        parts = layernorm_parts(dve, chain, y_of, y_of, norm, t + BATCH)[:-1] + [add]
                        return [lambda: dve.wait_ge(added, chunks_added)] + parts

                    def split_lo(par, e):
                        dve.wait_ge(w_hi_done, e * 2 + 2)
                        dve.tensor_tensor(w_hl[par][:, 1], w12[:, e], w_hl[par][:, 0].bitcast(F32),
                                          ALU.subtract).then_inc(w_split, 1)

                    split_lo(0, 0)
                    experts(dve, expert)


HEADS, KV, HD = 16, 4, 8
GQ = HEADS // KV
LAT = 32
WINDOW = 32
QK = (HEADS + KV) * HD
SLOT = 32
REPS = SLOT // HD
LOCAL_W = P + WINDOW
RMS_EPS = 1e-6
STEPS = KV * NB


def attention_layer1(nc, g, local):
    tag = "l_" if local else "g_"
    with ExitStack() as ctx:
        def sb(name, shape, dt=F32):
            return ctx.enter_context(nc.sbuf_tensor(tag + name, shape, dt))

        def sem(name):
            return ctx.enter_context(nc.semaphore(tag + name))

        w_in = sb("w_in", [P, 192])
        w_up = sb("w_up", [LAT, 2 * KV * HD])
        w_o = sb("w_o", [P, D])
        norm_w = sb("norm_w", [P, 1])
        cos, sin = sb("cos", [P, NB, HD // 2]), sb("sin", [P, NB, HD // 2])
        normed = sb("normed", [P, NB, D])
        normedT = sb("normedT", [P, SEQ])
        latT = sb("latT", [LAT, SEQ])
        qk = sb("qk", [P, NB, QK])
        squares = sb("squares", [P, NB, QK])
        part = [sb(f"part{i}", [P, NB * QK // 2]) for i in range(4)]
        turned = sb("turned", [P, NB, QK])
        ssq, rs = sb("ssq", [P, NB * (HEADS + KV)]), sb("rs", [P, NB * (HEADS + KV)])
        newton = sb("newton", [P, NB * (HEADS + KV)])
        ss_h, rs_h = sb("ss_h", [P, NB]), sb("rs_h", [P, NB])
        q_slots = [sb(f"q_slots{j}", [P, NB, P], F32R) for j in range(GQ)]
        k_slots = sb("k_slots", [P, NB, P], F32R)
        v_next = sb("v_next", [P, NB, KV * HD])
        values = sb("values", [P, NB, KV, SLOT])
        qT = [sb(f"qT{j}", [P, SEQ], F32R) for j in range(GQ)]
        kT = [sb(f"kT{h}", [P, SEQ], F32R) for h in range(KV)]
        PW = LOCAL_W if local else SEQ
        probsT = [sb(f"probsT{i}", [P, GQ, PW]) for i in range(2)]
        outT = [sb(f"outT{i}", [P, SEQ]) for i in range(2)]
        inv = sb("inv", [P, NB, GQ])
        att = sb("att", [P, NB, D])
        attT = sb("attT", [P, SEQ])

        s_ps = [ctx.enter_context(nc.psum_tensor(f"{tag}s_ps{i}", [P, SEQ], F32)) for i in range(2)]
        o_ps = ctx.enter_context(nc.psum_tensor(f"{tag}o_ps", [P, SEQ], F32))
        x_ps = ctx.enter_context(nc.psum_tensor(f"{tag}x_ps", [P, SEQ], F32))

        loaded, scaled, zeroed = sem("loaded"), sem("scaled"), sem("zeroed")
        chain, var_ready, rs_ready = sem("chain"), sem("var_ready"), sem("rs_ready")
        normedT_done, normedT_kept, lat_done, lat_kept = (sem(n) for n in (
            "normedT_done", "normedT_kept", "lat_done", "lat_kept"))
        qkv_done, qk_kept, v_kept, squared = sem("qkv_done"), sem("qk_kept"), sem("v_kept"), sem("squared")
        qk_var, qk_root = sem("qk_var"), sem("qk_root")
        half_rot, q_hi, k_hi = sem("half_rot"), sem("q_hi"), sem("k_hi")
        qk_turned, turned_kept = sem("qk_turned"), [sem("turned_kept_act"), sem("turned_kept_dve")]
        scored, exp_done, pv_done, o_kept = sem("scored"), sem("exp_done"), sem("pv_done"), sem("o_kept")
        back_done, att_kept, attT_done, attT_kept, out_done = (sem(n) for n in (
            "back_done", "att_kept", "attT_done", "attT_kept", "out_done"))

        names = {False: ("g_wq", "g_kv_down", "g_wo", "norm1_w", "c_rope_g"),
                 True: ("l_wq", "l_wk", "l_wo", "norm2_w", "c_rope_l")}[local]
        wq, wk, wo, nw = (g.inputs[f"L1_attn_{n}"] for n in names[:4])
        rope = g.inputs[names[4]]
        CHAIN_NORMED, CHAIN_TURNED = 3, 13
        CHAIN_PREPARED = CHAIN_TURNED + 1 + GQ
        CHAIN = CHAIN_PREPARED + KV * GQ + 1
        CHAIN_LOW_3 = CHAIN_TURNED + (KV - 1) * GQ
        TURN_BACK = 1 if local else 0
        TURN_INPUT, PROJECT, ROOT = (5 if local else 3), (11, 13), 24

        with nc.Block() as block:
            @block.sync
            def _(sp):
                sp.dma_start(w_in[:, 0:D], wq).then_inc(loaded, 16)
                sp.dma_start(w_in[:, D:D + 32], wk).then_inc(loaded, 16)
                if local:
                    sp.dma_start(w_in[:, D + 32:D + 64], g.inputs["L1_attn_l_wv"]).then_inc(loaded, 16)
                    sp.dma_start(w_up[:, 0:32], g.inputs["L1_attn_g_k_up"]).then_inc(loaded, 16)
                else:
                    sp.dma_start(w_up[:, 0:32], g.inputs["L1_attn_g_k_up"]).then_inc(loaded, 16)
                    sp.dma_start(w_up[:, 32:64], g.inputs["L1_attn_g_v_up"]).then_inc(loaded, 16)
                sp.dma_start(w_o[:], wo).then_inc(loaded, 16)
                sp.dma_start(norm_w[:], nw.rearrange("(p a) -> p a", a=1)).then_inc(loaded, 16)
                sp.dma_start(cos[:], rope[0].rearrange("(t p) n -> p t n", p=P)).then_inc(loaded, 16)
                sp.dma_start(sin[:], rope[1].rearrange("(t p) n -> p t n", p=P)).then_inc(loaded, 16)

            @block.gpsimd
            def _(pool):
                for j in range(GQ):
                    pool.memset(q_slots[j][:].bitcast(F32), 0.0)
                pool.memset(k_slots[:].bitcast(F32), 0.0)
                pool.memset(values[:], 0.0).then_inc(zeroed, 1)
                pool.wait_ge(zeroed, 1)
                pool.memset(values[:, :, :, HD:HD + 1], 1.0)

            @block.vector
            def _(dve):
                for h in range(KV):
                    dve.memset(kT[h][:].bitcast(F32), 0.0)
                dve.wait_ge(loaded, 8 * 16)
                width = 192 if local else 160
                dve.tensor_scalar(w_in[:, 0:width], w_in[:, 0:width], norm_w[:], None, ALU.mult)

        heads = QK // HD
        as_pairs = lambda t: t[:].rearrange("p t (h n two) -> p t h n two", h=heads, two=2)
        even, odd = (as_pairs(qk)[:, :, :, :, c] for c in range(2))
        t_even, t_odd = (as_pairs(turned)[:, :, :, :, c] for c in range(2))
        parts = [p[:].rearrange("p (t h n) -> p t h n", t=NB, h=heads) for p in part]
        spread = lambda t: t[:].unsqueeze(2).to_broadcast([P, NB, heads, HD // 2])
        slots = lambda t: t[:].rearrange("p t (s r d) -> p t s r d", s=KV, r=REPS)
        q_of = lambda j: turned[:, :, 0:HEADS * HD].rearrange("p t (s j d) -> p t s j d", s=KV, j=GQ)[:, :, :, j, :]
        k_of = turned[:, :, HEADS * HD:QK].rearrange("p t (s d) -> p t s d", s=KV)

        def query_cols(kb):
            lo, hi = kb * P, min(kb * P + LOCAL_W, SEQ) if local else SEQ
            starts = [lo] + ([HALF] if lo < HALF < hi else [])
            return [(a, min(hi, a // HALF * HALF + HALF)) for a in starts]

        def heads_at_once(kb):
            width = query_cols(kb)[-1][1] - kb * P
            return max(n for n in (1, 2, GQ) if n * 256 * -(-width // 256) <= SEQ)

        def units_before(n):
            a_head = [GQ // heads_at_once(kb) for kb in range(NB)]
            return n // NB * sum(a_head) + sum(a_head[:n % NB])

        UNITS = units_before(STEPS)

        def batches(eng, prepare, run):
            prepare(0)
            run(0, True, False)
            with eng.Fori(0, BATCH - 2) as i:
                run(i + 1, False, False)
            run(BATCH - 1, False, True)

        with nc.Block() as block:
            @block.gpsimd
            def _(pool):
                def prepare(x):
                    if not local:
                        inverse_root(pool, g.norm1, g.minus_half[:, 0:NB], x)
                    pool.wait_ge(var_ready, x + 1)
                    pool.tensor_tensor(rs_h[:], ss_h[:], g.minus_half[:, 0:NB], ALU.pow).then_inc(rs_ready, 1)
                    pool.wait_ge(qk_kept, x * 2 + 2)
                    pool.tensor_tensor(parts[2], even, spread(sin), ALU.mult).then_inc(half_rot, 1)
                    pool.tensor_tensor(parts[3], odd, spread(cos), ALU.mult).then_inc(half_rot, 1)

                def attend(b, first, last):
                    if not last:
                        prepare(b + 1)
                    if local and not first:
                        inverse_root(pool, g.norm1, g.minus_half[:, 0:NB], b - 1 + BATCH)

                batches(pool, prepare, attend)
                if local:
                    inverse_root(pool, g.norm1, g.minus_half[:, 0:NB], 2 * BATCH - 1)

            @block.tensor
            def _(pe):
                def turn_input(x, chained):
                    pe.wait_ge(chain, chained)
                    for blk in range(NB):
                        last = pe.transpose(x_ps[:, blk * P:(blk + 1) * P], normed[:, blk, :], g.ident[:])
                    last.then_inc(normedT_done, 1)

                def project_latent(x):
                    pe.wait_ge(normedT_kept, x + 1)
                    for c in range(2):
                        last = pe.matmul(x_ps[0:LAT, c * HALF:(c + 1) * HALF], w_in[:, D:D + LAT],
                                         normedT[:, c * HALF:(c + 1) * HALF], start=True, stop=True)
                    last.then_inc(lat_done, 1)

                def input_read(x):
                    if local:
                        pe.wait_ge(normedT_kept, x + 1)
                    else:
                        pe.wait_ge(lat_kept, x + 1)

                def projection_read(x, c):
                    pe.wait_ge(qk_kept, x * 2 + c + 1)
                    pe.wait_ge(v_kept, x * 2 + c + 1)

                def project(x, c):
                    input_read(x)
                    if c:
                        projection_read(x, 0)
                    for t in range(NB // 2):
                        blk = c * (NB // 2) + t
                        out = x_ps[:, t * 256:t * 256 + 192]
                        rows = slice(blk * P, (blk + 1) * P)
                        if local:
                            last = pe.matmul(out, normedT[:, rows], w_in[:], start=True, stop=True)
                        else:
                            pe.matmul(out[:, 0:D], normedT[:, rows], w_in[:, 0:D], start=True, stop=True)
                            last = pe.matmul(out[:, D:], latT[:, rows], w_up[:], start=True, stop=True)
                    last.then_inc(qkv_done, 1)

                def turn_qk(x, i, chained):
                    pe.wait_ge(chain, chained)
                    if i >= 2:
                        for eng in range(2):
                            pe.wait_ge(turned_kept[eng], x * (1 + GQ) + i - 1)
                    src = k_slots if i == 0 else q_slots[i - 1]
                    for blk in range(NB):
                        last = pe.transpose(s_ps[i % 2][:, blk * P:(blk + 1) * P], src[:, blk, :].bitcast(F32), g.ident[:])
                    last.then_inc(qk_turned, 1)

                def prepare(x):
                    turn_input(x, CHAIN_NORMED)
                    if not local:
                        project_latent(x)
                    project(x, 0)
                    project(x, 1)
                    projection_read(x, 1)
                    for i in range(1 + GQ):
                        turn_qk(x, i, CHAIN_TURNED + 1 + i)

                def attend(b, first, last_batch):
                    done = CHAIN_PREPARED + b * CHAIN

                    def score(n, unit):
                        h, kb = n // NB, n % NB
                        u = units_before(n) + unit
                        if u >= 2:
                            pe.wait_ge(exp_done, b * UNITS + u - 1)
                        together = heads_at_once(kb)
                        cols = query_cols(kb) if together == 1 else [(kb * P, query_cols(kb)[-1][1])]
                        for i in range(together):
                            off = i * (SEQ // together) - kb * P if together > 1 else 0
                            clears = together < GQ or i % 2 == 0
                            for a, e in cols:
                                pe.matmul(s_ps[u % 2][:, a + off:e + off], kT[h][:, kb * P:(kb + 1) * P],
                                          qT[unit * together + i][:, a:e], start=clears, stop=False,
                                          skip_group_check=True)
                            a = kb * P
                            width = cols[-1][1] - a if local else P
                            last = pe.matmul(s_ps[u % 2][:, a + off:a + off + width], g.ident_bf[:],
                                             (g.mask_window if local else g.mask_kq)[:, 0:width],
                                             start=False, stop=True, skip_group_check=True)
                        last.then_inc(scored, 1)

                    def weigh(n, chunks):
                        h, kb = n // NB, n % NB
                        cols = query_cols(kb)
                        for c in chunks:
                            if c >= len(cols):
                                continue
                            if c == 0:
                                pe.wait_ge(exp_done, b * UNITS + units_before(n + 1))
                            a, e = cols[c]
                            first = (kb == 0 and a == 0) or (a == HALF and (kb == 3 if local else kb == 0))
                            if first and h:
                                pe.wait_ge(o_kept, (b * KV + h) * 2 - (1 if a == 0 else 0))
                            elif first and a == 0:
                                pe.wait_ge(chain, done)
                            for j in range(GQ):
                                col = a - kb * P if local else a
                                last = pe.matmul(o_ps[j * SLOT:(j + 1) * SLOT, a:e], values[:, kb, h, :],
                                                 probsT[n % 2][:, j, col:col + e - a], start=first, stop=True,
                                                 skip_group_check=True)
                            if c == len(cols) - 1:
                                last.then_inc(pv_done, 1)

                    def turn_back(h):
                        pe.wait_ge(o_kept, (b * KV + h) * 2 + 2)
                        if h:
                            pe.wait_ge(att_kept, b * KV + h)
                        if h == 0 and not last_batch:
                            input_read(b + 1)
                        if h == 1 and not last_batch:
                            projection_read(b + 1, 1)
                        for blk in range(NB):
                            last = pe.transpose(x_ps[:, blk * P:(blk + 1) * P], outT[h % 2][:, blk * P:(blk + 1) * P],
                                                g.ident[:])
                        last.then_inc(back_done, 1)

                    def project_next(c):
                        pe.wait_ge(att_kept, b * KV + 1)
                        project(b + 1, c)

                    pieces = {} if last_batch else {
                        TURN_INPUT: lambda: turn_input(b + 1, done + CHAIN_NORMED),
                        PROJECT[0]: lambda: project_next(0), PROJECT[1]: lambda: project_next(1)}
                    if not (last_batch or local):
                        pieces[TURN_INPUT + 1] = lambda: project_latent(b + 1)
                    for eng in range(2):
                        pe.wait_ge(turned_kept[eng], (b + 1) * (1 + GQ))
                    for n in range(STEPS):
                        units = GQ // heads_at_once(n % NB)
                        for unit in range(units):
                            score(n, unit)
                            if n and unit == (units - 1) // 2:
                                weigh(n - 1, (0,) if units > 1 else (0, 1))
                        if n and units > 1:
                            weigh(n - 1, (1,))
                        if n >= NB and n % NB == TURN_BACK:
                            turn_back(n // NB - 1)
                        if n in pieces:
                            pieces[n]()
                    def turn_next(*which):
                        for i in which if not last_batch else ():
                            turn_qk(b + 1, i, done + (CHAIN_LOW_3 if i < 3 else CHAIN_LOW_3 + GQ) + i + 1)

                    weigh(STEPS - 1, (0, 1))
                    turn_back(KV - 1)
                    turn_next(0, 1)
                    pe.wait_ge(att_kept, b * KV + KV)
                    for blk in range(NB):
                        last = pe.transpose(x_ps[:, blk * P:(blk + 1) * P], att[:, blk, :], g.ident[:])
                    last.then_inc(attT_done, 1)
                    turn_next(2)
                    pe.wait_ge(attT_kept, b + 1)
                    for blk in range(NB):
                        last = pe.matmul(o_ps[:, blk * P:(blk + 1) * P], attT[:, blk * P:(blk + 1) * P], w_o[:],
                                         start=True, stop=True)
                    last.then_inc(out_done, 1)
                    turn_next(3, 4)

                batches(pe, prepare, attend)

            def keep_turned(eng, bank, x, which):
                cols = slice(bank * HALF, (bank + 1) * HALF)

                def keep(out, src):
                    return eng.tensor_copy(out, src) if bank else eng.activation(out, src, ACT.Copy)

                for i in which:
                    eng.wait_ge(qk_turned, x * (1 + GQ) + i + 1)
                    if i == 0:
                        for h in range(KV):
                            rows = slice(h * SLOT, (h + 1) * SLOT)
                            last = keep(kT[h][rows, cols], s_ps[0][rows, cols])
                    else:
                        last = keep(qT[i - 1][:, cols], s_ps[i % 2][:, cols])
                    last.then_inc(turned_kept[bank], 1)

            @block.scalar
            def _(act):
                def keep_input(x):
                    act.wait_ge(normedT_done, x + 1)
                    act.activation(normedT[:], x_ps[:], ACT.Copy).then_inc(normedT_kept, 1)

                def keep_latent(x):
                    act.wait_ge(lat_done, x + 1)
                    act.activation(latT[:], x_ps[0:LAT, :], ACT.Copy).then_inc(lat_kept, 1)

                def keep_qk(x, c):
                    act.wait_ge(qkv_done, x * 2 + c + 1)
                    src = x_ps[:].rearrange("p (t n) -> p t n", t=NB // 2)
                    act.activation(qk[:, 4 * c:4 * c + 4, :], src[:, :, 0:QK], ACT.Copy).then_inc(qk_kept, 1)

                def square(x):
                    act.wait_ge(qk_kept, x * 2 + 2)
                    act.activation(squares[:], qk[:], ACT.Square).then_inc(squared, 1)

                def root(x):
                    act.wait_ge(qk_var, x + 1)
                    act.activation(rs[:], ssq[:], ACT.Sqrt).then_inc(qk_root, 1)

                def high_parts(x, chained):
                    def k_part(r):
                        act.wait_ge(chain, chained)
                        act.activation(slots(k_slots)[:, :, :, r, :], k_of, ACT.Copy).then_inc(k_hi, 1)

                    def q_part(j, r):
                        act.activation(slots(q_slots[j])[:, :, :, r, :], q_of(j), ACT.Copy).then_inc(q_hi, 1)

                    return [*(lambda r=r: k_part(r) for r in range(2)),
                            *(lambda j=j, r=r: q_part(j, r) for j in range(GQ) for r in (0, 2))]

                def prepare(x):
                    keep_input(x)
                    if not local:
                        keep_latent(x)
                    keep_qk(x, 0)
                    keep_qk(x, 1)
                    square(x)
                    root(x)
                    for part in high_parts(x, CHAIN_TURNED):
                        part()
                    keep_turned(act, 0, x, range(1 + GQ))

                def attend(b, first, last):
                    highs = high_parts(b + 1, CHAIN_PREPARED + b * CHAIN + CHAIN_TURNED + 3 * GQ)
                    pieces = {}
                    if not last:
                        pieces = {TURN_INPUT + 1: lambda: keep_input(b + 1), PROJECT[0] + 1: lambda: keep_qk(b + 1, 0),
                                  PROJECT[1] + 1: lambda: keep_qk(b + 1, 1), PROJECT[1] + 2: lambda: square(b + 1),
                                  ROOT: lambda: root(b + 1)}
                        if not local:
                            pieces[TURN_INPUT + 2] = lambda: keep_latent(b + 1)
                    for n in range(STEPS):
                        kb = n % NB
                        together = heads_at_once(kb)
                        for unit in range(GQ // together):
                            u = units_before(n) + unit
                            act.wait_ge(scored, b * UNITS + u + 1)
                            if n >= 2 and unit == 0:
                                act.wait_ge(pv_done, b * STEPS + n - 1)
                            width = min(LOCAL_W if local else SEQ, SEQ - kb * P)
                            at = 0 if local else kb * P
                            out = probsT[n % 2][:, unit * together:(unit + 1) * together, at:at + width]
                            src = s_ps[u % 2][:, kb * P:SEQ].unsqueeze(1)
                            if together > 1:
                                src = s_ps[u % 2][:].rearrange("p (j n) -> p j n", j=together)[:, :, 0:width]
                            act.activation(out, src, ACT.Exp, scale=float(HD) ** -0.5).then_inc(exp_done, 1)
                        if n in pieces:
                            pieces[n]()
                        if not last:
                            for part in {STEPS - 2: highs[0:3], STEPS - 1: highs[3:]}.get(n, ()):
                                part()
                    if not last:
                        keep_turned(act, 0, b + 1, (0, 1))
                    act.wait_ge(attT_done, b + 1)
                    act.activation(attT[:], x_ps[:], ACT.Copy).then_inc(attT_kept, 1)
                    if not last:
                        keep_turned(act, 0, b + 1, (2, 3, 4))

                batches(act, prepare, attend)

            @block.vector
            def _(dve):
                def normalize(x, own):
                    hidden = g.hidden[:, ds(x * NB, NB), :]
                    if not local:
                        norm_chain = Chain(dve, g.norm1.chain, x * NORM_STEPS)
                        layernorm(dve, norm_chain, lambda blk: g.x[:, x * NB + blk, :],
                                  lambda blk: g.hidden[:, x * NB + blk, :], g.norm1, x)
                    own.did(dve.tensor_tensor(normed[:], hidden, hidden, ALU.mult))
                    own.settle()
                    own.did(dve.tensor_reduce(ss_h[:], normed[:], AX.X, ALU.add))
                    own.settle()
                    dve.tensor_scalar(ss_h[:], ss_h[:], 1.0 / D, RMS_EPS, ALU.mult, ALU.add).then_inc(var_ready, 1)
                    dve.wait_ge(rs_ready, x + 1)
                    own.did(dve.tensor_tensor(normed[:], hidden, rs_h[:].unsqueeze(2).to_broadcast([P, NB, D]), ALU.mult))

                def rotate(x, own):
                    for c in range(2):
                        dve.wait_ge(qk_kept, x * 2 + c + 1)
                        src = x_ps[:].rearrange("p (t n) -> p t n", t=NB // 2)[:, :, QK:192]
                        dve.tensor_copy(v_next[:, 4 * c:4 * c + 4, :], src).then_inc(v_kept, 1)
                    own.did(dve.tensor_tensor(parts[0], even, spread(cos), ALU.mult))
                    own.did(dve.tensor_tensor(parts[1], odd, spread(sin), ALU.mult))

                def sum_rotation(x, own):
                    dve.wait_ge(squared, x + 1)
                    own.did(dve.tensor_reduce(ssq[:], squares[:].rearrange("p t (h d) -> p (t h) d", d=HD), AX.X, ALU.add))
                    own.settle()
                    dve.tensor_scalar(ssq[:], ssq[:], 1.0 / HD, RMS_EPS, ALU.mult, ALU.add).then_inc(qk_var, 1)
                    own.did(dve.tensor_tensor(t_even, parts[0], parts[1], ALU.subtract))
                    dve.wait_ge(half_rot, x * 2 + 2)
                    own.did(dve.tensor_tensor(t_odd, parts[2], parts[3], ALU.add))

                def scale_heads(x, own):
                    dve.wait_ge(qk_root, x + 1)
                    own.did(dve.reciprocal(rs[:], rs[:]))
                    own.settle()
                    own.did(dve.tensor_tensor(newton[:], rs[:], rs[:], ALU.mult))
                    own.settle()
                    own.did(dve.scalar_tensor_tensor(newton[:], newton[:], -0.5, ssq[:], ALU.mult, ALU.mult))
                    own.settle()
                    own.did(dve.scalar_tensor_tensor(rs[:], newton[:], 1.5, rs[:], ALU.add, ALU.mult))
                    own.settle()
                    by_head = turned[:].rearrange("p t (h d) -> p (t h) d", d=HD)
                    own.did(dve.tensor_tensor(by_head, by_head, rs[:].unsqueeze(2).to_broadcast([P, NB * heads, HD]),
                                              ALU.mult))
                    own.settle()

                def low_parts(x, own, which):
                    for i in which:
                        if i == 0:
                            dve.wait_ge(k_hi, x * 2 + 2)
                            own.did(dve.tensor_tensor(slots(k_slots)[:, :, :, 2, :], k_of,
                                                      slots(k_slots)[:, :, :, 0, :].bitcast(F32), ALU.subtract))
                        else:
                            dve.wait_ge(q_hi, x * (2 * GQ) + 2 * i)
                            out = slots(q_slots[i - 1])
                            own.did(dve.tensor_tensor(out[:, :, :, 1, :], q_of(i - 1), out[:, :, :, 0, :].bitcast(F32),
                                                      ALU.subtract))

                def keep_values():
                    dve.tensor_copy(values[:, :, :, 0:HD], v_next[:].rearrange("p t (s d) -> p t s d", s=KV))

                def prepare(x):
                    own = Chain(dve, chain)
                    normalize(x, own)
                    assert own.n == CHAIN_NORMED
                    rotate(x, own)
                    sum_rotation(x, own)
                    scale_heads(x, own)
                    assert own.n == CHAIN_TURNED
                    low_parts(x, own, range(1 + GQ))
                    assert own.n == CHAIN_PREPARED
                    dve.wait_ge(v_kept, x * 2 + 2)
                    keep_values()
                    keep_turned(dve, 1, x, range(1 + GQ))

                def residual(x, count):
                    norm_chain = Chain(dve, g.norm1.chain, BATCH * NORM_STEPS + x * (NORM_STEPS + 1))
                    y_of = lambda blk: g.hidden[:, x * NB + blk, :]

                    def add():
                        norm_chain.settle()
                        batch = g.x[:, ds(x * NB, NB), :]
                        norm_chain.did(dve.tensor_tensor(batch, batch, g.hidden[:, ds(x * NB, NB), :], ALU.add))
                        norm_chain.settle()

                    return layernorm_parts(dve, norm_chain, y_of, y_of, g.norm1, count)[:-1] + [add]

                def attend(b, first, last):
                    own = Chain(dve, chain, CHAIN_PREPARED + b * CHAIN)
                    nexts = [rotate, sum_rotation, scale_heads,
                             lambda x, own: low_parts(x, own, range(3, 1 + GQ))]
                    ends = residual(b - 1, b - 1 + BATCH) if local and not first else []
                    ends_by_head = [ends[0:4], ends[4:5], ends[5:6], ends[6:]]
                    if not last:
                        normalize(b + 1, own)
                    for h in range(KV):
                        for c in range(2):
                            cols = slice(c * HALF, (c + 1) * HALF)
                            dve.wait_ge(pv_done, b * STEPS + h * NB + (c + 1) * NB // 2)
                            dve.tensor_copy(outT[h % 2][:, cols], o_ps[:, cols]).then_inc(o_kept, 1)
                        if h == KV - 1 and not last:
                            keep_values()
                            low_parts(b + 1, own, range(0, 3))
                        dve.wait_ge(back_done, b * KV + h + 1)
                        back = x_ps[:].rearrange("p (t j s) -> p t j s", t=NB, j=GQ)
                        own.did(dve.reciprocal(inv[:], back[:, :, :, HD]))
                        own.settle()
                        for j in range(GQ):
                            head = (h * GQ + j) * HD
                            ins = dve.tensor_tensor(att[:, :, head:head + HD], back[:, :, j, 0:HD],
                                                    inv[:, :, j:j + 1].to_broadcast([P, NB, HD]), ALU.mult)
                            if j < GQ - 1:
                                own.did(ins)
                        ins.then_inc(att_kept, 1)
                        if not last:
                            nexts[h](b + 1, own)
                            if h == KV - 1:
                                keep_turned(dve, 1, b + 1, (0, 1, 2))
                        for part in ends_by_head[h]:
                            part()
                    dve.wait_ge(out_done, b + 1)
                    hidden = g.hidden[:, ds(b * NB, NB), :]
                    own.did(dve.tensor_tensor(hidden, hidden, o_ps[:].rearrange("p (t n) -> p t n", t=NB), ALU.add))
                    own.settle()
                    assert last or own.n == CHAIN, own.n
                    if not last:
                        keep_turned(dve, 1, b + 1, (3, 4))

                batches(dve, prepare, attend)
                if local:
                    for part in residual(BATCH - 1, 2 * BATCH - 1):
                        part()


def layer1_attention(nc, g):
    with ExitStack() as ctx:
        g.hidden = ctx.enter_context(nc.sbuf_tensor("hidden", [P, NBLK, D], F32))
        g.norm1 = NormTiles(ctx, nc, "norm1")
        attention_layer1(nc, g, local=False)
        attention_layer1(nc, g, local=True)


SE, SS = 8, 64
SLOTS = SE * SS
SB = SLOTS // P
S_HID = 512
S_HB = S_HID // P
COLS = BATCH * SS
UNITS_A, UNITS_B = SB, NB // 2


def soft_mixture(nc, g, out):
    with ExitStack() as ctx:
        def sb(name, shape, dt=F32):
            return ctx.enter_context(nc.sbuf_tensor("s_" + name, shape, dt))

        def sem(name):
            return ctx.enter_context(nc.semaphore("s_" + name))

        w1 = sb("w1", [P, SE, S_HID])
        w2 = sb("w2", [P, SE, S_HB, D])
        b1 = sb("b1", [P, SE, S_HB])
        b2 = sb("b2", [P, SB, D])
        gamma, slot_gamma = sb("gamma", [P, D]), sb("slot_gamma", [P, D])
        slot_in = sb("slot_in", [P, SB, D])
        snT = [sb(f"snT{i}", [P, SLOTS], F32R) for i in range(2)]
        combine = sb("combine", [P, SB, NBLK * P])
        inv_c = sb("inv_c", [P, NBLK])
        slotsT = sb("slotsT", [P, SE, BATCH, SS])
        norm = NormTiles(ctx, nc, "s_norm")
        ss, rs = sb("ss", [P, NB]), sb("rs", [P, NB])

        loaded, chain, ss_ready, rs_ready = sem("loaded"), sem("chain"), sem("ss_ready"), sem("rs_ready")
        weights_loaded = sem("weights_loaded")
        turned, hi_done, lo_done = sem("turned"), sem("hi_done"), sem("lo_done")
        root = float(D) ** 0.5

        with ExitStack() as lctx:
            def lsb(name, shape, dt=F32):
                return lctx.enter_context(nc.sbuf_tensor("s_" + name, shape, dt))

            slots_n = lsb("slots_n", [P, SB, D])
            hidden, squares, xn = (lsb(n, [P, NB, D]) for n in ("hidden", "squares", "xn"))
            xT = [lsb(f"xT{i}", [P, SEQ], F32R) for i in range(2)]
            minus_max = lsb("minus_max", [P, UNITS_A + 2 * UNITS_B])
            sums, inv_d = lsb("sums", [P, UNITS_A + 2 * UNITS_B]), lsb("inv_d", [P, UNITS_A])
            exps = [lsb(f"exps{i}", [P, SEQ]) for i in range(2)]
            dispatch = lsb("dispatch", [P, NB, SLOTS])
            logits = [lctx.enter_context(nc.psum_tensor(f"s_logits{i}", [P, SEQ], F32)) for i in range(2)]
            tr = [lctx.enter_context(nc.psum_tensor(f"s_tr{i}", [P, SEQ], F32)) for i in range(2)]
            xT_hi_done, xT_lo_done, input_turned = sem("xT_hi_done"), sem("xT_lo_done"), sem("input_turned")
            lg_done, max_done, exp_done, scaled = sem("lg_done"), sem("max_done"), sem("exp_done"), sem("scaled")
            tr_done, slots_done = sem("tr_done"), sem("slots_done")
            read_act, read_dve = sem("read_act"), sem("read_dve")

            UNITS = UNITS_A + UNITS_B
            CHAIN_XN = NORM_STEPS + 2 + NB
            CHAIN = CHAIN_XN + UNITS_A + UNITS_B
            MIX_SLOTS = UNITS - 3

            def batches(eng, prepare, run):
                prepare(0)
                with eng.Fori(0, BATCH - 1) as b:
                    run(b, False)
                run(BATCH - 1, True)
            READS_ACT = UNITS + 1
            EXPS = UNITS_A + 2 * UNITS_B
            PARTS_AFTER = (0, 0, 0, 1, 2, 4, 5, 7, 10)
            exps_by = lambda u: u + 1 if u < UNITS_A else UNITS_A + 2 * (u - UNITS_A + 1)

            with nc.Block() as block:
                @block.sync
                def _(sp):
                    sp.dma_start(slot_in[:], g.inputs["L1_ffn_slot_embeds"].rearrange("(q e) s n -> (e s) q n", e=2)
                                 ).then_inc(loaded, 16)
                    for out, name in ((slot_gamma, "L1_ffn_slot_norm_gamma"), (gamma, "L1_ffn_norm_gamma")):
                        sp.dma_start(out[:], g.inputs[name].partition_broadcast(P)).then_inc(loaded, 16)
                    sp.dma_start(w1[:], g.inputs["L1_ffn_w1"].rearrange("e p n -> p e n")).then_inc(weights_loaded, 16)
                    for h in range(S_HB):
                        sp.dma_start(w2[:, :, h, :], g.inputs["L1_ffn_w2"][:, h * P:(h + 1) * P, :]
                                     .rearrange("e p n -> p e n")).then_inc(weights_loaded, 16)
                    with nc.allow_non_contiguous_dma(reason="biases, one value per partition"):
                        sp.dma_start(b1[:].rearrange("p e h -> p (e h)"),
                                     g.inputs["L1_ffn_b1"].rearrange("e (h p) -> p (e h)", p=P)).then_inc(weights_loaded, 16)
                    by_pair = g.inputs["L1_ffn_b2"].rearrange("(q e) n -> e q n", e=2)
                    for e in range(2):
                        sp.dma_start(b2[e * SS:(e + 1) * SS], by_pair[e].partition_broadcast(SS)
                                     ).then_inc(weights_loaded, 16)
                    sp.wait_ge(weights_loaded, 8 * 16)

                @block.gpsimd
                def _(pool):
                    pool.wait_ge(ss_ready, 1)
                    pool.tensor_tensor(rs[:, 0:SB], ss[:, 0:SB], g.minus_half[:, 0:SB], ALU.pow).then_inc(rs_ready, 1)
                    with pool.Fori(0, BATCH) as b:
                        inverse_root(pool, norm, g.minus_half[:, 0:NB], b)
                        pool.wait_ge(ss_ready, b + 2)
                        pool.tensor_tensor(rs[:], ss[:], g.minus_half[:, 0:NB], ALU.pow).then_inc(rs_ready, 1)

                @block.tensor
                def _(pe):
                    def turn_input(x, turns):
                        pe.wait_ge(norm.chain, CHAIN_XN + x * CHAIN)
                        if turns:
                            pe.wait_ge(read_dve, x * UNITS)
                            pe.wait_ge(read_act, x * READS_ACT)
                        for t in range(NB):
                            last = pe.transpose(tr[1][:, t * P:(t + 1) * P], xn[:, t, :], g.ident[:])
                        last.then_inc(input_turned, 1)

                    def batch(b, last_batch):
                        pe.wait_ge(xT_lo_done, b + 1)

                        def score(u):
                            if u >= 2:
                                pe.wait_ge(exp_done, b * EXPS + exps_by(u - 2))
                            for c in range(2):
                                if u < UNITS_A:
                                    a = [snT[i][:, u * P:(u + 1) * P] for i in range(2)]
                                    r = [xT[i][:, c * HALF:(c + 1) * HALF] for i in range(2)]
                                else:
                                    blk = (u - UNITS_A) * 2 + c
                                    a = [xT[i][:, blk * P:(blk + 1) * P] for i in range(2)]
                                    r = [snT[i][:] for i in range(2)]
                                for n, (l, m) in enumerate(split_passes(a, r)):
                                    last = pe.matmul(logits[u % 2][:, c * HALF:(c + 1) * HALF], l, m,
                                                     start=n == 0, stop=n == 2)
                            last.then_inc(lg_done, 1)

                        def turn(u):
                            if u < UNITS_A:
                                pe.wait_ge(scaled, b * UNITS_A + u + 1)
                            else:
                                pe.wait_ge(exp_done, b * EXPS + exps_by(u))
                            if u >= 2:
                                pe.wait_ge(read_dve, b * UNITS + u - 1)
                                pe.wait_ge(read_act, b * READS_ACT + (MIX_SLOTS + 2 if u == MIX_SLOTS + 1 else u - 1))
                            for t in range(NB):
                                last = pe.transpose(tr[u % 2][:, t * P:(t + 1) * P], exps[u % 2][:, t * P:(t + 1) * P],
                                                    g.ident[:])
                            last.then_inc(tr_done, 1)

                        def mix_slots():
                            pe.wait_ge(read_dve, b * UNITS + MIX_SLOTS)
                            pe.wait_ge(read_act, b * READS_ACT + MIX_SLOTS)
                            for t in range(NB):
                                last = pe.matmul(tr[0][:, 0:SLOTS], xn[:, t, :], dispatch[:, t, :], start=t == 0,
                                                 stop=t == NB - 1)
                            last.then_inc(slots_done, 1)

                        score(0)
                        for u in range(UNITS):
                            if u + 1 < UNITS:
                                score(u + 1)
                            turn(u)
                            if u == MIX_SLOTS:
                                mix_slots()
                        if not last_batch:
                            turn_input(b + 1, True)

                    pe.wait_ge(chain, 4 + SB)
                    for q in range(SB):
                        last = pe.transpose(logits[0][:, q * P:(q + 1) * P], slots_n[:, q, :], g.ident[:])
                    last.then_inc(turned, 1)
                    pe.wait_ge(lo_done, 1)
                    batches(pe, lambda x: turn_input(x, False), batch)

                def place(u, c):
                    src = tr[u % 2][:, c * HALF:(c + 1) * HALF].rearrange("p (t n) -> p t n", t=4)
                    if u < UNITS_A:
                        return (lambda b: dispatch[:, 4 * c:4 * c + 4, u * P:(u + 1) * P]), src
                    blk = (u - UNITS_A) * 2 + c
                    return (lambda b: combine[:, :, ds(b * SEQ + blk * P, P)]), src

                @block.scalar
                def _(act):
                    def high_part(x):
                        act.wait_ge(input_turned, x + 1)
                        act.activation(xT[0][:], tr[1][:], ACT.Copy).then_inc(xT_hi_done, 1)

                    def batch(b, last):
                        def move(u):
                            to, src = place(u, 0)
                            act.wait_ge(tr_done, b * UNITS + u + 1)
                            act.activation(to(b), src, ACT.Copy).then_inc(read_act, 1)

                        for u in range(UNITS):
                            act.wait_ge(max_done, b * UNITS + u + 1)
                            if u >= 2:
                                act.wait_ge(tr_done, b * UNITS + u - 1)
                            for i in range(1 if u < UNITS_A else 2):
                                w = SEQ if u < UNITS_A else HALF
                                n = exps_by(u) - (1 if u < UNITS_A else 2) + i
                                act.activation(exps[u % 2][:, i * w:(i + 1) * w], logits[u % 2][:, i * w:(i + 1) * w],
                                               ACT.Exp, bias=minus_max[:, n:n + 1], accum_out=sums[:, n:n + 1]
                                               ).then_inc(exp_done, 1)
                            if u:
                                move(u - 1)
                            if u - 1 == MIX_SLOTS:
                                act.wait_ge(slots_done, b + 1)
                                act.activation(slotsT[:, :, b, :], tr[0][:, 0:SLOTS].rearrange("p (e s) -> p e s", e=SE),
                                               ACT.Copy).then_inc(read_act, 1)
                        move(UNITS - 1)
                        if not last:
                            high_part(b + 1)

                    act.wait_ge(turned, 1)
                    act.activation(snT[0][:], logits[0][:, 0:SLOTS], ACT.Copy).then_inc(hi_done, 1)
                    batches(act, high_part, batch)

                @block.vector
                def _(dve):
                    def prepare_parts(x, own):
                        def mean_square():
                            own.did(dve.tensor_tensor(squares[:], hidden[:], hidden[:], ALU.mult))
                            own.settle()
                            own.did(dve.tensor_reduce(ss[:], squares[:], AX.X, ALU.add))
                            own.settle()
                            dve.tensor_scalar(ss[:], ss[:], 1e-24, None, ALU.max).then_inc(ss_ready, 1)

                        def scale():
                            dve.wait_ge(slots_done, x)
                            dve.wait_ge(rs_ready, x + 2)
                            for t in range(NB):
                                own.did(dve.scalar_tensor_tensor(xn[:, t, :], hidden[:, t, :], rs[:, t:t + 1], gamma[:],
                                                                 ALU.mult, ALU.mult))

                        return layernorm_parts(dve, own, lambda t: g.x[:, x * NB + t, :], lambda t: hidden[:, t, :],
                                               norm, x) + [mean_square, scale]

                    def low_part(x):
                        dve.wait_ge(xT_hi_done, x + 1)
                        dve.tensor_tensor(xT[1][:], tr[1][:], xT[0][:].bitcast(F32), ALU.subtract
                                          ).then_inc(xT_lo_done, 1)

                    def prepare(x):
                        for part in prepare_parts(x, Chain(dve, norm.chain)):
                            part()
                        low_part(x)

                    def batch(b, last):
                        own = Chain(dve, norm.chain, CHAIN_XN + b * CHAIN)
                        nexts = [] if last else prepare_parts(b + 1, own)
                        assert not nexts or len(nexts) == 10

                        def move(u):
                            to, src = place(u, 1)
                            dve.wait_ge(tr_done, b * UNITS + u + 1)
                            dve.tensor_copy(to(b), src).then_inc(read_dve, 1)

                        def largest(u):
                            dve.wait_ge(lg_done, b * UNITS + u + 1)
                            if u < UNITS_A:
                                ins = dve.tensor_reduce(minus_max[:, u:u + 1], logits[u % 2][:], AX.X, ALU.max, negate=True)
                            else:
                                n = exps_by(u) - 2
                                ins = dve.tensor_reduce(minus_max[:, n:n + 2], logits[u % 2][:].rearrange(
                                    "p (i n) -> p i n", i=2), AX.X, ALU.max, negate=True)
                            ins.then_inc(max_done, 1)

                        largest(0)
                        for u in range(UNITS):
                            dve.wait_ge(exp_done, b * EXPS + exps_by(u))
                            if u < UNITS_A:
                                own.did(dve.reciprocal(inv_d[:, u:u + 1], sums[:, u:u + 1]))
                                own.settle()
                                dve.tensor_scalar(exps[u % 2][:], exps[u % 2][:], inv_d[:, u:u + 1], None, ALU.mult
                                                  ).then_inc(scaled, 1)
                            else:
                                n = exps_by(u) - 2
                                own.did(dve.reciprocal(inv_c[:, ds(b * NB + 2 * (u - UNITS_A), 2)], sums[:, n:n + 2]))
                            if u + 1 < UNITS:
                                largest(u + 1)
                            move(u)
                            for part in nexts[PARTS_AFTER[u]:PARTS_AFTER[u + 1]]:
                                part()
                        assert last or own.n == CHAIN, own.n
                        if not last:
                            low_part(b + 1)

                    own = Chain(dve, chain)
                    dve.wait_ge(loaded, 3 * 16)
                    own.did(dve.tensor_scalar(gamma[:], gamma[:], root, None, ALU.mult))
                    own.did(dve.tensor_scalar(slot_gamma[:], slot_gamma[:], root, None, ALU.mult))
                    own.did(dve.tensor_tensor(slots_n[:], slot_in[:], slot_in[:], ALU.mult))
                    own.settle()
                    own.did(dve.tensor_reduce(ss[:, 0:SB], slots_n[:], AX.X, ALU.add))
                    own.settle()
                    dve.tensor_scalar(ss[:, 0:SB], ss[:, 0:SB], 1e-24, None, ALU.max).then_inc(ss_ready, 1)
                    dve.wait_ge(rs_ready, 1)
                    for q in range(SB):
                        own.did(dve.scalar_tensor_tensor(slots_n[:, q, :], slot_in[:, q, :], rs[:, q:q + 1],
                                                         slot_gamma[:], ALU.mult, ALU.mult))
                    own.settle()
                    assert own.n == 4 + SB
                    dve.wait_ge(hi_done, 1)
                    dve.tensor_tensor(snT[1][:], logits[0][:, 0:SLOTS], snT[0][:].bitcast(F32), ALU.subtract
                                      ).then_inc(lo_done, 1)
                    batches(dve, prepare, batch)

        with ExitStack() as ectx:
            def esb(name, shape, dt=F32):
                return ectx.enter_context(nc.sbuf_tensor("s_" + name, shape, dt))

            w1_e = [esb(f"w1_e{i}", [P, S_HID]) for i in range(2)]
            w2_e = [esb(f"w2_e{i}", [P, S_HB, D]) for i in range(2)]
            hT = [esb(f"hT{i}", [P, S_HB, COLS]) for i in range(2)]
            slot_out = esb("slot_out", [P, SB, BATCH, D])
            eo_b = [esb(f"eo_b{i}", [P, SB, D]) for i in range(2)]
            mixedT = esb("mixedT", [P, SEQ])
            mixed = esb("mixed", [P, NB, D])
            up = [ectx.enter_context(nc.psum_tensor(f"s_up{i}", [P, S_HB, COLS], F32)) for i in range(2)]
            down = ectx.enter_context(nc.psum_tensor("s_down", [P, BATCH * D], F32))
            w1_ready, w2_ready, up_done, gelu_done = sem("w1_ready"), sem("w2_ready"), sem("up_done"), sem("gelu_done")
            down_done, down_kept = sem("down_done"), sem("down_kept")

            with nc.Block() as block:
                @block.tensor
                def _(pe):
                    def raise_(par, e):
                        pe.wait_ge(w1_ready, e + 1)
                        for h in range(S_HB):
                            last = pe.matmul(up[par][:, h, :], w1_e[par][:, h * P:(h + 1) * P], slotsT[:, e],
                                             start=True, stop=True)
                            if h % 2:
                                last.then_inc(up_done, 1)

                    def lower(par, e, q):
                        pe.wait_ge(w2_ready, e + 1)
                        pe.wait_ge(gelu_done, (e + 1) * S_HB)
                        if par == 0:
                            pe.wait_ge(down_kept, q)
                        for b in range(BATCH):
                            for h in range(S_HB):
                                last = pe.matmul(down[par * SS:(par + 1) * SS, b * D:(b + 1) * D],
                                                 hT[par][:, h, b * SS:(b + 1) * SS], w2_e[par][:, h, :],
                                                 start=h == 0 and b == 0, stop=h == S_HB - 1, skip_group_check=True)
                        last.then_inc(down_done, 1)

                    raise_(0, 0)
                    with pe.Fori(0, SB - 1) as q:
                        for par in range(2):
                            raise_(1 - par, q * 2 + par + 1)
                            lower(par, q * 2 + par, q)
                    raise_(1, SE - 1)
                    for par in range(2):
                        lower(par, SE - 2 + par, SB - 1)

                @block.scalar
                def _(act):
                    with act.Fori(0, SB) as q:
                        for par in range(2):
                            e = q * 2 + par
                            for h in range(S_HB):
                                if h % 2 == 0:
                                    act.wait_ge(up_done, e * (S_HB // 2) + h // 2 + 1)
                                act.activation(hT[par][:, h, :], up[par][:, h, :], ACT.Gelu,
                                               bias=b1[:, e, h:h + 1]
                                               ).then_inc(gelu_done, 1)

                @block.vector
                def _(dve):
                    def take_up(par, e):
                        dve.tensor_copy(w1_e[par][:], w1[:, e, :]).then_inc(w1_ready, 1)

                    def take_down(par, e):
                        dve.tensor_copy(w2_e[par][:], w2[:, e]).then_inc(w2_ready, 1)

                    def keep(q):
                        dve.wait_ge(down_done, q * 2 + 2)
                        dve.tensor_tensor(slot_out[:, q], down[:].rearrange("p (b n) -> p b n", b=BATCH),
                                          b2[:, q, :].unsqueeze(1).to_broadcast([P, BATCH, D]), ALU.add
                                          ).then_inc(down_kept, 1)

                    for par in range(2):
                        take_up(par, par)
                        take_down(par, par)
                    with dve.Fori(0, SB - 1) as q:
                        for par in range(2):
                            dve.wait_ge(up_done, (q * 2 + par + 1) * (S_HB // 2))
                            take_up(par, q * 2 + par + 2)
                            dve.wait_ge(down_done, q * 2 + par + 1)
                            take_down(par, q * 2 + par + 2)
                        keep(q)
                    keep(SB - 1)

            eo_ready, mixT_done, mixT_kept, mix_done, mix_kept, x_done, stored = (sem(n) for n in (
                "eo_ready", "mixT_done", "mixT_kept", "mix_done", "mix_kept", "x_done", "stored"))
            mixT_ps, mix_ps = up[0], up[1]
            flat = lambda t: t[:].rearrange("p h n -> p (h n)")
            base = BATCH * CHAIN
            with nc.Block() as block:
                @block.sync
                def _(sp):
                    for b in range(BATCH):
                        sp.wait_ge(x_done, b + 1)
                        sp.dma_start(out[b].rearrange("(t p) n -> p t n", p=P), g.x[:, b * NB:(b + 1) * NB, :]
                                     ).then_inc(stored, 16)
                    sp.wait_ge(stored, BATCH * 16)

                @block.gpsimd
                def _(pool):
                    with pool.Fori(0, BATCH) as b:
                        inverse_root(pool, norm, g.minus_half[:, 0:NB], b + BATCH)

                @block.tensor
                def _(pe):
                    with pe.Fori(0, BATCH // 2) as pair:
                        for par in range(2):
                            b = pair * 2 + par
                            pe.wait_ge(eo_ready, b + 1)
                            for c in range(2):
                                for q in range(SB):
                                    last = pe.matmul(flat(mixT_ps)[:, c * HALF:(c + 1) * HALF], eo_b[par][:, q, :],
                                                     combine[:, q, ds(b * SEQ + c * HALF, HALF)], start=q == 0,
                                                     stop=q == SB - 1)
                            last.then_inc(mixT_done, 1)
                            pe.wait_ge(mixT_kept, b + 1)
                            pe.wait_ge(mix_kept, b)
                            for t in range(NB):
                                last = pe.transpose(flat(mix_ps)[:, t * P:(t + 1) * P], mixedT[:, t * P:(t + 1) * P],
                                                    g.ident[:])
                            last.then_inc(mix_done, 1)

                @block.scalar
                def _(act):
                    def take(par, b):
                        act.activation(eo_b[par][:], slot_out[:, :, b, :], ACT.Copy).then_inc(eo_ready, 1)

                    with act.Fori(0, BATCH // 2) as pair:
                        for par in range(2):
                            take(par, pair * 2 + par)
                        for par in range(2):
                            b = pair * 2 + par
                            act.wait_ge(mixT_done, b + 1)
                            act.activation(mixedT[:], flat(mixT_ps), ACT.Copy).then_inc(mixT_kept, 1)

                @block.vector
                def _(dve):
                    with dve.Fori(0, BATCH) as b:
                        own = Chain(dve, norm.chain, b * NORM_STEPS + base)
                        dve.wait_ge(x_done, b)
                        dve.wait_ge(mix_done, b + 1)
                        dve.tensor_tensor(mixed[:], flat(mix_ps).rearrange("p (t n) -> p t n", t=NB),
                                          inv_c[:, ds(b * NB, NB)].unsqueeze(2).to_broadcast([P, NB, D]),
                                          ALU.mult).then_inc(mix_kept, 1)
                        dve.wait_ge(mix_kept, b + 1)
                        layernorm(dve, own, lambda t: mixed[:, t, :], lambda t: mixed[:, t, :], norm, b + BATCH)
                        assert own.n == NORM_STEPS
                        batch = g.x[:, ds(b * NB, NB), :]
                        dve.tensor_tensor(batch, batch, mixed[:], ALU.add).then_inc(x_done, 1)


def constants():
    i = np.arange(P)
    k, q = i[:, None], np.arange(LOCAL_W)[None, :]

    def rotation(base):
        inv_freq = np.float32(1.0) / np.float32(base) ** (np.arange(0, HD, 2, dtype=np.float32) / np.float32(HD))
        angles = np.arange(SEQ, dtype=np.float32)[:, None] * inv_freq[None, :].astype(np.float32)
        return np.stack([np.cos(angles), np.sin(angles)]).astype(np.float32)

    return {
        "c_ident": np.eye(P, dtype=np.float32),
        "c_iota": np.arange(E_ROUTED, dtype=np.float32),
        "c_mask_kq": np.where(i[:, None] > i[None, :], -1e30, 0.0).astype(np.float32),
        "c_mask_window": np.where((q - k >= 0) & (q - k < WINDOW), 0.0, -1e30).astype(np.float32),
        "c_rope_g": rotation(1e6),
        "c_rope_l": rotation(1e4),
        "c_mask_qk": np.where(i[None, :] > i[:, None], -1e30, 0.0).astype(np.float32),
    }


class Shared:
    pass


def build(nc, aps, out):
    g = Shared()
    g.inputs = aps
    with ExitStack() as ctx:
        def sb(name, shape, dt=F32):
            return ctx.enter_context(nc.sbuf_tensor(name, shape, dt))

        g.x = sb("x", [P, NBLK, D])
        g.ident = sb("ident", [P, P])
        g.ident_bf = sb("ident_bf", [P, P], BF16)
        g.mask_qk = sb("mask_qk", [P, P], BF16)
        g.minus_half = sb("minus_half", [P, 256])
        g.mask_kq = sb("mask_kq", [P, P], BF16)
        g.mask_window = sb("mask_window", [P, LOCAL_W], BF16)
        staged = [sb(f"staged{i}", [P, LOCAL_W]) for i in range(3)]
        const_loaded = ctx.enter_context(nc.semaphore("const_loaded"))
        masks = ((g.inputs["c_mask_qk"], P), (g.inputs["c_mask_kq"], P), (g.inputs["c_mask_window"], LOCAL_W))
        with nc.Block() as block:
            @block.sync
            def _(sp):
                sp.dma_start(g.ident[:], g.inputs["c_ident"]).then_inc(const_loaded, 16)
                for n, (src, width) in enumerate(masks):
                    sp.dma_start(staged[n][:, 0:width], src).then_inc(const_loaded, 16)

            @block.gpsimd
            def _(pool):
                pool.memset(g.minus_half[:], -0.5)

            @block.vector
            def _(dve):
                dve.wait_ge(const_loaded, 4 * 16)
                dve.tensor_copy(g.ident_bf[:], g.ident[:])
                for n, (out, (_, width)) in enumerate(zip((g.mask_qk, g.mask_kq, g.mask_window), masks)):
                    dve.tensor_copy(out[:], staged[n][:, 0:width])
        attention_layer0(nc, g)
        mixture_layer0(nc, g)
        layer1_attention(nc, g)
        soft_mixture(nc, g, out)



def kernel(**inputs):
    import concourse.bacc as _bacc
    from concourse.bass_utils import run_bass_kernel_spmd as _run

    nc = _bacc.Bacc("TRN2", target_bir_lowering=False, num_devices=1)
    arrays, aps = {}, {}
    for name, a in (inputs | constants()).items():
        a = np.ascontiguousarray(a)
        arrays[f"in_{name}"] = a
        aps[name] = nc.dram_tensor(f"in_{name}", a.shape, mybir.dt.from_np(a.dtype), kind="ExternalInput").ap()
    out = nc.dram_tensor("out_x", (BATCH, SEQ, D), F32, kind="ExternalOutput").ap()
    build(nc, aps, out)
    return _run(nc, [arrays], core_ids=[0]).results[0]["out_x"]
```
